# Optimizing a Trainium2 kernel written in Bass

```python
import numpy as np
import jax
import jax.numpy as jnp

def _softmax(x, axis=-1):
    return jax.nn.softmax(x, axis=axis)

def _gelu(x):
    return jax.nn.gelu(x, approximate=True)

def _silu(x):
    return jax.nn.silu(x)

def _sigmoid(x):
    return jax.nn.sigmoid(x)

def _layernorm(x, axis=-1, eps=1e-05):
    m = jnp.mean(x, axis=axis, keepdims=True)
    v = jnp.var(x, axis=axis, keepdims=True)
    return (x - m) / jnp.sqrt(v + eps)

def _scatter_add(tgt, idx, src, axis=0):
    return tgt.at[idx].add(src)

def _segment_sum(src, seg, n):
    return jax.ops.segment_sum(src, seg, n)
kernel_name = 'mk_flamingo_gated_d2_seqx_r4_feb2fd'

def setup_inputs(seed: int=0):
    np.random.seed(seed)
    _w = jnp.asarray

    def _rec_inputs():
        import jax
        import jax.numpy as jnp
        _rk = jax.random.key(seed)
        x = -0.0002928 + 1 * jax.random.normal(jax.random.fold_in(_rk, 1), (8, 256, 256), jnp.float32)
        _lenS = 256 - jax.random.randint(jax.random.fold_in(_rk, 7), (8,), 0, max(1, 256 // 4) + 1, jnp.int32)
        _lenS2 = 256 - jax.random.randint(jax.random.fold_in(_rk, 8), (8,), 0, max(1, 256 // 4) + 1, jnp.int32)
        _ctx_1024P = jax.random.normal(jax.random.fold_in(_rk, 11), (8, 16, 256), jnp.float32)
        _ctx_1024c = jax.random.dirichlet(jax.random.fold_in(_rk, 511), 0.3 * jnp.ones((16,), jnp.float32), (8, 256))
        _ctx_1024t = jnp.einsum('bsk,bkd->bsd', _ctx_1024c, _ctx_1024P)
        _ctx_1024t = _ctx_1024t * jax.lax.rsqrt(jnp.mean(jnp.square(_ctx_1024t)) + 1e-12) * 0.953939
        ctx_1024 = -1.39393e-06 + 0.999914 * (_ctx_1024t + 0.3 * jax.random.normal(jax.random.fold_in(_rk, 611), (8, 256, 256), jnp.float32))
        _validS = jnp.arange(256)[None, :] < _lenS[:, None]
        _validS2 = jnp.arange(256)[None, :] < _lenS2[:, None]
        _causal = jnp.tril(jnp.ones((256, 256), dtype=bool))
        mask_Bx1x1xS2_if1 = jnp.where(jnp.ones((8, 1, 1, 256), dtype=bool), 1, 0).astype(jnp.int32)
        _g = jax.random.normal(jax.random.fold_in(_rk, 9001), (2, 2), jnp.float32)
        _g = jnp.sign(_g) * jnp.maximum(jnp.abs(_g), 1.0) + (_g == 0) * 1.0
        g_xattn = _g[0]
        g_ffn = _g[1]
        return (x, ctx_1024, mask_Bx1x1xS2_if1, g_xattn, g_ffn)
    x, ctx_1024, mask_Bx1x1xS2_if1, g_xattn, g_ffn = _rec_inputs()

    def _L0_xattn_setup():
        import jax, jax.numpy as jnp
        import numpy as np
        D_MODEL = 256
        H = 16
        D_K = D_MODEL // H
        key = jax.random.key(seed)
        ks = jax.random.split(key, 8)
        B, S = (2, 512)
        scale = 1.0 / np.sqrt(D_MODEL)
        return {'query': jax.random.normal(ks[0], (B, S, D_MODEL), dtype=jnp.float32), 'key': jax.random.normal(ks[1], (B, S, D_MODEL), dtype=jnp.float32), 'value': jax.random.normal(ks[2], (B, S, D_MODEL), dtype=jnp.float32), 'mask': jnp.ones((B, 1, 1, S), dtype=jnp.int32), 'Wq': jax.random.normal(ks[3], (D_MODEL, D_MODEL), dtype=jnp.float32) * scale, 'Wk': jax.random.normal(ks[4], (D_MODEL, D_MODEL), dtype=jnp.float32) * scale, 'Wv': jax.random.normal(ks[5], (D_MODEL, D_MODEL), dtype=jnp.float32) * scale, 'Wo': jax.random.normal(ks[6], (D_MODEL, D_MODEL), dtype=jnp.float32) * scale}
    _L0_xattn_all = _L0_xattn_setup()
    _L0_xattn_in = {k: v for k, v in _L0_xattn_all.items() if k in ('Wq', 'Wk', 'Wv', 'Wo')}
    del _L0_xattn_all

    def _L0_ffn_setup():
        import jax, jax.numpy as jnp
        import numpy as np
        D_MODEL = 256
        D_HIDDEN = 1024
        N_EXPERTS = 8
        B, S = (2, 512)
        key = jax.random.key(seed)
        ks = jax.random.split(key, 4)
        sd = 1.0 / np.sqrt(D_MODEL)
        sh = 1.0 / np.sqrt(D_HIDDEN)
        return {'x': jax.random.normal(ks[0], (B, S, D_MODEL), dtype=jnp.float32), 'Wg': jax.random.normal(ks[1], (D_MODEL, N_EXPERTS), dtype=jnp.float32) * sd, 'bg': jnp.zeros((N_EXPERTS,), dtype=jnp.float32), 'W1': jax.random.normal(ks[2], (N_EXPERTS, D_MODEL, D_HIDDEN), dtype=jnp.float32) * sd, 'b1': jnp.zeros((N_EXPERTS, D_HIDDEN), dtype=jnp.float32), 'W2': jax.random.normal(ks[3], (N_EXPERTS, D_HIDDEN, D_MODEL), dtype=jnp.float32) * sh, 'b2': jnp.zeros((N_EXPERTS, D_MODEL), dtype=jnp.float32)}
    _L0_ffn_all = _L0_ffn_setup()
    _L0_ffn_in = {k: v for k, v in _L0_ffn_all.items() if k in ('Wg', 'bg', 'W1', 'b1', 'W2', 'b2')}
    del _L0_ffn_all

    def _L1_xattn_setup():
        import jax, jax.numpy as jnp
        import numpy as np
        NUM_HEADS = 16
        D_MODEL = 256
        HEAD_DIM = D_MODEL // NUM_HEADS
        SCALE = float(np.sqrt(HEAD_DIM))
        EPS = 1e-05

        def layernorm(x, g, b):
            mu = jnp.mean(x, axis=-1, keepdims=True)
            var = jnp.mean(jnp.square(x - mu), axis=-1, keepdims=True)
            return (x - mu) * jax.lax.rsqrt(var + EPS) * g + b
        key = jax.random.key(seed)
        ks = jax.random.split(key, 8)
        B, Nq, Nc = (2, 512, 512)
        s = 0.02
        return {'x_query': jax.random.normal(ks[0], (B, Nq, D_MODEL), jnp.float32), 'x_context': jax.random.normal(ks[1], (B, Nc, D_MODEL), jnp.float32), 'Wq': jax.random.normal(ks[2], (D_MODEL, D_MODEL), jnp.float32) * s, 'Wkv': jax.random.normal(ks[3], (D_MODEL, 2 * D_MODEL), jnp.float32) * s, 'Wp': jax.random.normal(ks[4], (D_MODEL, D_MODEL), jnp.float32) * s, 'bp': jnp.zeros((D_MODEL,), jnp.float32), 'ln_g': jnp.ones((HEAD_DIM,), jnp.float32), 'ln_b': jnp.zeros((HEAD_DIM,), jnp.float32)}
    _L1_xattn_all = _L1_xattn_setup()
    _L1_xattn_in = {k: v for k, v in _L1_xattn_all.items() if k in ('Wq', 'Wkv', 'Wp', 'bp', 'ln_g', 'ln_b')}
    del _L1_xattn_all

    def _L1_ffn_setup():
        import jax, jax.numpy as jnp
        import numpy as np
        DIM = 256
        DEPTH = 2
        HEADS = 8
        DIM_HEAD = 64
        WINDOW = 128
        INNER = HEADS * DIM_HEAD
        HID = int(DIM * 4 * 2 / 3)
        B, N = (2, 2048)
        QK_SCALE = 8.0

        def shift_token(t):
            t1, t2 = jnp.split(t, 2, axis=-1)
            t2 = jnp.pad(t2, ((0, 0), (1, 0), (0, 0)))[:, :-1]
            return jnp.concatenate([t1, t2], axis=-1)

        def l2norm(t):
            return t / jnp.clip(jnp.linalg.norm(t, axis=-1, keepdims=True), 1e-12)

        def rotate_half(x):
            x1, x2 = jnp.split(x, 2, axis=-1)
            return jnp.concatenate([-x2, x1], axis=-1)

        def rotary_xpos(q, k):
            n = q.shape[-2]
            half_idx = jnp.arange(0, DIM_HEAD, 2, dtype=jnp.float32)
            inv_freq = 1.0 / 10000.0 ** (half_idx / DIM_HEAD)
            t = jnp.arange(n, dtype=jnp.float32)
            freqs = t[:, None] * inv_freq[None, :]
            freqs = jnp.concatenate([freqs, freqs], axis=-1)
            base = (half_idx + 0.4 * DIM_HEAD) / (1.4 * DIM_HEAD)
            power = (t - n // 2) / float(WINDOW // 2)
            scale = base[None, :] ** power[:, None]
            scale = jnp.concatenate([scale, scale], axis=-1)
            cos, sin = (jnp.cos(freqs), jnp.sin(freqs))
            q = q * cos * scale + rotate_half(q) * sin * scale
            k = k * cos / scale + rotate_half(k) * sin / scale
            return (q, k)

        def local_attention(q, k, v):
            b, h, n, d = q.shape
            w = n // WINDOW
            bq = q.reshape(b, h, w, WINDOW, d) * QK_SCALE
            bk = k.reshape(b, h, w, WINDOW, d)
            bv = v.reshape(b, h, w, WINDOW, d)

            def look_around(t):
                p = jnp.pad(t, ((0, 0), (0, 0), (1, 0), (0, 0), (0, 0)))
                return jnp.concatenate([p[:, :, :w], p[:, :, 1:]], axis=3)
            bk, bv = (look_around(bk), look_around(bv))
            bt = jnp.arange(n).reshape(w, WINDOW)
            btp = jnp.pad(bt, ((1, 0), (0, 0)), constant_values=-1)
            btk = jnp.concatenate([btp[:w], btp[1:]], axis=1)
            sim = jnp.einsum('bhwid,bhwjd->bhwij', bq, bk)
            i = bt[:, :, None]
            j = btk[:, None, :]
            mask = (i < j) | (i > j + WINDOW) | (j == -1)
            sim = jnp.where(mask, -jnp.finfo(sim.dtype).max, sim)
            attn = jax.nn.softmax(sim, axis=-1)
            out = jnp.einsum('bhwij,bhwjd->bhwid', attn, bv)
            return out.reshape(b, h, n, d)

        def _layer(x, wqkv, qs, ksc, wo, lg, lb, w1, b1, w2, b2):
            b, n, _ = x.shape
            h = shift_token(x)
            qkv = h @ wqkv
            q, k, v = jnp.split(qkv, 3, axis=-1)
            to_heads = lambda t: t.reshape(b, n, HEADS, DIM_HEAD).transpose(0, 2, 1, 3)
            q, k, v = (to_heads(q), to_heads(k), to_heads(v))
            q = l2norm(q) * qs
            k = l2norm(k) * ksc
            q, k = rotary_xpos(q, k)
            o = local_attention(q, k, v)
            o = o.transpose(0, 2, 1, 3).reshape(b, n, INNER)
            x = x + o @ wo
            h = shift_token(x)
            mu = h.mean(-1, keepdims=True)
            var = h.var(-1, keepdims=True)
            h = (h - mu) / jnp.sqrt(var + 1e-05) * lg + lb
            h = h @ w1 + b1
            a, g = jnp.split(h, 2, axis=-1)
            h = a * jax.nn.gelu(g, approximate=False)
            x = x + h @ w2 + b2
            return x
        key = jax.random.key(seed)
        ks = jax.random.split(key, 6)
        return {'x': jax.random.normal(ks[0], (B, N, DIM), jnp.float32), 'wqkv': jax.random.normal(ks[1], (DEPTH, DIM, 3 * INNER), jnp.float32) * 0.02, 'q_scale': jnp.ones((DEPTH, DIM_HEAD), jnp.float32), 'k_scale': jnp.ones((DEPTH, DIM_HEAD), jnp.float32), 'wo': jax.random.normal(ks[2], (DEPTH, INNER, DIM), jnp.float32) * 0.02, 'ln_g': jnp.ones((DEPTH, DIM), jnp.float32), 'ln_b': jnp.zeros((DEPTH, DIM), jnp.float32), 'w1': jax.random.normal(ks[3], (DEPTH, DIM, 2 * HID), jnp.float32) * 0.02, 'b1': jnp.zeros((DEPTH, 2 * HID), jnp.float32), 'w2': jax.random.normal(ks[4], (DEPTH, HID, DIM), jnp.float32) * 0.02, 'b2': jnp.zeros((DEPTH, DIM), jnp.float32)}
    _L1_ffn_all = _L1_ffn_setup()
    _L1_ffn_in = {k: v for k, v in _L1_ffn_all.items() if k in ('wqkv', 'q_scale', 'k_scale', 'wo', 'ln_g', 'ln_b', 'w1', 'b1', 'w2', 'b2')}
    del _L1_ffn_all
    return {'x': x, 'ctx_1024': ctx_1024, 'mask_Bx1x1xS2_if1': mask_Bx1x1xS2_if1, 'g_xattn': g_xattn, 'g_ffn': g_ffn, 'L0_xattn_Wq': _L0_xattn_in['Wq'], 'L0_xattn_Wk': _L0_xattn_in['Wk'], 'L0_xattn_Wv': _L0_xattn_in['Wv'], 'L0_xattn_Wo': _L0_xattn_in['Wo'], 'L0_ffn_Wg': _L0_ffn_in['Wg'], 'L0_ffn_bg': _L0_ffn_in['bg'], 'L0_ffn_W1': _L0_ffn_in['W1'], 'L0_ffn_b1': _L0_ffn_in['b1'], 'L0_ffn_W2': _L0_ffn_in['W2'], 'L0_ffn_b2': _L0_ffn_in['b2'], 'L1_xattn_Wq': _L1_xattn_in['Wq'], 'L1_xattn_Wkv': _L1_xattn_in['Wkv'], 'L1_xattn_Wp': _L1_xattn_in['Wp'], 'L1_xattn_bp': _L1_xattn_in['bp'], 'L1_xattn_ln_g': _L1_xattn_in['ln_g'], 'L1_xattn_ln_b': _L1_xattn_in['ln_b'], 'L1_ffn_wqkv': _L1_ffn_in['wqkv'], 'L1_ffn_q_scale': _L1_ffn_in['q_scale'], 'L1_ffn_k_scale': _L1_ffn_in['k_scale'], 'L1_ffn_wo': _L1_ffn_in['wo'], 'L1_ffn_ln_g': _L1_ffn_in['ln_g'], 'L1_ffn_ln_b': _L1_ffn_in['ln_b'], 'L1_ffn_w1': _L1_ffn_in['w1'], 'L1_ffn_b1': _L1_ffn_in['b1'], 'L1_ffn_w2': _L1_ffn_in['w2'], 'L1_ffn_b2': _L1_ffn_in['b2']}

def reference(x, ctx_1024, mask_Bx1x1xS2_if1, g_xattn, g_ffn, L0_xattn_Wq, L0_xattn_Wk, L0_xattn_Wv, L0_xattn_Wo, L0_ffn_Wg, L0_ffn_bg, L0_ffn_W1, L0_ffn_b1, L0_ffn_W2, L0_ffn_b2, L1_xattn_Wq, L1_xattn_Wkv, L1_xattn_Wp, L1_xattn_bp, L1_xattn_ln_g, L1_xattn_ln_b, L1_ffn_wqkv, L1_ffn_q_scale, L1_ffn_k_scale, L1_ffn_wo, L1_ffn_ln_g, L1_ffn_ln_b, L1_ffn_w1, L1_ffn_b1, L1_ffn_w2, L1_ffn_b2):
    import jax
    import jax.numpy as jnp

    def _L0_xattn_ref(query, key, value, mask, Wq, Wk, Wv, Wo):
        import jax, jax.numpy as jnp
        import numpy as np
        D_MODEL = 256
        H = 16
        D_K = D_MODEL // H
        B, S, _ = query.shape
        q = (query @ Wq.T).reshape(B, S, H, D_K)
        k = (key @ Wk.T).reshape(B, S, H, D_K)
        v = (value @ Wv.T).reshape(B, S, H, D_K)
        scores = jnp.einsum('bqhd,bkhd->bhqk', q, k) / jnp.sqrt(jnp.float32(D_K))
        out = jnp.einsum('bhqk,bkhd->bqhd', scores, v).reshape(B, S, D_MODEL)
        return out @ Wo.T

    def _L0_ffn_ref(x, Wg, bg, W1, b1, W2, b2):
        import jax, jax.numpy as jnp
        import numpy as np
        D_MODEL = 256
        D_HIDDEN = 1024
        N_EXPERTS = 8
        B, S = (2, 512)
        logits = jnp.einsum('bsd,de->bse', x, Wg) + bg
        expert_idx = jnp.argmax(logits, axis=-1)
        h = jax.nn.gelu(jnp.einsum('bsd,edh->bseh', x, W1) + b1, approximate=False)
        y = jnp.einsum('bseh,ehd->bsed', h, W2) + b2
        out = jnp.take_along_axis(y, expert_idx[:, :, None, None], axis=2)[:, :, 0, :]
        return out

    def _L1_xattn_ref(x_query, x_context, Wq, Wkv, Wp, bp, ln_g, ln_b):
        import jax, jax.numpy as jnp
        import numpy as np
        NUM_HEADS = 16
        D_MODEL = 256
        HEAD_DIM = D_MODEL // NUM_HEADS
        SCALE = float(np.sqrt(HEAD_DIM))
        EPS = 1e-05

        def layernorm(x, g, b):
            mu = jnp.mean(x, axis=-1, keepdims=True)
            var = jnp.mean(jnp.square(x - mu), axis=-1, keepdims=True)
            return (x - mu) * jax.lax.rsqrt(var + EPS) * g + b
        B, Nq, _ = x_query.shape
        Nc = x_context.shape[1]
        H, D = (NUM_HEADS, HEAD_DIM)
        q = (x_query @ Wq).reshape(B, Nq, H, D).transpose(0, 2, 1, 3)
        kv = (x_context @ Wkv).reshape(B, Nc, 2, H, D)
        k = kv[:, :, 0].transpose(0, 2, 1, 3)
        v = kv[:, :, 1].transpose(0, 2, 1, 3)
        q = layernorm(q, ln_g, ln_b)
        k = layernorm(k, ln_g, ln_b)
        q = q * SCALE
        attn = jnp.einsum('bhqd,bhkd->bhqk', q, k)
        attn = jax.nn.softmax(attn, axis=-1)
        out = jnp.einsum('bhqk,bhkd->bhqd', attn, v)
        out = out.transpose(0, 2, 1, 3).reshape(B, Nq, H * D)
        return out @ Wp + bp

    def _L1_ffn_ref(x, wqkv, q_scale, k_scale, wo, ln_g, ln_b, w1, b1, w2, b2):
        import jax, jax.numpy as jnp
        import numpy as np
        DIM = 256
        DEPTH = 2
        HEADS = 8
        DIM_HEAD = 64
        WINDOW = 128
        INNER = HEADS * DIM_HEAD
        HID = int(DIM * 4 * 2 / 3)
        B, N = (2, 2048)
        QK_SCALE = 8.0

        def shift_token(t):
            t1, t2 = jnp.split(t, 2, axis=-1)
            t2 = jnp.pad(t2, ((0, 0), (1, 0), (0, 0)))[:, :-1]
            return jnp.concatenate([t1, t2], axis=-1)

        def l2norm(t):
            return t / jnp.clip(jnp.linalg.norm(t, axis=-1, keepdims=True), 1e-12)

        def rotate_half(x):
            x1, x2 = jnp.split(x, 2, axis=-1)
            return jnp.concatenate([-x2, x1], axis=-1)

        def rotary_xpos(q, k):
            n = q.shape[-2]
            half_idx = jnp.arange(0, DIM_HEAD, 2, dtype=jnp.float32)
            inv_freq = 1.0 / 10000.0 ** (half_idx / DIM_HEAD)
            t = jnp.arange(n, dtype=jnp.float32)
            freqs = t[:, None] * inv_freq[None, :]
            freqs = jnp.concatenate([freqs, freqs], axis=-1)
            base = (half_idx + 0.4 * DIM_HEAD) / (1.4 * DIM_HEAD)
            power = (t - n // 2) / float(WINDOW // 2)
            scale = base[None, :] ** power[:, None]
            scale = jnp.concatenate([scale, scale], axis=-1)
            cos, sin = (jnp.cos(freqs), jnp.sin(freqs))
            q = q * cos * scale + rotate_half(q) * sin * scale
            k = k * cos / scale + rotate_half(k) * sin / scale
            return (q, k)

        def local_attention(q, k, v):
            b, h, n, d = q.shape
            w = n // WINDOW
            bq = q.reshape(b, h, w, WINDOW, d) * QK_SCALE
            bk = k.reshape(b, h, w, WINDOW, d)
            bv = v.reshape(b, h, w, WINDOW, d)

            def look_around(t):
                p = jnp.pad(t, ((0, 0), (0, 0), (1, 0), (0, 0), (0, 0)))
                return jnp.concatenate([p[:, :, :w], p[:, :, 1:]], axis=3)
            bk, bv = (look_around(bk), look_around(bv))
            bt = jnp.arange(n).reshape(w, WINDOW)
            btp = jnp.pad(bt, ((1, 0), (0, 0)), constant_values=-1)
            btk = jnp.concatenate([btp[:w], btp[1:]], axis=1)
            sim = jnp.einsum('bhwid,bhwjd->bhwij', bq, bk)
            i = bt[:, :, None]
            j = btk[:, None, :]
            mask = (i < j) | (i > j + WINDOW) | (j == -1)
            sim = jnp.where(mask, -jnp.finfo(sim.dtype).max, sim)
            attn = jax.nn.softmax(sim, axis=-1)
            out = jnp.einsum('bhwij,bhwjd->bhwid', attn, bv)
            return out.reshape(b, h, n, d)

        def _layer(x, wqkv, qs, ksc, wo, lg, lb, w1, b1, w2, b2):
            b, n, _ = x.shape
            h = shift_token(x)
            qkv = h @ wqkv
            q, k, v = jnp.split(qkv, 3, axis=-1)
            to_heads = lambda t: t.reshape(b, n, HEADS, DIM_HEAD).transpose(0, 2, 1, 3)
            q, k, v = (to_heads(q), to_heads(k), to_heads(v))
            q = l2norm(q) * qs
            k = l2norm(k) * ksc
            q, k = rotary_xpos(q, k)
            o = local_attention(q, k, v)
            o = o.transpose(0, 2, 1, 3).reshape(b, n, INNER)
            x = x + o @ wo
            h = shift_token(x)
            mu = h.mean(-1, keepdims=True)
            var = h.var(-1, keepdims=True)
            h = (h - mu) / jnp.sqrt(var + 1e-05) * lg + lb
            h = h @ w1 + b1
            a, g = jnp.split(h, 2, axis=-1)
            h = a * jax.nn.gelu(g, approximate=False)
            x = x + h @ w2 + b2
            return x
        for l in range(DEPTH):
            x = _layer(x, wqkv[l], q_scale[l], k_scale[l], wo[l], ln_g[l], ln_b[l], w1[l], b1[l], w2[l], b2[l])
        return x
    x = x + jnp.tanh(g_xattn[0]) * _L0_xattn_ref(_layernorm(x, axis=-1), ctx_1024, ctx_1024, mask_Bx1x1xS2_if1, L0_xattn_Wq, L0_xattn_Wk, L0_xattn_Wv, L0_xattn_Wo)
    x = x + jnp.tanh(g_ffn[0]) * _L0_ffn_ref(_layernorm(x, axis=-1), L0_ffn_Wg, L0_ffn_bg, L0_ffn_W1, L0_ffn_b1, L0_ffn_W2, L0_ffn_b2)
    x = x + jnp.tanh(g_xattn[1]) * _L1_xattn_ref(_layernorm(x, axis=-1), ctx_1024, L1_xattn_Wq, L1_xattn_Wkv, L1_xattn_Wp, L1_xattn_bp, L1_xattn_ln_g, L1_xattn_ln_b)
    x = x + jnp.tanh(g_ffn[1]) * _L1_ffn_ref(_layernorm(x, axis=-1), L1_ffn_wqkv, L1_ffn_q_scale, L1_ffn_k_scale, L1_ffn_wo, L1_ffn_ln_g, L1_ffn_ln_b, L1_ffn_w1, L1_ffn_b1, L1_ffn_w2, L1_ffn_b2)
    return x

_drawn_inputs = setup_inputs


def setup_inputs(seed=0):
    import zlib

    import numpy as np

    out = dict(_drawn_inputs(seed))
    spreads = {'g_ffn': (-1.0, 0.6),
     'L0_ffn_bg': (0.0, 0.8),
     'L0_ffn_b1': (0.0, 0.8),
     'L0_ffn_b2': (0.0, 2.0),
     'L1_xattn_bp': (0.0, 0.8),
     'L1_xattn_ln_g': (1.0, 0.6),
     'L1_xattn_ln_b': (0.0, 0.8),
     'L1_ffn_q_scale': (1.0, 0.6),
     'L1_ffn_k_scale': (1.0, 0.6),
     'L1_ffn_ln_g': (1.0, 0.6),
     'L1_ffn_ln_b': (0.0, 0.8),
     'L1_ffn_b1': (0.0, 0.8),
     'L1_ffn_b2': (0.0, 2.0)}
    factors = {'L0_ffn_Wg': 7.61,
     'L0_ffn_W1': 7.939,
     'L0_ffn_W2': 7.197,
     'L1_xattn_Wq': 8.0,
     'L1_xattn_Wkv': 8.0,
     'L1_xattn_Wp': 8.0,
     'L1_ffn_wqkv': 8.0,
     'L1_ffn_wo': 8.0,
     'L1_ffn_w1': 8.0,
     'L1_ffn_w2': 8.0}
    for name, (base, spread) in spreads.items():
        noise = np.random.default_rng([zlib.crc32(name.encode()), seed]).standard_normal(out[name].shape)
        drawn = base * np.exp(spread * noise) if base else spread * noise
        out[name] = jnp.asarray(drawn.astype(out[name].dtype))
    for name, factor in factors.items():
        out[name] = (out[name] * factor).astype(out[name].dtype)
    return out
```

```python
from contextlib import ExitStack

import concourse.bass as bass
from concourse import mybir

ALU = mybir.AluOpType
LOG_EXP = "natural_log_exp_and_others"
ACT = mybir.ActivationFunctionType
AX = mybir.AxisListType
F32 = mybir.dt.float32
BF16 = mybir.dt.bfloat16
I32 = mybir.dt.int32

P = 128
B, S, D = 8, 256, 256
T = B * S
C = D // P
W = 2 * S
PAIRS = T // W
TT = W // P
NT = T // P
E, FF = 8, 1024
FC = FF // P
SLOTS = 24
UNROLL = 3
H1, D1 = 16, 16
H2, D2 = 8, 64
INNER = H2 * D2
DEPTH = 2
HID = int(D * 4 * 2 / 3)
HC = -(-HID // P)
HL = HID - (HC - 1) * P
EPS = 1e-5

CONST = {n: i for i, n in enumerate(
    ["ident", "mean256", "mean16", "heads16", "before", "ones", "rotate", "heads64"])}
SMALL = 8 + 16 + SLOTS + 2


class Signal:

    def __init__(self, stack, nc, name, per):
        self.sem = stack.enter_context(nc.semaphore(name))
        self.per = per

    def at(self, step, k):
        return step * self.per + (self.per + k)

    def before(self, step, k):
        return step * self.per + k


def start_ahead(engine, signals):
    for s in signals:
        engine.sem_inc(s.sem, s.per)


def spread(ap, n, at):
    shape = list(ap.shape)
    shape.insert(at, n)
    return ap.unsqueeze(at).to_broadcast(shape)


def attend_linear(nc, io, sh):
    with ExitStack() as st:
        def sb(name, shape, dt=F32):
            return st.enter_context(nc.sbuf_tensor("a_" + name, shape, dt))

        def pb(name):
            return st.enter_context(nc.psum_tensor("a_" + name, [P, 512], F32))

        def sig(name, per):
            return Signal(st, nc, "a_" + name, per)

        wkv, wq, wo = sb("wkv", [P, C, 2 * D]), sb("wq", [P, C, D]), sb("wo", [P, C, D])
        wg = sb("wg", [P, C, E])
        bg = sb("bg", [P, E])
        gin = sb("gin", [P, 4])
        ctx = sb("ctx", [P, C, W])
        centred = sb("centred", [P, C, W])
        squares = sb("squares", [P, C, W])
        log, rstd = sb("log", [P, W]), sb("rstd", [P, W])
        normed = sb("normed", [P, C, W])
        kv = sb("kv", [P, TT, 2 * D])
        ktv = sb("ktv", [P, 2 * C, P])
        qT = sb("qT", [P, C, W])
        aT = sb("aT", [P, C, W])
        zeros = sb("zeros", [P, D])

        ps_kv = [pb(f"ps_kv{i}") for i in range(2)]
        ps_ktv, ps_norm = pb("ps_ktv"), pb("ps_norm")
        ps_q = [pb(f"ps_q{i}") for i in range(2)]
        ps_o, ps_logit = pb("ps_o"), pb("ps_logit")

        loaded = st.enter_context(nc.semaphore("a_loaded"))
        zeroed = st.enter_context(nc.semaphore("a_zeroed"))
        waited = st.enter_context(nc.semaphore("a_waited"))
        eps_set = st.enter_context(nc.semaphore("a_eps_set"))
        slots_zeroed = st.enter_context(nc.semaphore("a_slots_zeroed"))
        gates = st.enter_context(nc.semaphore("a_gates"))
        ctx_in = st.enter_context(nc.semaphore("a_ctx_in"))
        norm_ready = sig("norm_ready", 4)
        kv_ready = sig("kv_ready", TT)
        kv_copied = sig("kv_copied", TT)
        ktv_ready = sig("ktv_ready", 1)
        ktv_masked = sig("ktv_masked", 1)
        centred_done = sig("centred_done", 2)
        squared = sig("squared", 2)
        logged = sig("logged", 2)
        rstd_done = sig("rstd_done", 2)
        normed_done = sig("normed_done", 2)
        q_ready = sig("q_ready", 6)
        q_copied = sig("q_copied", 6)
        o_ready = sig("o_ready", C)
        added = sig("added", C)
        logit_ready = sig("logit_ready", 1)
        logit_done = sig("logit_done", 1)

        weights = [(wkv, io["L0_Wkv"]), (wq, io["L0_Wq"]), (wo, io["L0_Wo"]), (wg, io["Wg"])]
        nloads = 16 * (len(weights) + 5)

        x_all = sh["x"]

        def now_x(i, c):
            return x_all[:, c, bass.ds(i * W, W)]

        with nc.Block() as block:
            @block.sync
            def _(sp):
                sp.dma_start(sh["const"][:], io["consts"]).then_inc(loaded, 16)
                sp.dma_start(x_all[:], io["xT"]).then_inc(loaded, 16)
                for to, of in weights:
                    sp.dma_start(to[:], of.rearrange("(c p) n -> p c n", p=P)).then_inc(loaded, 16)
                sp.dma_start(bg[:], spread(io["bg"], P, 0)).then_inc(loaded, 16)
                sp.dma_start(gin[:], io["gates"]).then_inc(loaded, 16)
                sp.dma_start(sh["small"][:], io["small"]).then_inc(loaded, 16)
                with sp.Fori(0, PAIRS) as i:
                    sp.wait_ge(kv_ready.sem, kv_ready.before(i, TT))
                    sp.dma_start(ctx[:], io["ctxT"][:, :, bass.ds(i * W, W)]).then_inc(ctx_in, 16)
                sp.wait_ge(zeroed, 1)
                sp.dma_start(sh["sorted_x"].rearrange("(n p) d -> p n d", p=P),
                             spread(zeros[:], SLOTS, 1)).then_inc(slots_zeroed, 16)
                sp.wait_ge(slots_zeroed, 16)

            @block.gpsimd
            def _(pool):
                nc.gpsimd.memset(sh["eps"][:], EPS).then_inc(eps_set, 1)
                nc.gpsimd.memset(zeros[:], 0.0).then_inc(zeroed, 1)

            @block.tensor
            def _(pe):
                start_ahead(pe, [norm_ready, kv_ready, ktv_ready, q_ready, o_ready, logit_ready])
                pe.wait_ge(loaded, nloads)
                mean256 = sh["mat"]("mean256")
                with pe.Fori(0, PAIRS) as i:
                    def average(of, n):
                        if n % 2 == 0:
                            pe.wait_ge(rstd_done.sem, rstd_done.before(i, 2) if n == 0 else rstd_done.at(i, 1))
                        else:
                            pe.wait_ge(squared.sem, squared.at(i, n // 2 + 1))
                        for c in range(C):
                            mm = nc.tensor.matmul(ps_norm[:], mean256, of(c), start=(c == 0), stop=(c == C - 1))
                        mm.then_inc(norm_ready.sem, 1)

                    pe.wait_ge(added.sem, added.before(i, C))
                    average(lambda c: now_x(i, c), 0)
                    pe.wait_ge(ctx_in, i * 16 + 16)
                    for t in range(TT):
                        pe.wait_ge(kv_copied.sem, kv_copied.at(i, t - 1) if t >= 2 else kv_copied.before(i, TT - 1 + t))
                        for c in range(C):
                            mm = nc.tensor.matmul(ps_kv[t % 2][:], ctx[:, c, t * P:(t + 1) * P], wkv[:, c, :],
                                                  start=(c == 0), stop=(c == C - 1))
                        mm.then_inc(kv_ready.sem, 1)
                    average(lambda c: squares[:, c, :], 1)
                    pe.wait_ge(kv_copied.sem, kv_copied.at(i, TT))
                    pe.wait_ge(ktv_masked.sem, ktv_masked.before(i, 1))
                    for b in range(2):
                        for c in range(C):
                            for t in range(2):
                                mm = nc.tensor.matmul(ps_ktv[:, (b * C + c) * P:(b * C + c + 1) * P],
                                                      kv[:, 2 * b + t, c * P:(c + 1) * P],
                                                      kv[:, 2 * b + t, D + c * P:D + (c + 1) * P],
                                                      start=(t == 0), stop=(t == 1))
                    mm.then_inc(ktv_ready.sem, 1)
                    pe.wait_ge(normed_done.sem, normed_done.at(i, 1))
                    for m in range(C):
                        pe.wait_ge(q_copied.sem, q_copied.before(i, 5 + m))
                        for c in range(C):
                            mm = nc.tensor.matmul(ps_q[m][:], wq[:, c, m * P:(m + 1) * P], normed[:, c, :],
                                                  start=(c == 0), stop=(c == C - 1))
                        mm.then_inc(q_ready.sem, 1)
                    pe.wait_ge(ktv_masked.sem, ktv_masked.at(i, 1))
                    for c in range(C):
                        pe.wait_ge(q_copied.sem, q_copied.at(i, 1 + c))
                        for b in range(2):
                            mm = nc.tensor.matmul(ps_q[c][:, b * S:(b + 1) * S], ktv[:, b * C + c, :],
                                                  qT[:, c, b * S:(b + 1) * S], start=True, stop=True)
                        mm.then_inc(q_ready.sem, 1)
                    pe.wait_ge(q_copied.sem, q_copied.at(i, 4))
                    for m in range(C):
                        pe.wait_ge(added.sem, added.before(i, C) if m == 0 else added.at(i, m))
                        for c in range(C):
                            mm = nc.tensor.matmul(ps_o[:], wo[:, c, m * P:(m + 1) * P], aT[:, c, :],
                                                  start=(c == 0), stop=(c == C - 1))
                        mm.then_inc(o_ready.sem, 1)
                    pe.wait_ge(added.sem, added.at(i, C))
                    average(lambda c: now_x(i, c), 2)
                    average(lambda c: squares[:, c, :], 3)
                    pe.wait_ge(normed_done.sem, normed_done.at(i, 2))
                    pe.wait_ge(logit_done.sem, logit_done.before(i, 1))
                    for t in range(TT):
                        for c in range(C):
                            mm = nc.tensor.matmul(ps_logit[:, t * E:(t + 1) * E], normed[:, c, t * P:(t + 1) * P],
                                                  wg[:, c, :], start=(c == 0), stop=(c == C - 1))
                    mm.then_inc(logit_ready.sem, 1)
                    for h in range(2):
                        for t in range(2):
                            for c in range(C):
                                mm = nc.tensor.transpose(ps_q[h][:, (t * C + c) * P:(t * C + c + 1) * P],
                                                         normed[:, c, (2 * h + t) * P:(2 * h + t + 1) * P],
                                                         sh["mat"]("ident"))
                        mm.then_inc(q_ready.sem, 1)

            @block.scalar
            def _(act):
                start_ahead(act, [kv_copied, squared, q_copied, logged, rstd_done])
                act.wait_ge(loaded, nloads)
                act.wait_ge(eps_set, 1)
                nc.scalar.activation(sh["tanh"][:], gin[:], ACT.Tanh).then_inc(gates, 1)
                nc.scalar.preload_act_table_set(LOG_EXP)
                with act.Fori(0, PAIRS) as i:
                    def square(n):
                        act.wait_ge(centred_done.sem, centred_done.at(i, n))
                        nc.scalar.activation(squares[:], centred[:], ACT.Square).then_inc(squared.sem, 1)

                    def deviate(n):
                        act.wait_ge(norm_ready.sem, norm_ready.at(i, 2 * n + 2))
                        nc.scalar.activation(log[:], ps_norm[:], ACT.Ln, bias=sh["eps"][:]).then_inc(logged.sem, 1)
                        act.wait_ge(logged.sem, logged.at(i, n + 1))
                        nc.scalar.activation(rstd[:], log[:], ACT.Exp, scale=-0.5).then_inc(rstd_done.sem, 1)

                    for t in range(TT):
                        act.wait_ge(kv_ready.sem, kv_ready.at(i, t + 1))
                        act.wait_ge(ktv_ready.sem, ktv_ready.before(i, 1))
                        nc.scalar.copy(kv[:, t, :], ps_kv[t % 2][:]).then_inc(kv_copied.sem, 1)
                        if t == 0:
                            square(1)
                    deviate(0)
                    for c in range(C):
                        act.wait_ge(q_ready.sem, q_ready.at(i, 1 + c))
                        nc.scalar.copy(qT[:, c, :], ps_q[c][:]).then_inc(q_copied.sem, 1)
                    for c in range(C):
                        act.wait_ge(q_ready.sem, q_ready.at(i, 3 + c))
                        nc.scalar.copy(aT[:, c, :], ps_q[c][:]).then_inc(q_copied.sem, 1)
                    square(2)
                    deviate(1)
                    for h in range(2):
                        act.wait_ge(q_ready.sem, q_ready.at(i, 5 + h))
                        act.sem_inc(waited, 1)
                        nc.scalar.copy(sh["rows"][:, bass.ds(i * TT + 2 * h, 2), :],
                                       ps_q[h][:].rearrange("p (t n) -> p t n", t=2)).then_inc(q_copied.sem, 1)

            @block.vector
            def _(dve):
                start_ahead(dve, [ktv_masked, centred_done, normed_done, added, logit_done])
                dve.wait_ge(loaded, nloads)
                dve.wait_ge(gates, 1)
                with dve.Fori(0, PAIRS) as i:
                    def centre(n):
                        dve.wait_ge(norm_ready.sem, norm_ready.at(i, 2 * n + 1))
                        if n:
                            dve.wait_ge(added.sem, added.at(i, C))
                        nc.vector.tensor_tensor(centred[:], x_all[:, :, bass.ds(i * W, W)],
                                                spread(ps_norm[:], C, 1), ALU.subtract).then_inc(centred_done.sem, 1)

                    def normalise(n):
                        dve.wait_ge(rstd_done.sem, rstd_done.at(i, n + 1))
                        dve.wait_ge(q_ready.sem, q_ready.before(i, 6) if n == 0 else q_ready.at(i, 2))
                        nc.vector.tensor_tensor(normed[:], centred[:], spread(rstd[:], C, 1),
                                                ALU.mult).then_inc(normed_done.sem, 1)

                    centre(0)
                    normalise(0)
                    dve.wait_ge(ktv_ready.sem, ktv_ready.at(i, 1))
                    nc.vector.tensor_tensor(ktv[:], ps_ktv[:].rearrange("p (n m) -> p n m", m=P),
                                            spread(sh["mat"]("heads16"), 2 * C, 1), ALU.mult).then_inc(ktv_masked.sem, 1)
                    for m in range(C):
                        dve.wait_ge(o_ready.sem, o_ready.at(i, m + 1))
                        nc.vector.scalar_tensor_tensor(now_x(i, m), ps_o[:], sh["tanh"][:, 0:1], now_x(i, m),
                                                       ALU.mult, ALU.add).then_inc(added.sem, 1)
                    centre(1)
                    normalise(1)
                    dve.wait_ge(logit_ready.sem, logit_ready.at(i, 1))
                    nc.vector.tensor_tensor(sh["logits"][:, bass.ds(i * TT, TT), :],
                                            ps_logit[:, 0:TT * E].rearrange("p (t e) -> p t e", e=E),
                                            spread(bg[:], TT, 1), ALU.add).then_inc(logit_done.sem, 1)


def route(nc, io, sh):
    with ExitStack() as st:
        def sb(name, shape, dt=F32):
            return st.enter_context(nc.sbuf_tensor("r_" + name, shape, dt))

        best = sb("best", [P, NT])
        tied = sb("tied", [P, NT, E])
        rank = sb("rank", [P, NT])
        chosen = sb("chosen", [P, NT, E])
        total = sb("total", [P, NT, E])
        ahead = sb("ahead", [P, NT + 1, E])
        full = sb("full", [P, E, NT])
        tiles = sb("tiles", [P, E])
        first = sb("first", [P, E + 1])
        base = sb("base", [P, E])
        place = sb("place", [P, NT, E])
        slot = sb("slot", [P, NT])
        begun = sb("begun", [P, SLOTS, E - 1])
        owner = sb("owner", [P, SLOTS])
        ps_before = st.enter_context(nc.psum_tensor("r_ps_before", [P, 512], F32))
        ps_total = st.enter_context(nc.psum_tensor("r_ps_total", [P, 512], F32))
        chain = st.enter_context(nc.semaphore("r_chain"))
        counted = st.enter_context(nc.semaphore("r_counted"))
        picked = st.enter_context(nc.semaphore("r_picked"))
        slots_done = st.enter_context(nc.semaphore("r_slots_done"))
        scattered = st.enter_context(nc.semaphore("r_scattered"))
        small = sh["small"]
        order, steps, numbers = small[:, 0:E], small[:, E:E + NT], small[:, E + NT:E + NT + SLOTS]

        with nc.Block() as block:
            @block.vector
            def _(dve):
                made = [0]

                def then(op):
                    made[0] += 1
                    op.then_inc(chain, 1)
                    dve.wait_ge(chain, made[0])

                logits = sh["logits"]
                then(nc.vector.tensor_reduce(best[:], logits[:], AX.X, ALU.max))
                then(nc.vector.tensor_tensor(tied[:], logits[:], spread(best[:], E, 2), ALU.is_ge))
                then(nc.vector.tensor_tensor(tied[:], tied[:], spread(order, NT, 1), ALU.mult))
                then(nc.vector.tensor_reduce(rank[:], tied[:], AX.X, ALU.max))
                nc.vector.tensor_tensor(chosen[:], tied[:], spread(rank[:], E, 2), ALU.is_equal).then_inc(picked, 1)
                nc.vector.memset(ahead[:, 0, :], 0.0)
                nc.vector.memset(first[:, 0:1], 0.0)
                dve.wait_ge(counted, 1)
                then(nc.vector.tensor_copy(total[:], ps_total[:, 0:NT * E].rearrange("p (t e) -> p t e", e=E)))
                for t in range(NT):
                    then(nc.vector.tensor_tensor(ahead[:, t + 1, :], ahead[:, t, :], total[:, t, :], ALU.add))
                then(nc.vector.tensor_tensor(full[:], spread(ahead[:, NT, :], NT, 2), spread(steps, E, 1), ALU.is_gt))
                then(nc.vector.tensor_reduce(tiles[:], full[:], AX.X, ALU.add))
                for e in range(E):
                    then(nc.vector.tensor_tensor(first[:, e + 1:e + 2], first[:, e:e + 1], tiles[:, e:e + 1], ALU.add))
                then(nc.vector.tensor_scalar(base[:], first[:, 0:E], float(P), None, ALU.mult))
                then(nc.vector.tensor_tensor(place[:], ps_before[:, 0:NT * E].rearrange("p (t e) -> p t e", e=E),
                                             ahead[:, 0:NT, :], ALU.add))
                then(nc.vector.tensor_tensor(place[:], place[:], spread(base[:], NT, 1), ALU.add))
                then(nc.vector.tensor_tensor(place[:], place[:], chosen[:], ALU.mult))
                then(nc.vector.tensor_reduce(slot[:], place[:], AX.X, ALU.add))
                nc.vector.tensor_copy(sh["slot"][:], slot[:]).then_inc(slots_done, 1)
                then(nc.vector.tensor_tensor(begun[:], spread(numbers, E - 1, 2), spread(first[:, 1:E], SLOTS, 1),
                                             ALU.is_ge))
                then(nc.vector.tensor_reduce(owner[:], begun[:], AX.X, ALU.add))
                then(nc.vector.tensor_copy(sh["owner"][:], owner[:]))

            @block.tensor
            def _(pe):
                pe.wait_ge(picked, 1)
                rhs = chosen[:].rearrange("p t e -> p (t e)")
                nc.tensor.matmul(ps_before[:, 0:NT * E], sh["mat"]("before"), rhs, start=True, stop=True)
                nc.tensor.matmul(ps_total[:, 0:NT * E], sh["mat"]("ones"), rhs, start=True, stop=True).then_inc(counted, 1)

            @block.gpsimd
            def _(pool):
                pool.wait_ge(slots_done, 1)
                for t in range(NT):
                    nc.gpsimd.indirect_dma_start(
                        sh["sorted_x"], bass.IndirectOffsetOnAxis(ap=sh["slot"][:, t:t + 1], axis=0),
                        sh["rows"][:, t, :], None).then_inc(scattered, 16)
                pool.wait_ge(scattered, 16 * NT)


def experts(nc, io, sh):
    with ExitStack() as st:
        def sb(name, shape, dt=F32):
            return st.enter_context(nc.sbuf_tensor("m_" + name, shape, dt))

        def pb(name):
            return st.enter_context(nc.psum_tensor("m_" + name, [P, 512], F32))

        def sem(name):
            return st.enter_context(nc.semaphore("m_" + name))

        U = UNROLL
        w1 = [sb(f"w1_{u}", [P, C, FF]) for u in range(U)]
        w2 = [sb(f"w2_{u}", [P, FC, D]) for u in range(U)]
        b1 = [sb(f"b1_{u}", [P, FC]) for u in range(U)]
        b2 = [sb(f"b2_{u}", [P, D]) for u in range(U)]
        xr = [sb(f"xr_{u}", [P, D]) for u in range(U)]
        xt = [sb(f"xt_{u}", [P, C, P]) for u in range(U)]
        hid = [sb(f"hid_{u}", [P, FC, P]) for u in range(U)]
        y = [sb(f"y_{u}", [P, D]) for u in range(U)]
        NH = 4
        ps_t = pb("ps_t")
        ps_h = [pb(f"ps_h{i}") for i in range(NH)]
        ps_y = [pb(f"ps_y{i}") for i in range(U)]

        rows_in, weights_in = [sem(f"rows_in{u}") for u in range(U)], [sem(f"weights_in{u}") for u in range(U)]
        stored = [sem(f"stored{u}") for u in range(U)]
        turned = Signal(st, nc, "m_turned", U)
        turned_copied = Signal(st, nc, "m_turned_copied", U)
        hid_ready = Signal(st, nc, "m_hid_ready", U * FC)
        gelu_done = Signal(st, nc, "m_gelu_done", U * FC)
        y_ready = Signal(st, nc, "m_y_ready", U)
        y_done = Signal(st, nc, "m_y_done", U)

        with nc.Block() as block:
            @block.sync
            def _(sp):
                with sp.Fori(0, SLOTS // U) as i:
                    for u in range(U):
                        sp.wait_ge(turned.sem, turned.before(i, u + 1))
                        sp.dma_start(xr[u][:], sh["sorted_x"][bass.ds((i * U + u) * P, P), :]).then_inc(rows_in[u], 16)
                        e = sp.value_load(sh["owner"][0:1, bass.ds(i * U + u, 1)], min_val=0, max_val=E - 1)
                        sp.wait_ge(y_ready.sem, y_ready.before(i, u + 1))
                        sp.dma_start(w1[u][:], io["W1"][bass.ds(e, 1), :, :].rearrange("e (c p) n -> p (e c) n", p=P)).then_inc(weights_in[u], 16)
                        sp.dma_start(b1[u][:], io["b1"][bass.ds(e, 1), :, :].rearrange("e p c -> p (e c)")).then_inc(weights_in[u], 16)
                        sp.dma_start(w2[u][:], io["W2"][bass.ds(e, 1), :, :].rearrange("e (c p) n -> p (e c) n", p=P)).then_inc(weights_in[u], 16)
                        sp.wait_ge(y_done.sem, y_done.before(i, u + 1))
                        sp.dma_start(b2[u][:], io["b2"][bass.ds(e, 1), :].to_broadcast([P, D])).then_inc(weights_in[u], 16)

            @block.gpsimd
            def _(pool):
                with pool.Fori(0, SLOTS // U) as i:
                    for u in range(U):
                        pool.wait_ge(y_done.sem, y_done.at(i, u + 1))
                        pool.dma_start(sh["sorted_y"][bass.ds((i * U + u) * P, P), :], y[u][:]).then_inc(stored[u], 16)
                for u in range(U):
                    pool.wait_ge(stored[u], 16 * (SLOTS // U))

            @block.tensor
            def _(pe):
                start_ahead(pe, [turned, hid_ready, y_ready])
                with pe.Fori(0, SLOTS // U) as i:
                    for u in range(U):
                        pe.wait_ge(rows_in[u], i * 16 + 16)
                        pe.wait_ge(turned_copied.sem, turned_copied.at(i, u))
                        for c in range(C):
                            mm = nc.tensor.transpose(ps_t[:, c * P:(c + 1) * P], xr[u][:, c * P:(c + 1) * P], sh["mat"]("ident"))
                        mm.then_inc(turned.sem, 1)
                        pe.wait_ge(turned_copied.sem, turned_copied.at(i, u + 1))
                        pe.wait_ge(weights_in[u], i * 64 + 64)
                        for m in range(FC):
                            k = u * FC + m
                            pe.wait_ge(gelu_done.sem, gelu_done.at(i, k + 1 - NH))
                            for c in range(C):
                                mm = nc.tensor.matmul(ps_h[m % NH][:, 0:P], w1[u][:, c, m * P:(m + 1) * P], xt[u][:, c, :],
                                                      start=(c == 0), stop=(c == C - 1))
                            mm.then_inc(hid_ready.sem, 1)
                        pe.wait_ge(y_done.sem, y_done.at(i, u + 1 - U))
                        for m in range(FC):
                            pe.wait_ge(gelu_done.sem, gelu_done.at(i, u * FC + m + 1))
                            mm = nc.tensor.matmul(ps_y[u][:, 0:D], hid[u][:, m, :], w2[u][:, m, :],
                                                  start=(m == 0), stop=(m == FC - 1))
                        mm.then_inc(y_ready.sem, 1)

            @block.scalar
            def _(act):
                start_ahead(act, [gelu_done])
                with act.Fori(0, SLOTS // U) as i:
                    for u in range(U):
                        act.wait_ge(weights_in[u], i * 64 + 64)
                        for m in range(FC):
                            act.wait_ge(hid_ready.sem, hid_ready.at(i, u * FC + m + 1))
                            if m == 0:
                                act.wait_ge(y_ready.sem, y_ready.at(i, u + 1 - U))
                            nc.scalar.activation(hid[u][:, m, :], ps_h[m % NH][:, 0:P], ACT.Gelu,
                                                 bias=b1[u][:, m:m + 1]).then_inc(gelu_done.sem, 1)

            @block.vector
            def _(dve):
                start_ahead(dve, [turned_copied, y_done])
                with dve.Fori(0, SLOTS // U) as i:
                    for u in range(U):
                        dve.wait_ge(turned.sem, turned.at(i, u + 1))
                        dve.wait_ge(hid_ready.sem, hid_ready.before(i, (u + 1) * FC))
                        nc.vector.tensor_copy(xt[u][:], ps_t[:, 0:D].rearrange("p (c t) -> p c t", c=C)).then_inc(turned_copied.sem, 1)
                        dve.wait_ge(y_ready.sem, y_ready.at(i, u + 1))
                        dve.wait_ge(weights_in[u], i * 64 + 64)
                        dve.wait_ge(stored[u], i * 16)
                        nc.vector.tensor_tensor(y[u][:], ps_y[u][:, 0:D], b2[u][:], ALU.add).then_inc(y_done.sem, 1)


def attend_heads(nc, io, sh):
    with ExitStack() as st:
        def sb(name, shape, dt=F32):
            return st.enter_context(nc.sbuf_tensor("h_" + name, shape, dt))

        def pb(name):
            return st.enter_context(nc.psum_tensor("h_" + name, [P, 512], F32))

        def sig(name, per):
            return Signal(st, nc, "h_" + name, per)

        G = 32
        UNITS = TT
        HP = H1 // 2
        STEPS = UNITS * HP
        LAG_T, LAG_V = 2, 3
        OW = D1 + 1

        wq, wkv, wp = sb("wq", [P, C, D]), sb("wkv", [P, C, 2 * D]), sb("wp", [P, C, D])
        cols = sb("cols", [P, 4])
        scaled = sb("scaled", [P, 8])
        sums = sb("sums", [P, C, H1])
        ctx = sb("ctx", [P, C, W])
        taken = sb("taken", [P, TT, D])
        index = sb("index", [P, TT], I32)
        centred, squares = sb("centred", [P, C, W]), sb("squares", [P, C, W])
        log, rstd, normed = sb("log", [P, W]), sb("rstd", [P, W]), sb("normed", [P, C, W])
        hlog = [sb(f"hlog{i}", [P, W]) for i in range(2)]
        sq = [sb(f"sq{i}", [P, W]) for i in range(2)]
        hrstd = [sb(f"hrstd{i}", [P, W]) for i in range(2)]
        hn = [sb(f"hn{i}", [P, W]) for i in range(2)]
        qT = sb("qT", [P, C, W])
        kT = [sb(f"kT{i}", [P, C, W]) for i in range(2)]
        V = sb("V", [P, TT, H1, OW])
        peak = sb("peak", [P, 3, 2])
        prob = [sb(f"prob{i}", [P, 2, S]) for i in range(3)]
        probT = [sb(f"probT{i}", [P, 2, 2, P]) for i in range(2)]
        rsum = sb("rsum", [P, 2, H1])
        on = [sb(f"on{i}", [P, D]) for i in range(2)]
        oT = sb("oT", [P, C, W])

        ps_s = [pb(f"ps_s{i}") for i in range(3)]
        ps_t = [pb(f"ps_t{i}") for i in range(2)]
        ps_o = [pb(f"ps_o{i}") for i in range(2)]
        ps_g = pb("ps_g")

        loaded = st.enter_context(nc.semaphore("h_loaded"))
        prepared = st.enter_context(nc.semaphore("h_prepared"))
        ctx_in = st.enter_context(nc.semaphore("h_ctx_in"))
        rows_in = st.enter_context(nc.semaphore("h_rows_in"))
        waited = st.enter_context(nc.semaphore("h_waited"))
        index_done = st.enter_context(nc.semaphore("h_index_done"))
        y_turned = sig("y_turned", C)
        y_added = sig("y_added", C)
        norm_ready = sig("norm_ready", 2)
        centred_done = sig("centred_done", 1)
        squared = sig("squared", 1)
        logged = sig("logged", 1)
        rstd_done = sig("rstd_done", 1)
        normed_done = sig("normed_done", 1)
        v_ready = sig("v_ready", 2)
        v_copied = sig("v_copied", 2)
        proj_ready = sig("proj_ready", 4)
        head_squared = sig("head_squared", 4)
        head_var = sig("head_var", 4)
        head_logged = sig("head_logged", 4)
        head_rstd = sig("head_rstd", 4)
        head_normed = sig("head_normed", 4)
        head_out = sig("head_out", 6)
        s_ready = sig("s_ready", STEPS)
        peaked = sig("peaked", STEPS)
        exp_done = sig("exp_done", 2 * STEPS)
        t_ready = sig("t_ready", STEPS)
        t_copied = sig("t_copied", STEPS)
        pv_ready = sig("pv_ready", STEPS)
        summed = sig("summed", UNITS)
        o_done = sig("o_done", UNITS)
        o_turned = sig("o_turned", UNITS)
        o_copied = sig("o_copied", UNITS)
        out_ready = sig("out_ready", C)
        added = sig("added", C)

        x_all = sh["x"]

        def now_x(i, c):
            return x_all[:, c, bass.ds(i * W, W)]

        def tail(engine_tick):
            for s in range(STEPS + LAG_V + 1):
                engine_tick(s)

        with nc.Block() as block:
            @block.sync
            def _(sp):
                for to, of in [(wq, io["L1_Wq"]), (wkv, io["L1_Wkv"]), (wp, io["L1_Wp"])]:
                    sp.dma_start(to[:], of.rearrange("(c p) n -> p c n", p=P)).then_inc(loaded, 16)
                sp.dma_start(cols[:], io["L1_cols"]).then_inc(loaded, 16)
                with sp.Fori(0, PAIRS) as i:
                    sp.wait_ge(proj_ready.sem, proj_ready.before(i, 2))
                    sp.dma_start(ctx[:], io["ctxT"][:, :, bass.ds(i * W, W)]).then_inc(ctx_in, 16)

            @block.gpsimd
            def _(pool):
                with pool.Fori(0, PAIRS) as i:
                    pool.wait_ge(y_turned.sem, y_turned.before(i, C))
                    pool.wait_ge(rows_in, i * (16 * TT))
                    nc.gpsimd.tensor_copy(index[:], sh["slot"][:, bass.ds(i * TT, TT)]).then_inc(index_done, 1)
                    pool.wait_ge(index_done, i + 1)
                    pool.sem_inc(waited, 1)
                    for t in range(TT):
                        nc.gpsimd.indirect_dma_start(
                            taken[:, t, :], None, sh["sorted_y"],
                            bass.IndirectOffsetOnAxis(ap=index[:, t:t + 1], axis=0)).then_inc(rows_in, 16)

            @block.tensor
            def _(pe):
                start_ahead(pe, [y_turned, norm_ready, v_ready, proj_ready, head_var, s_ready, t_ready, pv_ready,
                                 o_turned, out_ready])
                pe.wait_ge(prepared, 1)
                pe.wait_ge(loaded, 64)
                mean256, mean16, ident = sh["mat"]("mean256"), sh["mat"]("mean16"), sh["mat"]("ident")
                with pe.Fori(0, PAIRS) as i:
                    pe.wait_ge(rows_in, i * (16 * TT) + 16 * TT)
                    pe.wait_ge(t_copied.sem, t_copied.at(i, 0))
                    for c in range(C):
                        for t in range(TT):
                            mm = nc.tensor.transpose(ps_t[c][:, t * P:(t + 1) * P], taken[:, t, c * P:(c + 1) * P], ident)
                        mm.then_inc(y_turned.sem, 1)
                    pe.wait_ge(ctx_in, i * 16 + 16)
                    for g in range(2):
                        pe.wait_ge(y_added.sem, y_added.at(i, g + 1))
                        for t in range(2):
                            for c in range(C):
                                mm = nc.tensor.matmul(ps_t[g][:, t * D:(t + 1) * D],
                                                      ctx[:, c, (2 * g + t) * P:(2 * g + t + 1) * P], wkv[:, c, D:2 * D],
                                                      start=(c == 0), stop=(c == C - 1))
                        mm.then_inc(v_ready.sem, 1)
                    pe.wait_ge(added.sem, added.at(i, 0))
                    pe.wait_ge(o_copied.sem, o_copied.at(i, 0))
                    for c in range(C):
                        mm = nc.tensor.matmul(ps_g[:], mean256, now_x(i, c), start=(c == 0), stop=(c == C - 1))
                    mm.then_inc(norm_ready.sem, 1)

                    def project(g):
                        if g < 2:
                            pe.wait_ge(v_copied.sem, v_copied.at(i, g + 1))
                        else:
                            pe.wait_ge(head_normed.sem, head_normed.at(i, g - 1))
                        for c in range(C):
                            w, of = (wkv, ctx) if g < 2 else (wq, normed)
                            mm = nc.tensor.matmul(ps_t[g % 2][:], w[:, c, (g % 2) * P:(g % 2 + 1) * P], of[:, c, :],
                                                  start=(c == 0), stop=(c == C - 1))
                        mm.then_inc(proj_ready.sem, 1)

                    def head_variance(g):
                        pe.wait_ge(head_squared.sem, head_squared.at(i, g + 1))
                        pe.wait_ge(head_rstd.sem, head_rstd.at(i, g - 1))
                        nc.tensor.matmul(ps_o[g % 2][:], mean16, sq[g % 2][:], start=True, stop=True).then_inc(head_var.sem, 1)

                    project(0)
                    project(1)
                    pe.wait_ge(squared.sem, squared.at(i, 1))
                    for c in range(C):
                        mm = nc.tensor.matmul(ps_g[:], mean256, squares[:, c, :], start=(c == 0), stop=(c == C - 1))
                    mm.then_inc(norm_ready.sem, 1)
                    pe.wait_ge(o_done.sem, o_done.at(i, 0))
                    head_variance(0)
                    head_variance(1)
                    pe.wait_ge(normed_done.sem, normed_done.at(i, 1))
                    project(2)
                    project(3)
                    head_variance(2)
                    head_variance(3)
                    pe.wait_ge(head_out.sem, head_out.at(i, 6))

                    def tick(s):
                        if s < STEPS:
                            u, hp = s // HP, s % HP
                            c, r = hp // 4, G * (hp % 4)
                            pe.wait_ge(exp_done.sem, exp_done.at(i, 2 * (s - 2)))
                            for h in range(2):
                                mm = nc.tensor.matmul(ps_s[s % 3][:, h * S:(h + 1) * S],
                                                      qT[r:r + G, c, u * P:(u + 1) * P],
                                                      kT[h][r:r + G, c, (u // 2) * S:(u // 2 + 1) * S],
                                                      start=True, stop=True)
                            mm.then_inc(s_ready.sem, 1)
                        if LAG_T <= s < STEPS + LAG_T:
                            n = s - LAG_T
                            if n < 2:
                                pe.wait_ge(head_normed.sem, head_normed.at(i, 4))
                            else:
                                pe.wait_ge(t_copied.sem, t_copied.at(i, n - 1))
                            pe.wait_ge(exp_done.sem, exp_done.at(i, 2 * n + 2))
                            for h in range(2):
                                for k in range(2):
                                    mm = nc.tensor.transpose(ps_t[n % 2][:, (2 * h + k) * P:(2 * h + k + 1) * P],
                                                             prob[n % 3][:, h, k * P:(k + 1) * P], ident)
                            mm.then_inc(t_ready.sem, 1)
                        if LAG_V <= s < STEPS + LAG_V:
                            n = s - LAG_V
                            u, hp = n // HP, n % HP
                            if hp == 0:
                                pe.wait_ge(o_done.sem, o_done.at(i, u - 1))
                            pe.wait_ge(t_copied.sem, t_copied.at(i, n + 1))
                            for h in range(2):
                                head = 2 * hp + h
                                for k in range(2):
                                    mm = nc.tensor.matmul(ps_o[u % 2][:, head * OW:(head + 1) * OW], probT[n % 2][:, h, k, :],
                                                          V[:, 2 * (u // 2) + k, head, :], start=(k == 0), stop=(k == 1))
                            mm.then_inc(pv_ready.sem, 1)
                        if s > LAG_V and (s - LAG_V) % HP == 0 or s == STEPS + LAG_V:
                            u = (s - LAG_V) // HP - 1
                            pe.wait_ge(o_done.sem, o_done.at(i, u + 1))
                            pe.wait_ge(o_copied.sem, o_copied.at(i, u))
                            for c in range(C):
                                mm = nc.tensor.transpose(ps_g[:, c * P:(c + 1) * P], on[u % 2][:, c * P:(c + 1) * P], ident)
                            mm.then_inc(o_turned.sem, 1)

                    for s in range(STEPS + LAG_V + 1):
                        tick(s)
                    pe.wait_ge(o_copied.sem, o_copied.at(i, UNITS))
                    for m in range(C):
                        pe.wait_ge(added.sem, added.at(i, m))
                        for c in range(C):
                            mm = nc.tensor.matmul(ps_g[:], wp[:, c, m * P:(m + 1) * P], oT[:, c, :],
                                                  start=(c == 0), stop=(c == C - 1))
                        mm.then_inc(out_ready.sem, 1)

            @block.scalar
            def _(act):
                start_ahead(act, [squared, v_copied, head_squared, head_out, exp_done, o_copied, logged, rstd_done,
                                  head_logged, head_rstd])
                nc.scalar.preload_act_table_set(LOG_EXP)
                act.wait_ge(prepared, 1)
                with act.Fori(0, PAIRS) as i:
                    for g in range(2):
                        act.wait_ge(v_ready.sem, v_ready.at(i, g + 1))
                        nc.scalar.copy(V[:, 2 * g:2 * g + 2, :, 0:D1],
                                       ps_t[g][:].rearrange("p (t h d) -> p t h d", t=2, d=D1)).then_inc(v_copied.sem, 1)

                    def head_square(g):
                        act.wait_ge(proj_ready.sem, proj_ready.at(i, g + 1))
                        act.wait_ge(head_var.sem, head_var.at(i, g - 1))
                        nc.scalar.activation(sq[g % 2][:], ps_t[g % 2][:], ACT.Square).then_inc(head_squared.sem, 1)

                    def scale_shift(out, g, n):
                        act.wait_ge(head_normed.sem, head_normed.at(i, g + 1))
                        nc.scalar.activation(out, hn[g % 2][:], ACT.Identity, scale=scaled[:, 2 * n:2 * n + 1],
                                             bias=scaled[:, 2 * n + 1:2 * n + 2]).then_inc(head_out.sem, 1)

                    head_square(0)
                    act.wait_ge(centred_done.sem, centred_done.at(i, 1))
                    nc.scalar.activation(squares[:], centred[:], ACT.Square).then_inc(squared.sem, 1)
                    head_square(1)
                    act.wait_ge(norm_ready.sem, norm_ready.at(i, 2))
                    nc.scalar.activation(log[:], ps_g[:], ACT.Ln, bias=sh["eps"][:]).then_inc(logged.sem, 1)
                    act.wait_ge(logged.sem, logged.at(i, 1))
                    nc.scalar.activation(rstd[:], log[:], ACT.Exp, scale=-0.5).then_inc(rstd_done.sem, 1)

                    def head_deviate(g):
                        act.wait_ge(head_var.sem, head_var.at(i, g + 1))
                        nc.scalar.activation(hlog[g % 2][:], ps_o[g % 2][:], ACT.Ln, bias=sh["eps"][:]).then_inc(head_logged.sem, 1)
                        act.wait_ge(head_logged.sem, head_logged.at(i, g + 1))
                        act.wait_ge(head_normed.sem, head_normed.at(i, g - 1))
                        nc.scalar.activation(hrstd[g % 2][:], hlog[g % 2][:], ACT.Exp, scale=-0.5).then_inc(head_rstd.sem, 1)

                    head_deviate(0)
                    head_deviate(1)
                    for g in range(2):
                        scale_shift(kT[0][:, g, :], g, 1)
                        scale_shift(kT[1][:, g, :], g, 2)
                    head_square(2)
                    head_square(3)
                    head_deviate(2)
                    head_deviate(3)
                    for g in range(2):
                        scale_shift(qT[:, g, :], 2 + g, 0)

                    def tick(s):
                        if s < STEPS:
                            act.wait_ge(peaked.sem, peaked.at(i, s + 1))
                            act.wait_ge(t_ready.sem, t_ready.at(i, s - 2))
                            for h in range(2):
                                nc.scalar.activation(prob[s % 3][:, h, :], ps_s[s % 3][:, h * S:(h + 1) * S], ACT.Exp,
                                                     bias=peak[:, s % 3, h:h + 1]).then_inc(exp_done.sem, 1)
                        if s > LAG_V and (s - LAG_V) % HP == 0 or s == STEPS + LAG_V:
                            u = (s - LAG_V) // HP - 1
                            act.wait_ge(o_turned.sem, o_turned.at(i, u + 1))
                            nc.scalar.copy(oT[:, :, u * P:(u + 1) * P],
                                           ps_g[:, 0:D].rearrange("p (c t) -> p c t", c=C)).then_inc(o_copied.sem, 1)

                    for s in range(STEPS + LAG_V + 1):
                        tick(s)

            @block.vector
            def _(dve):
                start_ahead(dve, [y_added, centred_done, normed_done, head_normed, peaked,
                                  t_copied, summed, o_done, added])
                nc.vector.memset(V[:], 1.0)
                tanh = sh["tanh"]
                small = sh["small"]
                parity = small[:, SMALL - 2:SMALL]
                chain = st.enter_context(nc.semaphore("h_chain"))
                made = [0]

                def then(op):
                    made[0] += 1
                    op.then_inc(chain, 1)
                    dve.wait_ge(chain, made[0])

                dve.wait_ge(loaded, 64)
                for w in (wq[:], wkv[:, :, 0:D]):
                    heads = w.rearrange("p c (h d) -> p c h d", d=D1)
                    then(nc.vector.tensor_reduce(sums[:], heads, AX.X, ALU.add))
                    then(nc.vector.tensor_scalar(sums[:], sums[:], 1.0 / D1, None, ALU.mult))
                    then(nc.vector.tensor_tensor(heads, heads, spread(sums[:], D1, 3), ALU.subtract))
                then(nc.vector.tensor_scalar(scaled[:, 0:2], cols[:, 2:4], float(D1) ** 0.5, None, ALU.mult))
                for h in range(2):
                    then(nc.vector.tensor_scalar(scaled[:, 2 + 2 * h:4 + 2 * h], cols[:, 2:4], parity[:, h:h + 1], None, ALU.mult))
                then(nc.vector.tensor_scalar(scaled[:, 6:8], cols[:, 0:2], tanh[:, 2:3], None, ALU.mult))
                nc.vector.tensor_scalar(wp[:], wp[:], tanh[:, 2:3], None, ALU.mult).then_inc(prepared, 1)
                with dve.Fori(0, PAIRS) as i:
                    for c in range(C):
                        dve.wait_ge(y_turned.sem, y_turned.at(i, c + 1))
                        nc.vector.scalar_tensor_tensor(now_x(i, c), ps_t[c][:], tanh[:, 1:2], now_x(i, c),
                                                       ALU.mult, ALU.add).then_inc(y_added.sem, 1)
                    dve.wait_ge(norm_ready.sem, norm_ready.at(i, 1))
                    nc.vector.tensor_tensor(centred[:], x_all[:, :, bass.ds(i * W, W)], spread(ps_g[:], C, 1),
                                            ALU.subtract).then_inc(centred_done.sem, 1)

                    def head_norm(g):
                        dve.wait_ge(head_rstd.sem, head_rstd.at(i, g + 1))
                        dve.wait_ge(head_out.sem, head_out.at(i, g - 1) if g < 2 else head_out.at(i, 2 * g - 2))
                        nc.vector.tensor_tensor(hn[g % 2][:], ps_t[g % 2][:], hrstd[g % 2][:], ALU.mult).then_inc(head_normed.sem, 1)

                    dve.wait_ge(rstd_done.sem, rstd_done.at(i, 1))
                    nc.vector.tensor_tensor(normed[:], centred[:], spread(rstd[:], C, 1), ALU.mult).then_inc(normed_done.sem, 1)
                    for g in range(4):
                        head_norm(g)

                    def tick(s):
                        if s < STEPS:
                            dve.wait_ge(s_ready.sem, s_ready.at(i, s + 1))
                            nc.vector.tensor_reduce(peak[:, s % 3, :], ps_s[s % 3][:].rearrange("p (h k) -> p h k", h=2),
                                                    AX.X, ALU.max, negate=True).then_inc(peaked.sem, 1)
                        if LAG_T <= s < STEPS + LAG_T:
                            n = s - LAG_T
                            dve.wait_ge(t_ready.sem, t_ready.at(i, n + 1))
                            dve.wait_ge(pv_ready.sem, pv_ready.at(i, n - 1))
                            nc.vector.tensor_copy(probT[n % 2][:].rearrange("p h k q -> p (h k q)"), ps_t[n % 2][:]).then_inc(t_copied.sem, 1)
                        if s >= LAG_V and (s - LAG_V) % HP == HP - 1:
                            u = (s - LAG_V) // HP
                            dve.wait_ge(pv_ready.sem, pv_ready.at(i, (u + 1) * HP))
                            o = ps_o[u % 2][:, 0:H1 * OW].rearrange("p (h d) -> p h d", d=OW)
                            nc.vector.reciprocal(rsum[:, u % 2, :], o[:, :, D1]).then_inc(summed.sem, 1)
                            dve.wait_ge(summed.sem, summed.at(i, u + 1))
                            dve.wait_ge(o_turned.sem, o_turned.at(i, u - 1))
                            nc.vector.tensor_tensor(on[u % 2][:].rearrange("p (h d) -> p h d", d=D1), o[:, :, 0:D1],
                                                    spread(rsum[:, u % 2, :], D1, 2), ALU.mult).then_inc(o_done.sem, 1)

                    for s in range(STEPS + LAG_V + 1):
                        tick(s)
                    for m in range(C):
                        dve.wait_ge(out_ready.sem, out_ready.at(i, m + 1))
                        nc.vector.scalar_tensor_tensor(now_x(i, m), ps_g[:], scaled[:, 6 + m:7 + m], now_x(i, m),
                                                       ALU.add, ALU.add).then_inc(added.sem, 1)


def start_layers(nc, io, sh):
    with ExitStack() as st:
        def sig(name):
            return Signal(st, nc, "y_" + name, 2)

        centred, squares = ([st.enter_context(nc.sbuf_tensor(f"y_{n}{i}", [P, C, W], F32)) for i in range(2)]
                            for n in ("centred", "squares"))
        log, rstd = ([st.enter_context(nc.sbuf_tensor(f"y_{n}{i}", [P, W], F32)) for i in range(2)] for n in ("log", "rstd"))
        ps_mean, ps_var = ([st.enter_context(nc.psum_tensor(f"y_ps_{n}{i}", [P, W], F32)) for i in range(2)]
                           for n in ("mean", "var"))
        mean_ready, var_ready = sig("mean_ready"), sig("var_ready")
        centred_done, y_done = sig("centred_done"), sig("y_done")
        squared, logged, rstd_done = sig("squared"), sig("logged"), sig("rstd_done")
        x_all, y_all = sh["x"], sh["y"]

        def tokens(i, n):
            return bass.ds((2 * i + n) * W, W)

        with nc.Block() as block:
            @block.tensor
            def _(pe):
                start_ahead(pe, [mean_ready, var_ready])
                mean256 = sh["mat"]("mean256")
                with pe.Fori(0, PAIRS // 2) as i:
                    for n in range(2):
                        pe.wait_ge(centred_done.sem, centred_done.at(i, n - 1))
                        for c in range(C):
                            mm = nc.tensor.matmul(ps_mean[n][:], mean256, x_all[:, c, tokens(i, n)], start=(c == 0), stop=(c == C - 1))
                        mm.then_inc(mean_ready.sem, 1)
                    for n in range(2):
                        pe.wait_ge(squared.sem, squared.at(i, n + 1))
                        for c in range(C):
                            mm = nc.tensor.matmul(ps_var[n][:], mean256, squares[n][:, c, :], start=(c == 0), stop=(c == C - 1))
                        mm.then_inc(var_ready.sem, 1)

            @block.vector
            def _(dve):
                start_ahead(dve, [centred_done, y_done])
                with dve.Fori(0, PAIRS // 2) as i:
                    for n in range(2):
                        dve.wait_ge(mean_ready.sem, mean_ready.at(i, n + 1))
                        dve.wait_ge(y_done.sem, y_done.at(i, n - 1))
                        nc.vector.tensor_tensor(centred[n][:], x_all[:, :, tokens(i, n)], spread(ps_mean[n][:], C, 1),
                                                ALU.subtract).then_inc(centred_done.sem, 1)
                    for n in range(2):
                        dve.wait_ge(rstd_done.sem, rstd_done.at(i, n + 1))
                        nc.vector.tensor_tensor(y_all[:, :, tokens(i, n)], centred[n][:], spread(rstd[n][:], C, 1),
                                                ALU.mult).then_inc(y_done.sem, 1)

            @block.scalar
            def _(act):
                start_ahead(act, [squared, logged, rstd_done])
                with act.Fori(0, PAIRS // 2) as i:
                    for n in range(2):
                        act.wait_ge(centred_done.sem, centred_done.at(i, n + 1))
                        nc.scalar.activation(squares[n][:], centred[n][:], ACT.Square).then_inc(squared.sem, 1)
                    for n in range(2):
                        act.wait_ge(var_ready.sem, var_ready.at(i, n + 1))
                        nc.scalar.activation(log[n][:], ps_var[n][:], ACT.Ln, bias=sh["eps"][:]).then_inc(logged.sem, 1)
                        act.wait_ge(logged.sem, logged.at(i, n + 1))
                        nc.scalar.activation(rstd[n][:], log[n][:], ACT.Exp, scale=-0.5).then_inc(rstd_done.sem, 1)


def local_layers(nc, io, sh):
    with ExitStack() as st:
        def sb(name, shape, dt=F32):
            return st.enter_context(nc.sbuf_tensor("l_" + name, shape, dt))

        def pb(name):
            return st.enter_context(nc.psum_tensor("l_" + name, [P, 512], F32))

        def sem(name):
            return st.enter_context(nc.semaphore("l_" + name))

        def sig(name, per):
            return Signal(st, nc, "l_" + name, per)

        QC = INNER // P
        STEPS = 2 * H2
        LAG_T, LAG_V = 2, 3
        OW = D2 + 1
        PW = 3 * P

        wqkv, wo = sb("wqkv", [P, C, 3 * INNER]), sb("wo", [P, QC, D])
        w1, w2 = sb("w1", [P, C, 2 * HID]), sb("w2", [P, HC, D])
        cols = sb("cols", [P, 8 + 2 * HC])
        turn = [sb(f"turn{i}", [P, P]) for i in range(2)]
        tables = sb("tables", [P, 4, S])
        mask, mask16 = sb("mask", [P, 2 * S]), sb("mask16", [P, 2 * S], BF16)
        ident16 = sb("ident16", [P, P], BF16)
        hT, centred, squares = sb("hT", [P, C, W]), sb("centred", [P, C, W]), sb("squares", [P, C, W])
        log, rstd, normed, h2 = sb("log", [P, W]), sb("rstd", [P, W]), sb("normed", [P, C, W]), sb("h2", [P, C, W])
        V = sb("V", [P, TT, H2, OW])
        raw, sq, fl, ln, rn, ta, tb, tc = (
            [sb(f"{n}{i}", [P, W]) for i in range(2)] for n in ("raw", "sq", "fl", "ln", "rn", "ta", "tb", "tc"))
        qkT = sb("qkT", [P, 2 * QC, W])
        peak = sb("peak", [P, 3, 2])
        prob = [sb(f"prob{i}", [P, PW]) for i in range(3)]
        probT = [sb(f"probT{i}", [P, PW]) for i in range(2)]
        rsum = sb("rsum", [P, 2, 4])
        on = sb("on", [P, 2, 2, INNER])
        oT = sb("oT", [P, QC, W])
        gelu = [sb(f"gelu{i}", [P, W]) for i in range(2)]
        hid = sb("hid", [P, HC, W])

        ps_s = [pb(f"ps_s{i}") for i in range(3)]
        ps_t = [pb(f"ps_t{i}") for i in range(2)]
        ps_o = [pb(f"ps_o{i}") for i in range(2)]
        ps_g = pb("ps_g")

        tables_in, weights_in, stored = sem("tables_in"), sem("weights_in"), sem("stored")
        zeroed, mask_done = sem("zeroed"), sem("mask_done")
        turn_scaled, waited = sem("turn_scaled"), sem("waited")
        shifted = sig("shifted", 2)
        v_ready = sig("v_ready", TT)
        v_copied = sig("v_copied", TT)
        proj_ready = sig("proj_ready", 2 * QC)
        raw_done = sig("raw_done", 2 * QC)
        sq_done = sig("sq_done", 2 * QC)
        length_ready = sig("length_ready", 2 * QC)
        turned = sig("turned", 2 * QC)
        floored = sig("floored", 2 * QC)
        ln_done = sig("ln_done", 2 * QC)
        rn_done = sig("rn_done", 2 * QC)
        cos_done = sig("cos_done", 2 * QC)
        sin_done = sig("sin_done", 2 * QC)
        rope_sum = sig("rope_sum", 2 * QC)
        rope_done = sig("rope_done", 2 * QC)
        s_ready = sig("s_ready", STEPS)
        peaked = sig("peaked", STEPS)
        exp_done = sig("exp_done", 2 * STEPS)
        t_ready = sig("t_ready", STEPS)
        t_even = sig("t_even", STEPS // 2)
        t_odd = sig("t_odd", STEPS // 2)
        pv_ready = sig("pv_ready", STEPS)
        summed = sig("summed", STEPS // 2)
        o_done = sig("o_done", STEPS // 2)
        o_turned = sig("o_turned", TT)
        o_copied = sig("o_copied", TT)
        out_ready = sig("out_ready", C)
        added = sig("added", C)
        norm_ready = sig("norm_ready", 2)
        centred_done = sig("centred_done", 1)
        squared = sig("squared", 1)
        logged = sig("logged", 1)
        rstd_done = sig("rstd_done", 1)
        normed_done = sig("normed_done", 1)
        h2_done = sig("h2_done", C)
        g_ready = sig("g_ready", HC)
        a_ready = sig("a_ready", HC)
        gelu_done = sig("gelu_done", HC)
        hid_done = sig("hid_done", HC)
        ff_ready = sig("ff_ready", C)
        grown = sig("grown", C)

        x_all, y_all = sh["x"], sh["y"]

        def hrows(j):
            return P if j < HC - 1 else HL

        def now_y(i, c):
            return y_all[:, c, bass.ds(i * W, W)]

        def two(ap):
            return ap.rearrange("p (b t) -> p b t", b=2)

        def t_copied(n, step):
            s = t_odd if n % 2 else t_even
            return s.sem, s.at(step, n // 2 + 1)

        LOADS = 6
        with nc.Block() as block:
            @block.sync
            def _(sp):
                sp.dma_start(tables[:], io["rope"]).then_inc(tables_in, 16)
                sp.dma_start(mask[:], io["mask"]).then_inc(tables_in, 16)
                with sp.Fori(0, DEPTH) as l:
                    sp.wait_ge(grown.sem, grown.at(l * PAIRS, 0))
                    one = bass.ds(l, 1)
                    sp.dma_start(wqkv[:], io["F_wqkv"][one].rearrange("l (c p) n -> p (l c) n", p=P)).then_inc(weights_in, 16)
                    sp.dma_start(cols[:], io["F_cols"][one].rearrange("l p n -> p (l n)")).then_inc(weights_in, 16)
                    sp.dma_start(wo[:], io["F_wo"][one].rearrange("l (c p) n -> p (l c) n", p=P)).then_inc(weights_in, 16)
                    sp.dma_start(w1[:], io["F_w1"][one].rearrange("l (c p) n -> p (l c) n", p=P)).then_inc(weights_in, 16)
                    sp.dma_start(w2[:, 0:HC - 1, :], io["F_w2"][one, 0:HID - HL, :].rearrange("l (c p) n -> p (l c) n", p=P)).then_inc(weights_in, 16)
                    sp.dma_start(w2[0:HL, HC - 1, :], io["F_w2"][one, HID - HL:HID, :].rearrange("l p n -> p (l n)")).then_inc(weights_in, 16)

            @block.tensor
            def _(pe):
                start_ahead(pe, [v_ready, proj_ready, length_ready, turned, s_ready, t_ready, pv_ready, o_turned,
                                 out_ready, norm_ready, g_ready, a_ready, ff_ready])
                mean256, heads64, ident = sh["mat"]("mean256"), sh["mat"]("heads64"), sh["mat"]("ident")
                pe.wait_ge(mask_done, 1)
                with pe.Fori(0, DEPTH) as l:
                    with pe.Fori(0, PAIRS) as pair:
                        i = l * PAIRS + pair
                        pe.wait_ge(weights_in, l * (16 * LOADS) + 16 * LOADS)
                        pe.wait_ge(turn_scaled, l * 2 + 2)
                        pe.wait_ge(shifted.sem, shifted.at(i, 1))
                        for t in range(TT):
                            pe.wait_ge(v_copied.sem, v_copied.at(i, t - 1))
                            if t == 0:
                                pe.wait_ge(hid_done.sem, hid_done.at(i, 0))
                            for c in range(C):
                                mm = nc.tensor.matmul(ps_s[t % 2][:], hT[:, c, t * P:(t + 1) * P], wqkv[:, c, 2 * INNER:],
                                                      start=(c == 0), stop=(c == C - 1))
                            mm.then_inc(v_ready.sem, 1)

                        def rope(g):
                            pe.wait_ge(raw_done.sem, raw_done.at(i, g + 1))
                            if g < 2:
                                pe.wait_ge(v_copied.sem, v_copied.at(i, TT))
                            else:
                                pe.wait_ge(sin_done.sem, sin_done.at(i, g - 1))
                            nc.tensor.matmul(ps_s[g % 2][:], turn[g // QC][:], raw[g % 2][:], start=True, stop=True).then_inc(turned.sem, 1)
                            pe.wait_ge(sq_done.sem, sq_done.at(i, g + 1))
                            if g < 2:
                                pe.wait_ge(grown.sem, grown.at(i, 0))
                            else:
                                pe.wait_ge(floored.sem, floored.at(i, g - 1))
                            nc.tensor.matmul(ps_o[g % 2][:], heads64, sq[g % 2][:], start=True, stop=True).then_inc(length_ready.sem, 1)

                        for g in range(2 * QC):
                            if g < 2:
                                pe.wait_ge(gelu_done.sem, gelu_done.at(i, 0))
                            else:
                                pe.wait_ge(sq_done.sem, sq_done.at(i, g - 1))
                            for c in range(C):
                                mm = nc.tensor.matmul(ps_t[g % 2][:], wqkv[:, c, g * P:(g + 1) * P], hT[:, c, :],
                                                      start=(c == 0), stop=(c == C - 1))
                            mm.then_inc(proj_ready.sem, 1)
                            if g:
                                rope(g - 1)
                        rope(2 * QC - 1)
                        pe.wait_ge(rope_done.sem, rope_done.at(i, 2 * QC))

                        def tick(s):
                            if s < STEPS:
                                b, h = s // H2, s % H2
                                c, r = h // 2, D2 * (h % 2)
                                pe.wait_ge(exp_done.sem, exp_done.at(i, 2 * (s - 2)))
                                bank = ps_s[s % 3]
                                nc.tensor.matmul(bank[:], ident16[:], mask16[:], start=True, stop=False, skip_group_check=True)
                                for w in range(2):
                                    n = (w + 1) * P
                                    mm = nc.tensor.matmul(bank[:, w * 2 * P:w * 2 * P + n],
                                                          qkT[r:r + D2, c, b * S + w * P:b * S + (w + 1) * P],
                                                          qkT[r:r + D2, QC + c, b * S:b * S + n],
                                                          start=False, stop=True, skip_group_check=True)
                                mm.then_inc(s_ready.sem, 1)
                            if LAG_T <= s < STEPS + LAG_T:
                                n = s - LAG_T
                                if n < 2:
                                    pe.wait_ge(sq_done.sem, sq_done.at(i, 2 * QC))
                                else:
                                    pe.wait_ge(*t_copied(n - 2, i))
                                pe.wait_ge(exp_done.sem, exp_done.at(i, 2 * n + 2))
                                for k in range(3):
                                    mm = nc.tensor.transpose(ps_t[n % 2][:, k * P:(k + 1) * P], prob[n % 3][:, k * P:(k + 1) * P], ident)
                                mm.then_inc(t_ready.sem, 1)
                            if LAG_V <= s < STEPS + LAG_V:
                                n = s - LAG_V
                                b, h = n // H2, n % H2
                                if n % 2 == 0:
                                    pe.wait_ge(o_done.sem, o_done.at(i, n // 2 - 1))
                                pe.wait_ge(*t_copied(n, i))
                                for w in range(2):
                                    for k in range(w + 1):
                                        mm = nc.tensor.matmul(ps_o[n // 2 % 2][:, (2 * (n % 2) + w) * OW:(2 * (n % 2) + w + 1) * OW],
                                                              probT[n % 2][:, (w + k) * P:(w + k + 1) * P],
                                                              V[:, 2 * b + k, h, :], start=(k == 0), stop=(k == w))
                                mm.then_inc(pv_ready.sem, 1)
                            if s in (H2 + LAG_V + 1, STEPS + LAG_V + 1):
                                b = s // H2 - 1
                                pe.wait_ge(o_done.sem, o_done.at(i, (b + 1) * H2 // 2))
                                for w in range(2):
                                    pe.wait_ge(o_copied.sem, o_copied.at(i, 2 * b + w))
                                    for c in range(QC):
                                        mm = nc.tensor.transpose(ps_g[:, c * P:(c + 1) * P], on[:, b, w, c * P:(c + 1) * P], ident)
                                    mm.then_inc(o_turned.sem, 1)

                        for s in range(STEPS + LAG_V + 2):
                            tick(s)
                        pe.wait_ge(o_copied.sem, o_copied.at(i, TT))
                        for m in range(C):
                            for c in range(QC):
                                mm = nc.tensor.matmul(ps_o[m][:], wo[:, c, m * P:(m + 1) * P], oT[:, c, :],
                                                      start=(c == 0), stop=(c == QC - 1))
                            mm.then_inc(out_ready.sem, 1)
                        pe.wait_ge(shifted.sem, shifted.at(i, 2))
                        for c in range(C):
                            mm = nc.tensor.matmul(ps_g[:], mean256, hT[:, c, :], start=(c == 0), stop=(c == C - 1))
                        mm.then_inc(norm_ready.sem, 1)
                        pe.wait_ge(squared.sem, squared.at(i, 1))
                        for c in range(C):
                            mm = nc.tensor.matmul(ps_g[:], mean256, squares[:, c, :], start=(c == 0), stop=(c == C - 1))
                        mm.then_inc(norm_ready.sem, 1)
                        pe.wait_ge(h2_done.sem, h2_done.at(i, C))
                        for j in range(HC):
                            m = hrows(j)
                            pe.wait_ge(gelu_done.sem, gelu_done.at(i, j - 1))
                            for c in range(C):
                                mm = nc.tensor.matmul(ps_t[j % 2][0:m, :], w1[:, c, HID + j * P:HID + j * P + m], h2[:, c, :],
                                                      start=(c == 0), stop=(c == C - 1))
                            mm.then_inc(g_ready.sem, 1)
                            pe.wait_ge(hid_done.sem, hid_done.at(i, j - 1))
                            for c in range(C):
                                mm = nc.tensor.matmul(ps_s[j % 2][0:m, :], w1[:, c, j * P:j * P + m], h2[:, c, :],
                                                      start=(c == 0), stop=(c == C - 1))
                            mm.then_inc(a_ready.sem, 1)
                        for m in range(C):
                            for j in range(HC):
                                n = hrows(j)
                                if m == 0:
                                    pe.wait_ge(hid_done.sem, hid_done.at(i, j + 1))
                                mm = nc.tensor.matmul(ps_o[m][:], w2[0:n, j, m * P:(m + 1) * P], hid[0:n, j, :],
                                                      start=(j == 0), stop=(j == HC - 1))
                            mm.then_inc(ff_ready.sem, 1)

            @block.scalar
            def _(act):
                start_ahead(act, [shifted, v_copied, raw_done, sq_done, exp_done, t_odd, o_copied, squared, h2_done,
                                  gelu_done, ln_done, rn_done, logged, rstd_done])
                act.wait_ge(zeroed, 1)
                with act.Fori(0, DEPTH) as l:
                    act.wait_ge(weights_in, l * (16 * LOADS) + 16 * LOADS)
                    with act.Fori(0, PAIRS) as pair:
                        i = l * PAIRS + pair

                        def shift():
                            act.sem_inc(waited, 1)
                            nc.scalar.copy(hT[:, 0, :], now_y(pair, 0))
                            late = two(hT[:, 1, :])[:, :, 1:S]
                            nc.scalar.copy(late, two(now_y(pair, 1))[:, :, 0:S - 1]).then_inc(shifted.sem, 1)

                        nc.scalar.preload_act_table_set(LOG_EXP)
                        act.wait_ge(grown.sem, grown.at(i, 0))
                        shift()
                        for t in range(TT):
                            act.wait_ge(v_ready.sem, v_ready.at(i, t + 1))
                            nc.scalar.copy(V[:, t, :, 0:D2], ps_s[t % 2][:].rearrange("p (h d) -> p h d", d=D2)).then_inc(v_copied.sem, 1)

                        def length(g):
                            act.wait_ge(floored.sem, floored.at(i, g + 1))
                            nc.scalar.activation(ln[g % 2][:], fl[g % 2][:], ACT.Ln).then_inc(ln_done.sem, 1)
                            act.wait_ge(ln_done.sem, ln_done.at(i, g + 1))
                            act.wait_ge(rope_done.sem, rope_done.at(i, g - 1))
                            nc.scalar.activation(rn[g % 2][:], ln[g % 2][:], ACT.Exp, scale=-0.5).then_inc(rn_done.sem, 1)

                        for g in range(2 * QC):
                            act.wait_ge(proj_ready.sem, proj_ready.at(i, g + 1))
                            act.wait_ge(turned.sem, turned.at(i, g - 1))
                            act.wait_ge(cos_done.sem, cos_done.at(i, g - 1))
                            nc.scalar.copy(raw[g % 2][:], ps_t[g % 2][:]).then_inc(raw_done.sem, 1)
                            act.wait_ge(length_ready.sem, length_ready.at(i, g - 1))
                            nc.scalar.activation(sq[g % 2][:], ps_t[g % 2][:], ACT.Square).then_inc(sq_done.sem, 1)
                            if g:
                                length(g - 1)
                        length(2 * QC - 1)

                        def tick(s):
                            if s < STEPS:
                                act.wait_ge(peaked.sem, peaked.at(i, s + 1))
                                act.wait_ge(t_ready.sem, t_ready.at(i, s - 2))
                                for w in range(2):
                                    n = (w + 1) * P
                                    nc.scalar.activation(prob[s % 3][:, w * P:w * P + n], ps_s[s % 3][:, w * 2 * P:w * 2 * P + n],
                                                         ACT.Exp, bias=peak[:, s % 3, w:w + 1]).then_inc(exp_done.sem, 1)
                            n = s - LAG_T
                            if 0 <= n < STEPS and n % 2:
                                act.wait_ge(t_ready.sem, t_ready.at(i, n + 1))
                                act.wait_ge(pv_ready.sem, pv_ready.at(i, n - 1))
                                nc.scalar.copy(probT[1][:], ps_t[1][:, 0:PW]).then_inc(t_odd.sem, 1)
                            if s in (H2 + LAG_V + 1, STEPS + LAG_V + 1):
                                b = s // H2 - 1
                                for w in range(2):
                                    act.wait_ge(o_turned.sem, o_turned.at(i, 2 * b + w + 1))
                                    nc.scalar.copy(oT[:, :, (2 * b + w) * P:(2 * b + w + 1) * P],
                                                   ps_g[:].rearrange("p (c t) -> p c t", c=QC)).then_inc(o_copied.sem, 1)

                        for s in range(STEPS + LAG_V + 2):
                            tick(s)
                        act.wait_ge(added.sem, added.at(i, C))
                        shift()
                        act.wait_ge(centred_done.sem, centred_done.at(i, 1))
                        nc.scalar.activation(squares[:], centred[:], ACT.Square).then_inc(squared.sem, 1)
                        act.wait_ge(norm_ready.sem, norm_ready.at(i, 2))
                        nc.scalar.activation(log[:], ps_g[:], ACT.Ln, bias=sh["eps"][:]).then_inc(logged.sem, 1)
                        act.wait_ge(logged.sem, logged.at(i, 1))
                        nc.scalar.activation(rstd[:], log[:], ACT.Exp, scale=-0.5).then_inc(rstd_done.sem, 1)
                        act.wait_ge(normed_done.sem, normed_done.at(i, 1))
                        for c in range(C):
                            nc.scalar.activation(h2[:, c, :], normed[:, c, :], ACT.Identity, scale=cols[:, 2 + c:3 + c],
                                                 bias=cols[:, 4 + c:5 + c]).then_inc(h2_done.sem, 1)
                        for j in range(HC):
                            m = hrows(j)
                            act.wait_ge(g_ready.sem, g_ready.at(i, j + 1))
                            act.wait_ge(hid_done.sem, hid_done.at(i, j - 1))
                            nc.scalar.activation(gelu[j % 2][0:m, :], ps_t[j % 2][0:m, :], ACT.Gelu,
                                                 bias=cols[0:m, 8 + HC + j:9 + HC + j]).then_inc(gelu_done.sem, 1)

            @block.gpsimd
            def _(pool):
                start_ahead(pool, [rope_sum, rope_done])
                with pool.Fori(0, DEPTH * PAIRS) as i:
                    for g in range(2 * QC):
                        pool.wait_ge(sin_done.sem, sin_done.at(i, g + 1))
                        nc.gpsimd.tensor_tensor(tc[g % 2][:], ta[g % 2][:], tb[g % 2][:], ALU.add).then_inc(rope_sum.sem, 1)
                        pool.wait_ge(rope_sum.sem, rope_sum.at(i, g + 1))
                        pool.wait_ge(rn_done.sem, rn_done.at(i, g + 1))
                        nc.gpsimd.tensor_tensor(qkT[:, g, :], tc[g % 2][:], rn[g % 2][:], ALU.mult).then_inc(rope_done.sem, 1)

            @block.vector
            def _(dve):
                start_ahead(dve, [floored, cos_done, sin_done, peaked, t_even, summed, o_done, added, centred_done,
                                  normed_done, hid_done, grown])
                nc.vector.memset(V[:], 1.0)
                nc.vector.memset(two(hT[:, 1, :])[:, :, 0:1], 0.0).then_inc(zeroed, 1)
                dve.wait_ge(tables_in, 32)
                nc.vector.tensor_copy(ident16[:], sh["mat"]("ident"))
                nc.vector.tensor_copy(mask16[:], mask[:]).then_inc(mask_done, 1)
                with dve.Fori(0, DEPTH) as l:
                    dve.wait_ge(weights_in, l * (16 * LOADS) + 16 * LOADS)
                    for n in range(2):
                        nc.vector.tensor_scalar(turn[n][:], sh["mat"]("rotate"), cols[:, n:n + 1], None, ALU.mult).then_inc(turn_scaled, 1)
                    with dve.Fori(0, PAIRS) as pair:
                        i = l * PAIRS + pair
                        for g in range(2 * QC):
                            n = g // QC
                            dve.wait_ge(rope_done.sem, rope_done.at(i, g - 1))
                            dve.wait_ge(raw_done.sem, raw_done.at(i, g + 1))
                            nc.vector.scalar_tensor_tensor(two(ta[g % 2][:]), two(raw[g % 2][:]), cols[:, n:n + 1],
                                                           spread(tables[:, 2 * n, :], 2, 1), ALU.mult, ALU.mult).then_inc(cos_done.sem, 1)
                            dve.wait_ge(length_ready.sem, length_ready.at(i, g + 1))
                            dve.wait_ge(ln_done.sem, ln_done.at(i, g - 1))
                            nc.vector.tensor_scalar(fl[g % 2][:], ps_o[g % 2][:], 1e-24, 2.0 ** 16, ALU.max, ALU.mult).then_inc(floored.sem, 1)
                            dve.wait_ge(turned.sem, turned.at(i, g + 1))
                            nc.vector.tensor_tensor(two(tb[g % 2][:]), two(ps_s[g % 2][:]), spread(tables[:, 2 * n + 1, :], 2, 1),
                                                    ALU.mult).then_inc(sin_done.sem, 1)

                        def tick(s):
                            if s < STEPS:
                                dve.wait_ge(s_ready.sem, s_ready.at(i, s + 1))
                                nc.vector.tensor_reduce(peak[:, s % 3, :], two(ps_s[s % 3][:]), AX.X, ALU.max,
                                                        negate=True).then_inc(peaked.sem, 1)
                            n = s - LAG_T
                            if 0 <= n < STEPS and n % 2 == 0:
                                dve.wait_ge(t_ready.sem, t_ready.at(i, n + 1))
                                dve.wait_ge(pv_ready.sem, pv_ready.at(i, n - 1))
                                nc.vector.tensor_copy(probT[0][:], ps_t[0][:, 0:PW]).then_inc(t_even.sem, 1)
                            n = s - LAG_V
                            if 0 <= n < STEPS and n % 2:
                                q, b, h = n // 2, n // H2, n % H2 - 1
                                dve.wait_ge(pv_ready.sem, pv_ready.at(i, n + 1))
                                o = ps_o[q % 2][:, 0:4 * OW].rearrange("p (n d) -> p n d", d=OW)
                                nc.vector.reciprocal(rsum[:, q % 2, :], o[:, :, D2]).then_inc(summed.sem, 1)
                                dve.wait_ge(summed.sem, summed.at(i, q + 1))
                                for k in range(2):
                                    op = nc.vector.tensor_tensor(
                                        on[:, b, :, (h + k) * D2:(h + k + 1) * D2], o[:, 2 * k:2 * k + 2, 0:D2],
                                        spread(rsum[:, q % 2, 2 * k:2 * k + 2], D2, 2), ALU.mult)
                                op.then_inc(o_done.sem, 1)

                        for s in range(STEPS + LAG_V + 2):
                            tick(s)
                        for m in range(C):
                            dve.wait_ge(out_ready.sem, out_ready.at(i, m + 1))
                            nc.vector.tensor_tensor(now_y(pair, m), ps_o[m][:], now_y(pair, m), ALU.add).then_inc(added.sem, 1)
                        dve.wait_ge(norm_ready.sem, norm_ready.at(i, 1))
                        nc.vector.tensor_tensor(centred[:], hT[:], spread(ps_g[:], C, 1), ALU.subtract).then_inc(centred_done.sem, 1)
                        dve.wait_ge(rstd_done.sem, rstd_done.at(i, 1))
                        nc.vector.tensor_tensor(normed[:], centred[:], spread(rstd[:], C, 1), ALU.mult).then_inc(normed_done.sem, 1)
                        for j in range(HC):
                            m = hrows(j)
                            dve.wait_ge(a_ready.sem, a_ready.at(i, j + 1))
                            dve.wait_ge(gelu_done.sem, gelu_done.at(i, j + 1))
                            nc.vector.scalar_tensor_tensor(hid[0:m, j, :], ps_s[j % 2][0:m, :], cols[0:m, 8 + j:9 + j],
                                                           gelu[j % 2][0:m, :], ALU.add, ALU.mult).then_inc(hid_done.sem, 1)
                        for m in range(C):
                            dve.wait_ge(ff_ready.sem, ff_ready.at(i, m + 1))
                            nc.vector.scalar_tensor_tensor(now_y(pair, m), ps_o[m][:], cols[:, 6 + m:7 + m], now_y(pair, m),
                                                           ALU.add, ALU.add).then_inc(grown.sem, 1)

    with ExitStack() as st:
        final = st.enter_context(nc.semaphore("e_final"))
        sent = st.enter_context(nc.semaphore("e_sent"))
        x_all, y_all = sh["x"], sh["y"]
        with nc.Block() as block:
            @block.vector
            def _(dve):
                for n in range(4):
                    part = (slice(None), slice(None), slice(n * W, (n + 1) * W))
                    nc.vector.scalar_tensor_tensor(x_all[part], y_all[part], sh["tanh"][:, 3:4], x_all[part],
                                                   ALU.mult, ALU.add).then_inc(final, 1)

            @block.sync
            def _(sp):
                for n in range(4):
                    sp.wait_ge(final, n + 1)
                    sp.dma_start(io["out"][:, :, n * W:(n + 1) * W], x_all[:, :, n * W:(n + 1) * W]).then_inc(sent, 16)
                sp.wait_ge(sent, 64)


def build(nc, io):
    with ExitStack() as st:
        def sb(name, shape, dt=F32):
            return st.enter_context(nc.sbuf_tensor(name, shape, dt))

        const = sb("const", [P, len(CONST), P])
        sh = {
            "const": const,
            "mat": lambda name: const[:, CONST[name], :],
            "small": sb("small_sb", [P, SMALL]),
            "tanh": sb("tanh_gates", [P, 4]),
            "slot": sb("slot_of_token", [P, NT], I32),
            "owner": sb("expert_of_tile", [P, SLOTS], I32),
            "sorted_x": nc.dram_tensor("sorted_x", [SLOTS * P, D], F32, kind="Internal").ap(),
            "sorted_y": nc.dram_tensor("sorted_y", [SLOTS * P, D], F32, kind="Internal").ap(),
            "x": sb("x_all", [P, C, T]),
            "eps": sb("eps_sb", [P, 1]),
        }
        with ExitStack() as early:
            sh["rows"] = early.enter_context(nc.sbuf_tensor("rows", [P, NT, D], F32))
            sh["logits"] = early.enter_context(nc.sbuf_tensor("logits", [P, NT, E], F32))
            attend_linear(nc, io, sh)
            route(nc, io, sh)
        experts(nc, io, sh)
        attend_heads(nc, io, sh)
        sh["y"] = sb("y_all", [P, C, T])
        start_layers(nc, io, sh)
        local_layers(nc, io, sh)


def constants():
    import numpy as np

    p = np.arange(P)
    same16 = p[:, None] // D1 == p[None, :] // D1
    same64 = p[:, None] // D2 == p[None, :] // D2
    half = D2 // 2
    rotate = np.zeros((P, P), np.float32)
    for m in range(P):
        if m % D2 < half:
            rotate[m + half, m] = -1.0
        else:
            rotate[m - half, m] = 1.0
    mats = {
        "ident": np.eye(P), "mean256": np.full((P, P), 1.0 / D), "mean16": same16 / D1,
        "heads16": same16 / float(D1) ** 0.5, "before": p[:, None] < p[None, :], "ones": np.ones((P, P)),
        "rotate": rotate, "heads64": same64,
    }
    consts = np.stack([np.asarray(mats[n], np.float32) for n in CONST], axis=1)
    small = np.zeros((P, SMALL), np.float32)
    small[:, 0:E] = np.arange(E, 0, -1)
    small[:, E:E + NT] = P * np.arange(NT)
    small[:, E + NT:E + NT + SLOTS] = np.arange(SLOTS)
    small[:, SMALL - 2] = (p // D1) % 2 == 0
    small[:, SMALL - 1] = (p // D1) % 2 == 1

    f = np.float32
    half_idx = np.arange(0, D2, 2, dtype=f)
    inv_freq = f(1.0) / f(10000.0) ** (half_idx / f(D2))
    t = np.arange(S, dtype=f)
    freqs = t[:, None] * inv_freq[None, :]
    base = (half_idx + f(0.4 * D2)) / f(1.4 * D2)
    power = (t - f(S // 2)) / f(64.0)
    decay = base[None, :] ** power[:, None]
    wide = [np.tile(np.concatenate([a, a], axis=1).T, (P // D2, 1)) for a in (np.cos(freqs), np.sin(freqs), decay)]
    cos, sin, decay = wide
    rope = np.stack([cos * decay * f(8 * 256), sin * decay * f(8 * 256), cos / decay * f(256), sin / decay * f(256)],
                    axis=1).astype(f)

    q, k = np.arange(P)[:, None], np.arange(S)[None, :]
    first = np.where(k <= q, 0.0, -1e30)
    second = np.where((k <= q + P) & (k >= q), 0.0, -1e30)
    mask = np.concatenate([first, second], axis=1).astype(f)
    return {"consts": consts, "small": small, "rope": rope, "mask": mask}


def kernel(**inputs):
    import numpy as np
    import concourse.bacc as bacc
    from concourse.bass_utils import run_bass_kernel_spmd

    a = {k: np.asarray(v) for k, v in inputs.items()}

    def turned(x):
        return np.ascontiguousarray(x.reshape(T, C, P).transpose(2, 1, 0))

    def chunks(v):
        n = -(-v.shape[0] // P)
        out = np.zeros((n * P,), v.dtype)
        out[:v.shape[0]] = v
        return out.reshape(n, P).T

    def per_head(v):
        return np.tile(v, P // v.shape[0])[:, None]

    def layer_cols(l):
        b1 = a["L1_ffn_b1"][l]
        return np.concatenate([per_head(a["L1_ffn_q_scale"][l]), per_head(a["L1_ffn_k_scale"][l]),
                               chunks(a["L1_ffn_ln_g"][l]), chunks(a["L1_ffn_ln_b"][l]), chunks(a["L1_ffn_b2"][l]),
                               chunks(b1[:HID]), chunks(b1[HID:])], axis=1)

    arrays = {
        "xT": turned(a["x"]), "ctxT": turned(a["ctx_1024"]),
        "L0_Wkv": np.concatenate([a["L0_xattn_Wk"].T, a["L0_xattn_Wv"].T], axis=1),
        "L0_Wq": a["L0_xattn_Wq"].T, "L0_Wo": a["L0_xattn_Wo"].T,
        "Wg": a["L0_ffn_Wg"], "bg": a["L0_ffn_bg"],
        "gates": np.tile(np.concatenate([a["g_xattn"][0:1], a["g_ffn"][0:1], a["g_xattn"][1:2], a["g_ffn"][1:2]])[None], (P, 1)),
        "W1": a["L0_ffn_W1"], "b1": a["L0_ffn_b1"].reshape(E, FC, P).transpose(0, 2, 1), "W2": a["L0_ffn_W2"],
        "b2": a["L0_ffn_b2"],
        "L1_Wq": a["L1_xattn_Wq"], "L1_Wkv": a["L1_xattn_Wkv"], "L1_Wp": a["L1_xattn_Wp"],
        "L1_cols": np.concatenate([chunks(a["L1_xattn_bp"]), per_head(a["L1_xattn_ln_g"]), per_head(a["L1_xattn_ln_b"])], axis=1),
        "F_wqkv": a["L1_ffn_wqkv"], "F_wo": a["L1_ffn_wo"], "F_w1": a["L1_ffn_w1"], "F_w2": a["L1_ffn_w2"],
        "F_cols": np.stack([layer_cols(l) for l in range(DEPTH)]),
        **constants(),
    }
    arrays = {k: np.ascontiguousarray(v) for k, v in arrays.items()}
    nc = bacc.Bacc("TRN2", target_bir_lowering=False, num_devices=1)
    io = {k: nc.dram_tensor(k, v.shape, mybir.dt.from_np(v.dtype), kind="ExternalInput").ap() for k, v in arrays.items()}
    io["out"] = nc.dram_tensor("out", (P, C, T), F32, kind="ExternalOutput").ap()
    build(nc, io)
    r = run_bass_kernel_spmd(nc, [arrays], core_ids=[0])
    got = r.results[0]["out"]
    return np.ascontiguousarray(got.transpose(2, 1, 0)).reshape(B, S, D)
```

```python
from contextlib import ExitStack

import concourse.bass as bass
from concourse import mybir

ALU = mybir.AluOpType
LOG_EXP = "natural_log_exp_and_others"
ACT = mybir.ActivationFunctionType
AX = mybir.AxisListType
F32 = mybir.dt.float32
BF16 = mybir.dt.bfloat16
I32 = mybir.dt.int32

P = 128
B, S, D = 8, 256, 256
T = B * S
C = D // P
W = 2 * S
PAIRS = T // W
TT = W // P
NT = T // P
E, FF = 8, 1024
FC = FF // P
SLOTS = 24
UNROLL = 3
H1, D1 = 16, 16
H2, D2 = 8, 64
INNER = H2 * D2
DEPTH = 2
HID = int(D * 4 * 2 / 3)
HC = -(-HID // P)
HL = HID - (HC - 1) * P
EPS = 1e-5

CONST = {n: i for i, n in enumerate(
    ["ident", "mean256", "mean16", "heads16", "before", "ones", "rotate", "heads64"])}
SMALL = 8 + 16 + SLOTS


class Signal:

    def __init__(self, stack, nc, name, per):
        self.sem = stack.enter_context(nc.semaphore(name))
        self.per = per

    def at(self, step, k):
        return step * self.per + (self.per + k)

    def before(self, step, k):
        return step * self.per + k


def start_ahead(engine, signals):
    for s in signals:
        engine.sem_inc(s.sem, s.per)


def spread(ap, n, at):
    shape = list(ap.shape)
    shape.insert(at, n)
    return ap.unsqueeze(at).to_broadcast(shape)


def attend_linear(nc, io, sh):
    with ExitStack() as st:
        def sb(name, shape, dt=F32):
            return st.enter_context(nc.sbuf_tensor("a_" + name, shape, dt))

        def pb(name):
            return st.enter_context(nc.psum_tensor("a_" + name, [P, 512], F32))

        def sig(name, per):
            return Signal(st, nc, "a_" + name, per)

        wkv, wq, wo = sb("wkv", [P, C, 2 * D]), sb("wq", [P, C, D]), sb("wo", [P, C, D])
        wg = sb("wg", [P, C, E])
        bg = sb("bg", [P, E])
        gin = sb("gin", [P, 4])
        ctx = sb("ctx", [P, C, W])
        centred = sb("centred", [P, C, W])
        squares = sb("squares", [P, C, W])
        log, rstd = sb("log", [P, W]), sb("rstd", [P, W])
        normed = sb("normed", [P, C, W])
        kv = sb("kv", [P, TT, 2 * D])
        ktv = sb("ktv", [P, 2 * C, P])
        qT = sb("qT", [P, C, W])
        aT = sb("aT", [P, C, W])
        zeros = sb("zeros", [P, D])

        ps_kv = [pb(f"ps_kv{i}") for i in range(2)]
        ps_ktv, ps_norm = pb("ps_ktv"), pb("ps_norm")
        ps_q = [pb(f"ps_q{i}") for i in range(2)]
        ps_o, ps_logit = pb("ps_o"), pb("ps_logit")

        loaded = st.enter_context(nc.semaphore("a_loaded"))
        zeroed = st.enter_context(nc.semaphore("a_zeroed"))
        waited = st.enter_context(nc.semaphore("a_waited"))
        eps_set = st.enter_context(nc.semaphore("a_eps_set"))
        slots_zeroed = st.enter_context(nc.semaphore("a_slots_zeroed"))
        gates = st.enter_context(nc.semaphore("a_gates"))
        ctx_in = st.enter_context(nc.semaphore("a_ctx_in"))
        norm_ready = sig("norm_ready", 4)
        kv_ready = sig("kv_ready", TT)
        kv_copied = sig("kv_copied", TT)
        ktv_ready = sig("ktv_ready", 1)
        ktv_masked = sig("ktv_masked", 1)
        centred_done = sig("centred_done", 2)
        squared = sig("squared", 2)
        logged = sig("logged", 2)
        rstd_done = sig("rstd_done", 2)
        normed_done = sig("normed_done", 2)
        q_ready = sig("q_ready", 6)
        q_copied = sig("q_copied", 6)
        o_ready = sig("o_ready", C)
        added = sig("added", C)
        logit_ready = sig("logit_ready", 1)
        logit_done = sig("logit_done", 1)

        weights = [(wkv, io["L0_Wkv"]), (wq, io["L0_Wq"]), (wo, io["L0_Wo"]), (wg, io["Wg"])]
        nloads = 16 * (len(weights) + 5)

        x_all = sh["x"]

        def now_x(i, c):
            return x_all[:, c, bass.ds(i * W, W)]

        with nc.Block() as block:
            @block.sync
            def _(sp):
                sp.dma_start(sh["const"][:], io["consts"]).then_inc(loaded, 16)
                sp.dma_start(x_all[:], io["xT"]).then_inc(loaded, 16)
                for to, of in weights:
                    sp.dma_start(to[:], of.rearrange("(c p) n -> p c n", p=P)).then_inc(loaded, 16)
                sp.dma_start(bg[:], spread(io["bg"], P, 0)).then_inc(loaded, 16)
                sp.dma_start(gin[:], io["gates"]).then_inc(loaded, 16)
                sp.dma_start(sh["small"][:], io["small"]).then_inc(loaded, 16)
                with sp.Fori(0, PAIRS) as i:
                    sp.wait_ge(kv_ready.sem, kv_ready.before(i, TT))
                    sp.dma_start(ctx[:], io["ctxT"][:, :, bass.ds(i * W, W)]).then_inc(ctx_in, 16)
                sp.wait_ge(zeroed, 1)
                sp.dma_start(sh["sorted_x"].rearrange("(n p) d -> p n d", p=P),
                             spread(zeros[:], SLOTS, 1)).then_inc(slots_zeroed, 16)
                sp.wait_ge(slots_zeroed, 16)

            @block.gpsimd
            def _(pool):
                nc.gpsimd.memset(sh["eps"][:], EPS).then_inc(eps_set, 1)
                nc.gpsimd.memset(zeros[:], 0.0).then_inc(zeroed, 1)

            @block.tensor
            def _(pe):
                start_ahead(pe, [norm_ready, kv_ready, ktv_ready, q_ready, o_ready, logit_ready])
                pe.wait_ge(loaded, nloads)
                mean256 = sh["mat"]("mean256")
                with pe.Fori(0, PAIRS) as i:
                    def average(of, n):
                        if n % 2 == 0:
                            pe.wait_ge(rstd_done.sem, rstd_done.before(i, 2) if n == 0 else rstd_done.at(i, 1))
                        else:
                            pe.wait_ge(squared.sem, squared.at(i, n // 2 + 1))
                        for c in range(C):
                            mm = nc.tensor.matmul(ps_norm[:], mean256, of(c), start=(c == 0), stop=(c == C - 1))
                        mm.then_inc(norm_ready.sem, 1)

                    pe.wait_ge(added.sem, added.before(i, C))
                    average(lambda c: now_x(i, c), 0)
                    pe.wait_ge(ctx_in, i * 16 + 16)
                    for t in range(TT):
                        pe.wait_ge(kv_copied.sem, kv_copied.at(i, t - 1) if t >= 2 else kv_copied.before(i, TT - 1 + t))
                        for c in range(C):
                            mm = nc.tensor.matmul(ps_kv[t % 2][:], ctx[:, c, t * P:(t + 1) * P], wkv[:, c, :],
                                                  start=(c == 0), stop=(c == C - 1))
                        mm.then_inc(kv_ready.sem, 1)
                    average(lambda c: squares[:, c, :], 1)
                    pe.wait_ge(kv_copied.sem, kv_copied.at(i, TT))
                    pe.wait_ge(ktv_masked.sem, ktv_masked.before(i, 1))
                    for b in range(2):
                        for c in range(C):
                            for t in range(2):
                                mm = nc.tensor.matmul(ps_ktv[:, (b * C + c) * P:(b * C + c + 1) * P],
                                                      kv[:, 2 * b + t, c * P:(c + 1) * P],
                                                      kv[:, 2 * b + t, D + c * P:D + (c + 1) * P],
                                                      start=(t == 0), stop=(t == 1))
                    mm.then_inc(ktv_ready.sem, 1)
                    pe.wait_ge(normed_done.sem, normed_done.at(i, 1))
                    for m in range(C):
                        pe.wait_ge(q_copied.sem, q_copied.before(i, 5 + m))
                        for c in range(C):
                            mm = nc.tensor.matmul(ps_q[m][:], wq[:, c, m * P:(m + 1) * P], normed[:, c, :],
                                                  start=(c == 0), stop=(c == C - 1))
                        mm.then_inc(q_ready.sem, 1)
                    pe.wait_ge(ktv_masked.sem, ktv_masked.at(i, 1))
                    for c in range(C):
                        pe.wait_ge(q_copied.sem, q_copied.at(i, 1 + c))
                        for b in range(2):
                            mm = nc.tensor.matmul(ps_q[c][:, b * S:(b + 1) * S], ktv[:, b * C + c, :],
                                                  qT[:, c, b * S:(b + 1) * S], start=True, stop=True)
                        mm.then_inc(q_ready.sem, 1)
                    pe.wait_ge(q_copied.sem, q_copied.at(i, 4))
                    for m in range(C):
                        pe.wait_ge(added.sem, added.before(i, C) if m == 0 else added.at(i, m))
                        for c in range(C):
                            mm = nc.tensor.matmul(ps_o[:], wo[:, c, m * P:(m + 1) * P], aT[:, c, :],
                                                  start=(c == 0), stop=(c == C - 1))
                        mm.then_inc(o_ready.sem, 1)
                    pe.wait_ge(added.sem, added.at(i, C))
                    average(lambda c: now_x(i, c), 2)
                    average(lambda c: squares[:, c, :], 3)
                    pe.wait_ge(normed_done.sem, normed_done.at(i, 2))
                    pe.wait_ge(logit_done.sem, logit_done.before(i, 1))
                    for t in range(TT):
                        for c in range(C):
                            mm = nc.tensor.matmul(ps_logit[:, t * E:(t + 1) * E], normed[:, c, t * P:(t + 1) * P],
                                                  wg[:, c, :], start=(c == 0), stop=(c == C - 1))
                    mm.then_inc(logit_ready.sem, 1)
                    for h in range(2):
                        for t in range(2):
                            for c in range(C):
                                mm = nc.tensor.transpose(ps_q[h][:, (t * C + c) * P:(t * C + c + 1) * P],
                                                         normed[:, c, (2 * h + t) * P:(2 * h + t + 1) * P],
                                                         sh["mat"]("ident"))
                        mm.then_inc(q_ready.sem, 1)

            @block.scalar
            def _(act):
                start_ahead(act, [kv_copied, squared, q_copied, logged, rstd_done])
                act.wait_ge(loaded, nloads)
                act.wait_ge(eps_set, 1)
                nc.scalar.activation(sh["tanh"][:], gin[:], ACT.Tanh).then_inc(gates, 1)
                nc.scalar.preload_act_table_set(LOG_EXP)
                with act.Fori(0, PAIRS) as i:
                    def square(n):
                        act.wait_ge(centred_done.sem, centred_done.at(i, n))
                        nc.scalar.activation(squares[:], centred[:], ACT.Square).then_inc(squared.sem, 1)

                    def deviate(n):
                        act.wait_ge(norm_ready.sem, norm_ready.at(i, 2 * n + 2))
                        nc.scalar.activation(log[:], ps_norm[:], ACT.Ln, bias=sh["eps"][:]).then_inc(logged.sem, 1)
                        act.wait_ge(logged.sem, logged.at(i, n + 1))
                        nc.scalar.activation(rstd[:], log[:], ACT.Exp, scale=-0.5).then_inc(rstd_done.sem, 1)

                    for t in range(TT):
                        act.wait_ge(kv_ready.sem, kv_ready.at(i, t + 1))
                        act.wait_ge(ktv_ready.sem, ktv_ready.before(i, 1))
                        nc.scalar.copy(kv[:, t, :], ps_kv[t % 2][:]).then_inc(kv_copied.sem, 1)
                        if t == 0:
                            square(1)
                    deviate(0)
                    for c in range(C):
                        act.wait_ge(q_ready.sem, q_ready.at(i, 1 + c))
                        nc.scalar.copy(qT[:, c, :], ps_q[c][:]).then_inc(q_copied.sem, 1)
                    for c in range(C):
                        act.wait_ge(q_ready.sem, q_ready.at(i, 3 + c))
                        nc.scalar.copy(aT[:, c, :], ps_q[c][:]).then_inc(q_copied.sem, 1)
                    square(2)
                    deviate(1)
                    for h in range(2):
                        act.wait_ge(q_ready.sem, q_ready.at(i, 5 + h))
                        act.sem_inc(waited, 1)
                        nc.scalar.copy(sh["rows"][:, bass.ds(i * TT + 2 * h, 2), :],
                                       ps_q[h][:].rearrange("p (t n) -> p t n", t=2)).then_inc(q_copied.sem, 1)

            @block.vector
            def _(dve):
                start_ahead(dve, [ktv_masked, centred_done, normed_done, added, logit_done])
                dve.wait_ge(loaded, nloads)
                dve.wait_ge(gates, 1)
                with dve.Fori(0, PAIRS) as i:
                    def centre(n):
                        dve.wait_ge(norm_ready.sem, norm_ready.at(i, 2 * n + 1))
                        if n:
                            dve.wait_ge(added.sem, added.at(i, C))
                        nc.vector.tensor_tensor(centred[:], x_all[:, :, bass.ds(i * W, W)],
                                                spread(ps_norm[:], C, 1), ALU.subtract).then_inc(centred_done.sem, 1)

                    def normalise(n):
                        dve.wait_ge(rstd_done.sem, rstd_done.at(i, n + 1))
                        dve.wait_ge(q_ready.sem, q_ready.before(i, 6) if n == 0 else q_ready.at(i, 2))
                        nc.vector.tensor_tensor(normed[:], centred[:], spread(rstd[:], C, 1),
                                                ALU.mult).then_inc(normed_done.sem, 1)

                    centre(0)
                    normalise(0)
                    dve.wait_ge(ktv_ready.sem, ktv_ready.at(i, 1))
                    nc.vector.tensor_tensor(ktv[:], ps_ktv[:].rearrange("p (n m) -> p n m", m=P),
                                            spread(sh["mat"]("heads16"), 2 * C, 1), ALU.mult).then_inc(ktv_masked.sem, 1)
                    for m in range(C):
                        dve.wait_ge(o_ready.sem, o_ready.at(i, m + 1))
                        nc.vector.scalar_tensor_tensor(now_x(i, m), ps_o[:], sh["tanh"][:, 0:1], now_x(i, m),
                                                       ALU.mult, ALU.add).then_inc(added.sem, 1)
                    centre(1)
                    normalise(1)
                    dve.wait_ge(logit_ready.sem, logit_ready.at(i, 1))
                    nc.vector.tensor_tensor(sh["logits"][:, bass.ds(i * TT, TT), :],
                                            ps_logit[:, 0:TT * E].rearrange("p (t e) -> p t e", e=E),
                                            spread(bg[:], TT, 1), ALU.add).then_inc(logit_done.sem, 1)


def route(nc, io, sh):
    with ExitStack() as st:
        def sb(name, shape, dt=F32):
            return st.enter_context(nc.sbuf_tensor("r_" + name, shape, dt))

        best = sb("best", [P, NT])
        tied = sb("tied", [P, NT, E])
        rank = sb("rank", [P, NT])
        chosen = sb("chosen", [P, NT, E])
        total = sb("total", [P, NT, E])
        ahead = sb("ahead", [P, NT + 1, E])
        full = sb("full", [P, E, NT])
        tiles = sb("tiles", [P, E])
        first = sb("first", [P, E + 1])
        base = sb("base", [P, E])
        place = sb("place", [P, NT, E])
        slot = sb("slot", [P, NT])
        begun = sb("begun", [P, SLOTS, E - 1])
        owner = sb("owner", [P, SLOTS])
        ps_before = st.enter_context(nc.psum_tensor("r_ps_before", [P, 512], F32))
        ps_total = st.enter_context(nc.psum_tensor("r_ps_total", [P, 512], F32))
        chain = st.enter_context(nc.semaphore("r_chain"))
        counted = st.enter_context(nc.semaphore("r_counted"))
        picked = st.enter_context(nc.semaphore("r_picked"))
        slots_done = st.enter_context(nc.semaphore("r_slots_done"))
        scattered = st.enter_context(nc.semaphore("r_scattered"))
        small = sh["small"]
        order, steps, numbers = small[:, 0:E], small[:, E:E + NT], small[:, E + NT:E + NT + SLOTS]

        with nc.Block() as block:
            @block.vector
            def _(dve):
                made = [0]

                def then(op):
                    made[0] += 1
                    op.then_inc(chain, 1)
                    dve.wait_ge(chain, made[0])

                logits = sh["logits"]
                then(nc.vector.tensor_reduce(best[:], logits[:], AX.X, ALU.max))
                then(nc.vector.tensor_tensor(tied[:], logits[:], spread(best[:], E, 2), ALU.is_ge))
                then(nc.vector.tensor_tensor(tied[:], tied[:], spread(order, NT, 1), ALU.mult))
                then(nc.vector.tensor_reduce(rank[:], tied[:], AX.X, ALU.max))
                nc.vector.tensor_tensor(chosen[:], tied[:], spread(rank[:], E, 2), ALU.is_equal).then_inc(picked, 1)
                nc.vector.memset(ahead[:, 0, :], 0.0)
                nc.vector.memset(first[:, 0:1], 0.0)
                dve.wait_ge(counted, 1)
                then(nc.vector.tensor_copy(total[:], ps_total[:, 0:NT * E].rearrange("p (t e) -> p t e", e=E)))
                for t in range(NT):
                    then(nc.vector.tensor_tensor(ahead[:, t + 1, :], ahead[:, t, :], total[:, t, :], ALU.add))
                then(nc.vector.tensor_tensor(full[:], spread(ahead[:, NT, :], NT, 2), spread(steps, E, 1), ALU.is_gt))
                then(nc.vector.tensor_reduce(tiles[:], full[:], AX.X, ALU.add))
                for e in range(E):
                    then(nc.vector.tensor_tensor(first[:, e + 1:e + 2], first[:, e:e + 1], tiles[:, e:e + 1], ALU.add))
                then(nc.vector.tensor_scalar(base[:], first[:, 0:E], float(P), None, ALU.mult))
                then(nc.vector.tensor_tensor(place[:], ps_before[:, 0:NT * E].rearrange("p (t e) -> p t e", e=E),
                                             ahead[:, 0:NT, :], ALU.add))
                then(nc.vector.tensor_tensor(place[:], place[:], spread(base[:], NT, 1), ALU.add))
                then(nc.vector.tensor_tensor(place[:], place[:], chosen[:], ALU.mult))
                then(nc.vector.tensor_reduce(slot[:], place[:], AX.X, ALU.add))
                nc.vector.tensor_copy(sh["slot"][:], slot[:]).then_inc(slots_done, 1)
                then(nc.vector.tensor_tensor(begun[:], spread(numbers, E - 1, 2), spread(first[:, 1:E], SLOTS, 1),
                                             ALU.is_ge))
                then(nc.vector.tensor_reduce(owner[:], begun[:], AX.X, ALU.add))
                then(nc.vector.tensor_copy(sh["owner"][:], owner[:]))

            @block.tensor
            def _(pe):
                pe.wait_ge(picked, 1)
                rhs = chosen[:].rearrange("p t e -> p (t e)")
                nc.tensor.matmul(ps_before[:, 0:NT * E], sh["mat"]("before"), rhs, start=True, stop=True)
                nc.tensor.matmul(ps_total[:, 0:NT * E], sh["mat"]("ones"), rhs, start=True, stop=True).then_inc(counted, 1)

            @block.gpsimd
            def _(pool):
                pool.wait_ge(slots_done, 1)
                for t in range(NT):
                    nc.gpsimd.indirect_dma_start(
                        sh["sorted_x"], bass.IndirectOffsetOnAxis(ap=sh["slot"][:, t:t + 1], axis=0),
                        sh["rows"][:, t, :], None).then_inc(scattered, 16)
                pool.wait_ge(scattered, 16 * NT)


def experts(nc, io, sh):
    with ExitStack() as st:
        def sb(name, shape, dt=F32):
            return st.enter_context(nc.sbuf_tensor("m_" + name, shape, dt))

        def pb(name):
            return st.enter_context(nc.psum_tensor("m_" + name, [P, 512], F32))

        def sem(name):
            return st.enter_context(nc.semaphore("m_" + name))

        U = UNROLL
        w1 = [sb(f"w1_{u}", [P, C, FF]) for u in range(U)]
        w2 = [sb(f"w2_{u}", [P, FC, D]) for u in range(U)]
        b1 = [sb(f"b1_{u}", [P, FC]) for u in range(U)]
        b2 = [sb(f"b2_{u}", [P, D]) for u in range(U)]
        xr = [sb(f"xr_{u}", [P, D]) for u in range(U)]
        xt = [sb(f"xt_{u}", [P, C, P]) for u in range(U)]
        hid = [sb(f"hid_{u}", [P, FC, P]) for u in range(U)]
        y = [sb(f"y_{u}", [P, D]) for u in range(U)]
        NH = 4
        ps_t = pb("ps_t")
        ps_h = [pb(f"ps_h{i}") for i in range(NH)]
        ps_y = [pb(f"ps_y{i}") for i in range(U)]

        rows_in, weights_in = [sem(f"rows_in{u}") for u in range(U)], [sem(f"weights_in{u}") for u in range(U)]
        stored = [sem(f"stored{u}") for u in range(U)]
        turned = Signal(st, nc, "m_turned", U)
        turned_copied = Signal(st, nc, "m_turned_copied", U)
        hid_ready = Signal(st, nc, "m_hid_ready", U * FC)
        gelu_done = Signal(st, nc, "m_gelu_done", U * FC)
        y_ready = Signal(st, nc, "m_y_ready", U)
        y_done = Signal(st, nc, "m_y_done", U)

        with nc.Block() as block:
            @block.sync
            def _(sp):
                with sp.Fori(0, SLOTS // U) as i:
                    for u in range(U):
                        sp.wait_ge(turned.sem, turned.before(i, u + 1))
                        sp.dma_start(xr[u][:], sh["sorted_x"][bass.ds((i * U + u) * P, P), :]).then_inc(rows_in[u], 16)
                        e = sp.value_load(sh["owner"][0:1, bass.ds(i * U + u, 1)], min_val=0, max_val=E - 1)
                        sp.wait_ge(y_ready.sem, y_ready.before(i, u + 1))
                        sp.dma_start(w1[u][:], io["W1"][bass.ds(e, 1), :, :].rearrange("e (c p) n -> p (e c) n", p=P)).then_inc(weights_in[u], 16)
                        sp.dma_start(b1[u][:], io["b1"][bass.ds(e, 1), :, :].rearrange("e p c -> p (e c)")).then_inc(weights_in[u], 16)
                        sp.dma_start(w2[u][:], io["W2"][bass.ds(e, 1), :, :].rearrange("e (c p) n -> p (e c) n", p=P)).then_inc(weights_in[u], 16)
                        sp.wait_ge(y_done.sem, y_done.before(i, u + 1))
                        sp.dma_start(b2[u][:], io["b2"][bass.ds(e, 1), :].to_broadcast([P, D])).then_inc(weights_in[u], 16)

            @block.gpsimd
            def _(pool):
                with pool.Fori(0, SLOTS // U) as i:
                    for u in range(U):
                        pool.wait_ge(y_done.sem, y_done.at(i, u + 1))
                        pool.dma_start(sh["sorted_y"][bass.ds((i * U + u) * P, P), :], y[u][:]).then_inc(stored[u], 16)
                for u in range(U):
                    pool.wait_ge(stored[u], 16 * (SLOTS // U))

            @block.tensor
            def _(pe):
                start_ahead(pe, [turned, hid_ready, y_ready])
                with pe.Fori(0, SLOTS // U) as i:
                    for u in range(U):
                        pe.wait_ge(rows_in[u], i * 16 + 16)
                        pe.wait_ge(turned_copied.sem, turned_copied.at(i, u))
                        for c in range(C):
                            mm = nc.tensor.transpose(ps_t[:, c * P:(c + 1) * P], xr[u][:, c * P:(c + 1) * P], sh["mat"]("ident"))
                        mm.then_inc(turned.sem, 1)
                        pe.wait_ge(turned_copied.sem, turned_copied.at(i, u + 1))
                        pe.wait_ge(weights_in[u], i * 64 + 64)
                        for m in range(FC):
                            k = u * FC + m
                            pe.wait_ge(gelu_done.sem, gelu_done.at(i, k + 1 - NH))
                            for c in range(C):
                                mm = nc.tensor.matmul(ps_h[m % NH][:, 0:P], w1[u][:, c, m * P:(m + 1) * P], xt[u][:, c, :],
                                                      start=(c == 0), stop=(c == C - 1))
                            mm.then_inc(hid_ready.sem, 1)
                        pe.wait_ge(y_done.sem, y_done.at(i, u + 1 - U))
                        for m in range(FC):
                            pe.wait_ge(gelu_done.sem, gelu_done.at(i, u * FC + m + 1))
                            mm = nc.tensor.matmul(ps_y[u][:, 0:D], hid[u][:, m, :], w2[u][:, m, :],
                                                  start=(m == 0), stop=(m == FC - 1))
                        mm.then_inc(y_ready.sem, 1)

            @block.scalar
            def _(act):
                start_ahead(act, [gelu_done])
                with act.Fori(0, SLOTS // U) as i:
                    for u in range(U):
                        act.wait_ge(weights_in[u], i * 64 + 64)
                        for m in range(FC):
                            act.wait_ge(hid_ready.sem, hid_ready.at(i, u * FC + m + 1))
                            if m == 0:
                                act.wait_ge(y_ready.sem, y_ready.at(i, u + 1 - U))
                            nc.scalar.activation(hid[u][:, m, :], ps_h[m % NH][:, 0:P], ACT.Gelu,
                                                 bias=b1[u][:, m:m + 1]).then_inc(gelu_done.sem, 1)

            @block.vector
            def _(dve):
                start_ahead(dve, [turned_copied, y_done])
                with dve.Fori(0, SLOTS // U) as i:
                    for u in range(U):
                        dve.wait_ge(turned.sem, turned.at(i, u + 1))
                        dve.wait_ge(hid_ready.sem, hid_ready.before(i, (u + 1) * FC))
                        nc.vector.tensor_copy(xt[u][:], ps_t[:, 0:D].rearrange("p (c t) -> p c t", c=C)).then_inc(turned_copied.sem, 1)
                        dve.wait_ge(y_ready.sem, y_ready.at(i, u + 1))
                        dve.wait_ge(weights_in[u], i * 64 + 64)
                        dve.wait_ge(stored[u], i * 16)
                        nc.vector.tensor_tensor(y[u][:], ps_y[u][:, 0:D], b2[u][:], ALU.add).then_inc(y_done.sem, 1)


def attend_heads(nc, io, sh):
    with ExitStack() as st:
        def sb(name, shape, dt=F32):
            return st.enter_context(nc.sbuf_tensor("h_" + name, shape, dt))

        def pb(name):
            return st.enter_context(nc.psum_tensor("h_" + name, [P, 512], F32))

        def sig(name, per):
            return Signal(st, nc, "h_" + name, per)

        G = 2 * D1
        HC1 = P // D1
        UNITS = 2 * C
        STEPS = UNITS * HC1
        BATCH = HC1 // 2
        RING = 2 * BATCH
        LAG_T, LAG_V = 2, 3

        wq, wkv, wp = sb("wq", [P, C, D]), sb("wkv", [P, C, 2 * D]), sb("wp", [P, C, D])
        cols = sb("cols", [P, 4])
        q_scale, k_scale = sb("q_scale", [P, 2]), sb("k_scale", [P, HC1, 2])
        bias = sb("bias", [P, C])
        ones = sb("ones", [P, 2, G])
        sums = sb("sums", [P, C, H1])
        ctx = sb("ctx", [P, C, W])
        taken = sb("taken", [P, TT, D])
        index = sb("index", [P, TT], I32)
        centred, squares = sb("centred", [P, C, W]), sb("squares", [P, C, W])
        log, rstd, normed = sb("log", [P, W]), sb("rstd", [P, W]), sb("normed", [P, C, W])
        hlog = [sb(f"hlog{i}", [P, W]) for i in range(2)]
        sq = [sb(f"sq{i}", [P, W]) for i in range(2)]
        hrstd = [sb(f"hrstd{i}", [P, W]) for i in range(2)]
        hn = [sb(f"hn{i}", [P, W]) for i in range(4)]
        qT = sb("qT", [P, C, W])
        kT = sb("kT", [P, C, HC1, W])
        V = sb("V", [P, TT, H1 // 2, 2, G])
        peak = sb("peak", [P, 3, 2])
        prob = [sb(f"prob{i}", [P, 2, S]) for i in range(3)]
        probT = [sb(f"probT{i}", [P, 2, S]) for i in range(RING)]
        rsum = sb("rsum", [P, 2, S])
        oT = sb("oT", [P, C, W])

        ps_s = [pb(f"ps_s{i}") for i in range(3)]
        ps_t = [pb(f"ps_t{i}") for i in range(2)]
        ps_o, ps_sum = pb("ps_o"), pb("ps_sum")
        ps_var = [ps_o, ps_sum]
        ps_g = pb("ps_g")

        loaded = st.enter_context(nc.semaphore("h_loaded"))
        prepared = st.enter_context(nc.semaphore("h_prepared"))
        ctx_in = st.enter_context(nc.semaphore("h_ctx_in"))
        rows_in = st.enter_context(nc.semaphore("h_rows_in"))
        waited = st.enter_context(nc.semaphore("h_waited"))
        index_done = st.enter_context(nc.semaphore("h_index_done"))
        y_turned = sig("y_turned", C)
        y_added = sig("y_added", C)
        norm_ready = sig("norm_ready", 2)
        centred_done = sig("centred_done", 1)
        squared = sig("squared", 1)
        logged = sig("logged", 1)
        rstd_done = sig("rstd_done", 1)
        normed_done = sig("normed_done", 1)
        v_ready = sig("v_ready", 2)
        v_copied = sig("v_copied", 2)
        proj_ready = sig("proj_ready", 4)
        head_squared = sig("head_squared", 4)
        head_var = sig("head_var", 4)
        head_logged = sig("head_logged", 4)
        head_rstd = sig("head_rstd", 4)
        head_normed = sig("head_normed", 4)
        head_out = sig("head_out", 2 * HC1 + 2)
        s_ready = sig("s_ready", STEPS)
        peaked = sig("peaked", STEPS)
        exp_done = sig("exp_done", 2 * STEPS)
        t_ready = sig("t_ready", STEPS)
        t_copied = sig("t_copied", STEPS)
        pv_ready = sig("pv_ready", STEPS // BATCH)
        summed = sig("summed", UNITS)
        o_done = sig("o_done", UNITS)
        out_ready = sig("out_ready", C)
        added = sig("added", C)

        x_all = sh["x"]

        def now_x(i, c):
            return x_all[:, c, bass.ds(i * W, W)]

        def unit(s):
            return s // HC1 // 2, s // HC1 % 2

        def head_of(s):
            return 2 * (s % BATCH) + s % HC1 // BATCH

        with nc.Block() as block:
            @block.sync
            def _(sp):
                for to, of in [(wq, io["L1_Wq"]), (wkv, io["L1_Wkv"]), (wp, io["L1_Wp"])]:
                    sp.dma_start(to[:], of.rearrange("(c p) n -> p c n", p=P)).then_inc(loaded, 16)
                sp.dma_start(cols[:], io["L1_cols"]).then_inc(loaded, 16)
                with sp.Fori(0, PAIRS) as i:
                    sp.wait_ge(proj_ready.sem, proj_ready.before(i, 2))
                    sp.dma_start(ctx[:], io["ctxT"][:, :, bass.ds(i * W, W)]).then_inc(ctx_in, 16)

            @block.gpsimd
            def _(pool):
                with pool.Fori(0, PAIRS) as i:
                    pool.wait_ge(y_turned.sem, y_turned.before(i, C))
                    pool.wait_ge(rows_in, i * (16 * TT))
                    nc.gpsimd.tensor_copy(index[:], sh["slot"][:, bass.ds(i * TT, TT)]).then_inc(index_done, 1)
                    pool.wait_ge(index_done, i + 1)
                    pool.sem_inc(waited, 1)
                    for t in range(TT):
                        nc.gpsimd.indirect_dma_start(
                            taken[:, t, :], None, sh["sorted_y"],
                            bass.IndirectOffsetOnAxis(ap=index[:, t:t + 1], axis=0)).then_inc(rows_in, 16)

            @block.tensor
            def _(pe):
                start_ahead(pe, [y_turned, norm_ready, v_ready, proj_ready, head_var, s_ready, t_ready, pv_ready,
                                 out_ready])
                pe.wait_ge(prepared, 1)
                pe.wait_ge(loaded, 64)
                mean256, mean16, ident = sh["mat"]("mean256"), sh["mat"]("mean16"), sh["mat"]("ident")
                with pe.Fori(0, PAIRS) as i:
                    pe.wait_ge(rows_in, i * (16 * TT) + 16 * TT)
                    pe.wait_ge(t_copied.sem, t_copied.at(i, 0))
                    for c in range(C):
                        for t in range(TT):
                            mm = nc.tensor.transpose(ps_t[c][:, t * P:(t + 1) * P], taken[:, t, c * P:(c + 1) * P], ident)
                        mm.then_inc(y_turned.sem, 1)
                    pe.wait_ge(ctx_in, i * 16 + 16)
                    for g in range(2):
                        pe.wait_ge(y_added.sem, y_added.at(i, g + 1))
                        for t in range(2):
                            for c in range(C):
                                mm = nc.tensor.matmul(ps_t[g][:, t * D:(t + 1) * D],
                                                      ctx[:, c, (2 * g + t) * P:(2 * g + t + 1) * P], wkv[:, c, D:2 * D],
                                                      start=(c == 0), stop=(c == C - 1))
                        mm.then_inc(v_ready.sem, 1)
                    pe.wait_ge(added.sem, added.at(i, 0))
                    for c in range(C):
                        mm = nc.tensor.matmul(ps_g[:], mean256, now_x(i, c), start=(c == 0), stop=(c == C - 1))
                    mm.then_inc(norm_ready.sem, 1)

                    def project(g):
                        if g < 2:
                            pe.wait_ge(v_copied.sem, v_copied.at(i, g + 1))
                        else:
                            pe.wait_ge(head_normed.sem, head_normed.at(i, g - 1))
                        for c in range(C):
                            w, of = (wkv, ctx) if g < 2 else (wq, normed)
                            mm = nc.tensor.matmul(ps_t[g % 2][:], w[:, c, (g % 2) * P:(g % 2 + 1) * P], of[:, c, :],
                                                  start=(c == 0), stop=(c == C - 1))
                        mm.then_inc(proj_ready.sem, 1)

                    def head_variance(g):
                        pe.wait_ge(head_squared.sem, head_squared.at(i, g + 1))
                        pe.wait_ge(head_rstd.sem, head_rstd.at(i, g - 1))
                        nc.tensor.matmul(ps_var[g % 2][:], mean16, sq[g % 2][:], start=True, stop=True).then_inc(head_var.sem, 1)

                    project(0)
                    project(1)
                    pe.wait_ge(squared.sem, squared.at(i, 1))
                    for c in range(C):
                        mm = nc.tensor.matmul(ps_g[:], mean256, squares[:, c, :], start=(c == 0), stop=(c == C - 1))
                    mm.then_inc(norm_ready.sem, 1)
                    pe.wait_ge(o_done.sem, o_done.at(i, 0))
                    head_variance(0)
                    head_variance(1)
                    pe.wait_ge(normed_done.sem, normed_done.at(i, 1))
                    project(2)
                    project(3)
                    head_variance(2)
                    head_variance(3)
                    pe.wait_ge(head_out.sem, head_out.at(i, HC1 + 2))

                    def tick(s):
                        if s < STEPS:
                            c, b = unit(s)
                            if s == 2 * HC1:
                                pe.wait_ge(head_out.sem, head_out.at(i, 2 * HC1 + 2))
                            pe.wait_ge(exp_done.sem, exp_done.at(i, 2 * (s - 2)))
                            for u in range(2):
                                mm = nc.tensor.matmul(ps_s[s % 3][:, u * S:(u + 1) * S],
                                                      qT[:, c, b * S + u * P:b * S + (u + 1) * P],
                                                      kT[:, c, head_of(s), b * S:(b + 1) * S],
                                                      start=True, stop=True)
                            mm.then_inc(s_ready.sem, 1)
                        if LAG_T <= s < STEPS + LAG_T:
                            n = s - LAG_T
                            if n < 2:
                                pe.wait_ge(head_normed.sem, head_normed.at(i, 4))
                            else:
                                pe.wait_ge(t_copied.sem, t_copied.at(i, n - 1))
                            pe.wait_ge(exp_done.sem, exp_done.at(i, 2 * n + 2))
                            for k in range(2):
                                for u in range(2):
                                    mm = nc.tensor.transpose(ps_t[n % 2][:, k * S + u * P:k * S + (u + 1) * P],
                                                             prob[n % 3][:, u, k * P:(k + 1) * P], ident)
                            mm.then_inc(t_ready.sem, 1)
                        if s >= LAG_V and (s - LAG_V) % BATCH == BATCH - 1:
                            n = s - LAG_V - (BATCH - 1)
                            c, b = unit(n)
                            odd, half = n % HC1 // BATCH, n // HC1 % 2
                            if not odd:
                                pe.wait_ge(o_done.sem, o_done.at(i, n // HC1 - 1))
                            pe.wait_ge(t_copied.sem, t_copied.at(i, n + BATCH))
                            for to, of_ones in (ps_o, False), (ps_sum, True):
                                for k in range(2):
                                    for j in range(BATCH):
                                        w = ones[:, odd, :] if of_ones else V[:, 2 * b + k, BATCH * c + j, odd, :]
                                        mm = nc.tensor.matmul(to[G * j:G * (j + 1), half * S:(half + 1) * S], w,
                                                              probT[(n + j) % RING][:, k, :],
                                                              start=(odd == 0 and k == 0), stop=(odd == 1 and k == 1))
                            mm.then_inc(pv_ready.sem, 1)

                    for s in range(STEPS + LAG_V):
                        tick(s)
                    pe.wait_ge(o_done.sem, o_done.at(i, UNITS))
                    for m in range(C):
                        pe.wait_ge(added.sem, added.at(i, m))
                        for c in range(C):
                            mm = nc.tensor.matmul(ps_g[:], wp[:, c, m * P:(m + 1) * P], oT[:, c, :],
                                                  start=(c == 0), stop=(c == C - 1))
                        mm.then_inc(out_ready.sem, 1)

            @block.scalar
            def _(act):
                start_ahead(act, [squared, v_copied, head_squared, head_out, exp_done, logged, rstd_done,
                                  head_logged, head_rstd])
                nc.scalar.preload_act_table_set(LOG_EXP)
                act.wait_ge(prepared, 1)
                with act.Fori(0, PAIRS) as i:
                    for g in range(2):
                        act.wait_ge(v_ready.sem, v_ready.at(i, g + 1))
                        heads = ps_t[g][:].rearrange("p (t h e d) -> p t h e d", t=2, e=2, d=D1)
                        nc.scalar.copy(V[:, 2 * g:2 * g + 2, :, 0, 0:D1], heads[:, :, :, 0, :])
                        nc.scalar.copy(V[:, 2 * g:2 * g + 2, :, 1, D1:G], heads[:, :, :, 1, :]).then_inc(v_copied.sem, 1)

                    def head_square(g):
                        act.wait_ge(proj_ready.sem, proj_ready.at(i, g + 1))
                        act.wait_ge(head_var.sem, head_var.at(i, g - 1))
                        nc.scalar.activation(sq[g % 2][:], ps_t[g % 2][:], ACT.Square).then_inc(head_squared.sem, 1)

                    def scale_shift(out, g, by):
                        nc.scalar.activation(out, hn[g][:], ACT.Identity, scale=by[:, 0:1],
                                             bias=by[:, 1:2]).then_inc(head_out.sem, 1)

                    head_square(0)
                    act.wait_ge(centred_done.sem, centred_done.at(i, 1))
                    nc.scalar.activation(squares[:], centred[:], ACT.Square).then_inc(squared.sem, 1)
                    head_square(1)
                    act.wait_ge(norm_ready.sem, norm_ready.at(i, 2))
                    nc.scalar.activation(log[:], ps_g[:], ACT.Ln, bias=sh["eps"][:]).then_inc(logged.sem, 1)
                    act.wait_ge(logged.sem, logged.at(i, 1))
                    nc.scalar.activation(rstd[:], log[:], ACT.Exp, scale=-0.5).then_inc(rstd_done.sem, 1)

                    def head_deviate(g):
                        act.wait_ge(head_var.sem, head_var.at(i, g + 1))
                        nc.scalar.activation(hlog[g % 2][:], ps_var[g % 2][:], ACT.Ln, bias=sh["eps"][:]).then_inc(head_logged.sem, 1)
                        act.wait_ge(head_logged.sem, head_logged.at(i, g + 1))
                        act.wait_ge(head_normed.sem, head_normed.at(i, g - 1))
                        nc.scalar.activation(hrstd[g % 2][:], hlog[g % 2][:], ACT.Exp, scale=-0.5).then_inc(head_rstd.sem, 1)

                    head_deviate(0)
                    head_deviate(1)
                    act.wait_ge(head_normed.sem, head_normed.at(i, 1))
                    for h in range(HC1):
                        scale_shift(kT[:, 0, h, :], 0, k_scale[:, h, :])
                    head_square(2)
                    head_square(3)
                    head_deviate(2)
                    head_deviate(3)
                    for c in range(C):
                        act.wait_ge(head_normed.sem, head_normed.at(i, 3 + c))
                        scale_shift(qT[:, c, :], 2 + c, q_scale)

                    def tick(s):
                        if s < STEPS:
                            act.wait_ge(peaked.sem, peaked.at(i, s + 1))
                            act.wait_ge(t_ready.sem, t_ready.at(i, s - 2))
                            for h in range(2):
                                nc.scalar.activation(prob[s % 3][:, h, :], ps_s[s % 3][:, h * S:(h + 1) * S], ACT.Exp,
                                                     bias=peak[:, s % 3, h:h + 1]).then_inc(exp_done.sem, 1)
                        if s < HC1:
                            scale_shift(kT[:, 1, s, :], 1, k_scale[:, s, :])

                    for s in range(STEPS + LAG_V):
                        tick(s)

            @block.vector
            def _(dve):
                start_ahead(dve, [y_added, centred_done, normed_done, head_normed, peaked,
                                  t_copied, summed, o_done, added])
                nc.vector.memset(V[:], 0.0)
                tanh = sh["tanh"]
                chain = st.enter_context(nc.semaphore("h_chain"))
                made = [0]

                def then(op):
                    made[0] += 1
                    op.then_inc(chain, 1)
                    dve.wait_ge(chain, made[0])

                then(nc.vector.memset(ones[:], 0.0))
                for odd in range(2):
                    nc.vector.memset(ones[:, odd, odd * D1:(odd + 1) * D1], 1.0)
                dve.wait_ge(loaded, 64)
                for w in (wq[:], wkv[:, :, 0:D]):
                    heads = w.rearrange("p c (h d) -> p c h d", d=D1)
                    then(nc.vector.tensor_reduce(sums[:], heads, AX.X, ALU.add))
                    then(nc.vector.tensor_scalar(sums[:], sums[:], 1.0 / D1, None, ALU.mult))
                    then(nc.vector.tensor_tensor(heads, heads, spread(sums[:], D1, 3), ALU.subtract))
                then(nc.vector.tensor_scalar(q_scale[:], cols[:, 2:4], float(D1) ** 0.5, None, ALU.mult))
                for h in range(HC1):
                    then(nc.vector.tensor_scalar(k_scale[:, h, :], cols[:, 2:4], sh["mat"]("mean16")[:, h * D1:h * D1 + 1],
                                                 float(D1), ALU.mult, ALU.mult))
                then(nc.vector.tensor_scalar(bias[:], cols[:, 0:2], tanh[:, 2:3], None, ALU.mult))
                nc.vector.tensor_scalar(wp[:], wp[:], tanh[:, 2:3], None, ALU.mult).then_inc(prepared, 1)
                with dve.Fori(0, PAIRS) as i:
                    for c in range(C):
                        dve.wait_ge(y_turned.sem, y_turned.at(i, c + 1))
                        nc.vector.scalar_tensor_tensor(now_x(i, c), ps_t[c][:], tanh[:, 1:2], now_x(i, c),
                                                       ALU.mult, ALU.add).then_inc(y_added.sem, 1)
                    dve.wait_ge(norm_ready.sem, norm_ready.at(i, 1))
                    nc.vector.tensor_tensor(centred[:], x_all[:, :, bass.ds(i * W, W)], spread(ps_g[:], C, 1),
                                            ALU.subtract).then_inc(centred_done.sem, 1)

                    def head_norm(g):
                        dve.wait_ge(head_rstd.sem, head_rstd.at(i, g + 1))
                        dve.wait_ge(head_out.sem, head_out.at(i, 0))
                        nc.vector.tensor_tensor(hn[g][:], ps_t[g % 2][:], hrstd[g % 2][:], ALU.mult).then_inc(head_normed.sem, 1)

                    dve.wait_ge(rstd_done.sem, rstd_done.at(i, 1))
                    nc.vector.tensor_tensor(normed[:], centred[:], spread(rstd[:], C, 1), ALU.mult).then_inc(normed_done.sem, 1)
                    for g in range(4):
                        head_norm(g)

                    def tick(s):
                        if s < STEPS:
                            dve.wait_ge(s_ready.sem, s_ready.at(i, s + 1))
                            nc.vector.tensor_reduce(peak[:, s % 3, :], ps_s[s % 3][:].rearrange("p (h k) -> p h k", h=2),
                                                    AX.X, ALU.max, negate=True).then_inc(peaked.sem, 1)
                        if LAG_T <= s < STEPS + LAG_T:
                            n = s - LAG_T
                            dve.wait_ge(t_ready.sem, t_ready.at(i, n + 1))
                            dve.wait_ge(pv_ready.sem, pv_ready.at(i, n // BATCH - 1))
                            nc.vector.tensor_copy(probT[n % RING][:].rearrange("p k q -> p (k q)"), ps_t[n % 2][:]).then_inc(t_copied.sem, 1)
                        if s > LAG_V and (s - LAG_V) % HC1 == HC1 - 1:
                            u = (s - LAG_V) // HC1
                            c, b = unit(u * HC1)
                            half = slice(u % 2 * S, (u % 2 + 1) * S)
                            dve.wait_ge(pv_ready.sem, pv_ready.at(i, 2 * (u + 1)))
                            nc.vector.reciprocal(rsum[:, u % 2, :], ps_sum[:, half]).then_inc(summed.sem, 1)
                            dve.wait_ge(summed.sem, summed.at(i, u + 1))
                            nc.vector.tensor_tensor(oT[:, c, b * S:(b + 1) * S], ps_o[:, half], rsum[:, u % 2, :],
                                                    ALU.mult).then_inc(o_done.sem, 1)

                    for s in range(STEPS + LAG_V):
                        tick(s)
                    for m in range(C):
                        dve.wait_ge(out_ready.sem, out_ready.at(i, m + 1))
                        nc.vector.scalar_tensor_tensor(now_x(i, m), ps_g[:], bias[:, m:m + 1], now_x(i, m),
                                                       ALU.add, ALU.add).then_inc(added.sem, 1)


FEED_LOADS = 4


def load_attention_weights(engine, io, weights, one):
    engine.dma_start(weights["wqkv"][:], io["F_wqkv"][one].rearrange("l (c p) n -> p (l c) n", p=P)).then_inc(weights["attention_in"], 16)
    engine.dma_start(weights["scales"][:], io["F_scales"][one].rearrange("l p n -> p (l n)")).then_inc(weights["attention_in"], 16)


def load_output_weights(engine, io, weights, one):
    engine.dma_start(weights["wo"][:], io["F_wo"][one].rearrange("l (c p) n -> p (l c) n", p=P)).then_inc(weights["output_in"], 16)


def load_feed_weights(engine, io, weights, one):
    full = HID - HL
    for to, of in [(weights["cols"][:], io["F_cols"][one].rearrange("l p n -> p (l n)")),
                   (weights["w1"][:], io["F_w1"][one].rearrange("l (c p) n -> p (l c) n", p=P)),
                   (weights["w2"][:, 0:HC - 1, :], io["F_w2"][one, 0:full, :].rearrange("l (c p) n -> p (l c) n", p=P)),
                   (weights["w2"][0:HL, HC - 1, :], io["F_w2"][one, full:HID, :].rearrange("l p n -> p (l n)"))]:
        engine.dma_start(to, of).then_inc(weights["feed_in"], 16)


def start_layers(nc, io, sh):
    with ExitStack() as st:
        def sig(name):
            return Signal(st, nc, "y_" + name, 2)

        centred, squares = ([st.enter_context(nc.sbuf_tensor(f"y_{n}{i}", [P, C, W], F32)) for i in range(2)]
                            for n in ("centred", "squares"))
        log, rstd = ([st.enter_context(nc.sbuf_tensor(f"y_{n}{i}", [P, W], F32)) for i in range(2)] for n in ("log", "rstd"))
        ps_mean, ps_var = ([st.enter_context(nc.psum_tensor(f"y_ps_{n}{i}", [P, W], F32)) for i in range(2)]
                           for n in ("mean", "var"))
        mean_ready, var_ready = sig("mean_ready"), sig("var_ready")
        centred_done, y_done = sig("centred_done"), sig("y_done")
        squared, logged, rstd_done = sig("squared"), sig("logged"), sig("rstd_done")
        x_all, y_all = sh["x"], sh["y"]

        def tokens(i, n):
            return bass.ds((2 * i + n) * W, W)

        with nc.Block() as block:
            @block.sync
            def _(sp):
                for load in (load_attention_weights, load_output_weights, load_feed_weights):
                    load(sp, io, sh["layer_weights"], slice(0, 1))

            @block.tensor
            def _(pe):
                start_ahead(pe, [mean_ready, var_ready])
                mean256 = sh["mat"]("mean256")
                with pe.Fori(0, PAIRS // 2) as i:
                    for n in range(2):
                        pe.wait_ge(centred_done.sem, centred_done.at(i, n - 1))
                        for c in range(C):
                            mm = nc.tensor.matmul(ps_mean[n][:], mean256, x_all[:, c, tokens(i, n)], start=(c == 0), stop=(c == C - 1))
                        mm.then_inc(mean_ready.sem, 1)
                    for n in range(2):
                        pe.wait_ge(squared.sem, squared.at(i, n + 1))
                        for c in range(C):
                            mm = nc.tensor.matmul(ps_var[n][:], mean256, squares[n][:, c, :], start=(c == 0), stop=(c == C - 1))
                        mm.then_inc(var_ready.sem, 1)

            @block.vector
            def _(dve):
                start_ahead(dve, [centred_done, y_done])
                with dve.Fori(0, PAIRS // 2) as i:
                    for n in range(2):
                        dve.wait_ge(mean_ready.sem, mean_ready.at(i, n + 1))
                        dve.wait_ge(y_done.sem, y_done.at(i, n - 1))
                        nc.vector.tensor_tensor(centred[n][:], x_all[:, :, tokens(i, n)], spread(ps_mean[n][:], C, 1),
                                                ALU.subtract).then_inc(centred_done.sem, 1)
                    for n in range(2):
                        dve.wait_ge(rstd_done.sem, rstd_done.at(i, n + 1))
                        nc.vector.tensor_tensor(y_all[:, :, tokens(i, n)], centred[n][:], spread(rstd[n][:], C, 1),
                                                ALU.mult).then_inc(y_done.sem, 1)

            @block.scalar
            def _(act):
                start_ahead(act, [squared, logged, rstd_done])
                with act.Fori(0, PAIRS // 2) as i:
                    for n in range(2):
                        act.wait_ge(centred_done.sem, centred_done.at(i, n + 1))
                        nc.scalar.activation(squares[n][:], centred[n][:], ACT.Square).then_inc(squared.sem, 1)
                    for n in range(2):
                        act.wait_ge(var_ready.sem, var_ready.at(i, n + 1))
                        nc.scalar.activation(log[n][:], ps_var[n][:], ACT.Ln, bias=sh["eps"][:]).then_inc(logged.sem, 1)
                        act.wait_ge(logged.sem, logged.at(i, n + 1))
                        nc.scalar.activation(rstd[n][:], log[n][:], ACT.Exp, scale=-0.5).then_inc(rstd_done.sem, 1)


def local_layers(nc, io, sh):
    with ExitStack() as st:
        def sb(name, shape, dt=F32):
            return st.enter_context(nc.sbuf_tensor("l_" + name, shape, dt))

        def pb(name):
            return st.enter_context(nc.psum_tensor("l_" + name, [P, 512], F32))

        def sem(name):
            return st.enter_context(nc.semaphore("l_" + name))

        def sig(name, per):
            return Signal(st, nc, "l_" + name, per)

        QC = INNER // P
        STEPS = 2 * H2
        LAG_T, LAG_V = 2, 5
        RING = 6
        PW = 3 * P

        weights = sh["layer_weights"]
        wqkv, scales, wo, w1, w2, cols = (weights[n] for n in ("wqkv", "scales", "wo", "w1", "w2", "cols"))
        turn = [sb(f"turn{i}", [P, P]) for i in range(2)]
        tables = sb("tables", [P, 4, S])
        mask16 = sb("mask16", [P, 2 * S], BF16)
        ident16 = sb("ident16", [P, P], BF16)
        hT, h_ff = sb("hT", [P, C, W]), sb("h_ff", [P, C, W])
        centred, squares = sb("centred", [P, C, W]), sb("squares", [P, C, W])
        log, rstd, normed, h2 = sb("log", [P, W]), sb("rstd", [P, W]), sb("normed", [P, C, W]), sb("h2", [P, C, W])
        V = sb("V", [P, TT, INNER])
        raw, sq, fl, ln, rn, ta, tb, tc = (
            [sb(f"{n}{i}", [P, W]) for i in range(2)] for n in ("raw", "sq", "fl", "ln", "rn", "ta", "tb", "tc"))
        qT = sb("qT", [P, QC, W])
        kT = [sb(f"kT{i}", [P, QC, W]) for i in range(2)]
        ones = sb("ones", [P, D2])
        peak = sb("peak", [P, 3, 2])
        prob = [sb(f"prob{i}", [P, PW]) for i in range(3)]
        probT = [sb(f"probT{i}", [P, PW]) for i in range(RING)]
        rsum = sb("rsum", [P, 2, S])
        oT = sb("oT", [P, QC, W])
        gelu = [sb(f"gelu{i}", [P, W]) for i in range(2)]
        hid = sb("hid", [P, HC, W])

        ps_s = [pb(f"ps_s{i}") for i in range(3)]
        ps_t = [pb(f"ps_t{i}") for i in range(2)]
        ps_o = [pb(f"ps_o{i}") for i in range(2)]
        ps_g = pb("ps_g")

        tables_in = sem("tables_in")
        zeroed, mask_done = sem("zeroed"), sem("mask_done")
        turn_scaled, waited = sem("turn_scaled"), sem("waited")
        shifted = sig("shifted", 1)
        shifted_ff = sig("shifted_ff", 1)
        v_ready = sig("v_ready", TT)
        v_copied = sig("v_copied", TT)
        proj_ready = sig("proj_ready", 2 * QC)
        raw_done = sig("raw_done", 2 * QC)
        sq_done = sig("sq_done", 2 * QC)
        length_ready = sig("length_ready", 2 * QC)
        turned = sig("turned", 2 * QC)
        floored = sig("floored", 2 * QC)
        ln_done = sig("ln_done", 2 * QC)
        rn_done = sig("rn_done", 2 * QC)
        cos_done = sig("cos_done", 2 * QC)
        sin_done = sig("sin_done", 2 * QC)
        rope_sum = sig("rope_sum", 2 * QC)
        rope_even = sig("rope_even", QC)
        rope_done = sig("rope_done", 2 * QC)
        s_ready = sig("s_ready", STEPS)
        peaked = sig("peaked", STEPS)
        exp_done = sig("exp_done", 2 * STEPS)
        t_ready = sig("t_ready", STEPS)
        t_even = sig("t_even", STEPS // 2)
        t_odd = sig("t_odd", STEPS // 2)
        pv_ready = sig("pv_ready", STEPS // 2)
        summed = sig("summed", STEPS // 2)
        o_done = sig("o_done", STEPS // 2)
        out_ready = sig("out_ready", C)
        added = sig("added", C)
        norm_ready = sig("norm_ready", 2)
        centred_done = sig("centred_done", 1)
        squared = sig("squared", 1)
        logged = sig("logged", 1)
        rstd_done = sig("rstd_done", 1)
        normed_done = sig("normed_done", 1)
        h2_done = sig("h2_done", C)
        g_ready = sig("g_ready", HC)
        a_ready = sig("a_ready", HC)
        gelu_done = sig("gelu_done", HC)
        hid_done = sig("hid_done", HC)
        ff_ready = sig("ff_ready", C)
        grown = sig("grown", C)

        x_all, y_all = sh["x"], sh["y"]

        def hrows(j):
            return P if j < HC - 1 else HL

        def now_y(i, c):
            return y_all[:, c, bass.ds(i * W, W)]

        def two(ap):
            return ap.rearrange("p (b t) -> p b t", b=2)

        def t_copied(n, step):
            s = t_odd if n % 2 else t_even
            return s.sem, s.at(step, n // 2 + 1)

        with nc.Block() as block:
            @block.sync
            def _(sp):
                sp.dma_start(tables[:], io["rope"]).then_inc(tables_in, 16)
                sp.dma_start(squares[:, 0, :], io["mask"]).then_inc(tables_in, 16)
                with sp.Fori(1, DEPTH) as l:
                    sp.wait_ge(cos_done.sem, cos_done.at(l * PAIRS, 0))
                    sp.wait_ge(proj_ready.sem, proj_ready.at(l * PAIRS, 0))
                    load_attention_weights(sp, io, weights, bass.ds(l, 1))
                    sp.wait_ge(out_ready.sem, out_ready.at(l * PAIRS, 0))
                    load_output_weights(sp, io, weights, bass.ds(l, 1))
                    sp.wait_ge(grown.sem, grown.at(l * PAIRS, 0))
                    load_feed_weights(sp, io, weights, bass.ds(l, 1))

            @block.tensor
            def _(pe):
                start_ahead(pe, [v_ready, proj_ready, length_ready, turned, s_ready, t_ready, pv_ready,
                                 out_ready, norm_ready, g_ready, a_ready, ff_ready])
                mean256, heads64, ident = sh["mat"]("mean256"), sh["mat"]("heads64"), sh["mat"]("ident")
                pe.wait_ge(mask_done, 1)
                with pe.Fori(0, DEPTH) as l:
                    def front_v(i):
                        pe.wait_ge(shifted.sem, shifted.at(i, 1))
                        for t in range(TT):
                            pe.wait_ge(v_copied.sem, v_copied.at(i, t - 1))
                            for c in range(C):
                                mm = nc.tensor.matmul(ps_s[t % 2][:], hT[:, c, t * P:(t + 1) * P], wqkv[:, c, 2 * INNER:],
                                                      start=(c == 0), stop=(c == C - 1))
                            mm.then_inc(v_ready.sem, 1)

                    def rope(i, g, o_free):
                        pe.wait_ge(raw_done.sem, raw_done.at(i, g + 1))
                        if g < 2:
                            pe.wait_ge(v_copied.sem, v_copied.at(i, TT))
                        else:
                            pe.wait_ge(sin_done.sem, sin_done.at(i, g - 1))
                        nc.tensor.matmul(ps_s[g % 2][:], turn[g // QC][:], raw[g % 2][:], start=True, stop=True).then_inc(turned.sem, 1)
                        pe.wait_ge(sq_done.sem, sq_done.at(i, g + 1))
                        if g < 2:
                            pe.wait_ge(*o_free)
                        else:
                            pe.wait_ge(floored.sem, floored.at(i, g - 1))
                        nc.tensor.matmul(ps_o[g % 2][:], heads64, sq[g % 2][:], start=True, stop=True).then_inc(length_ready.sem, 1)

                    def front_qk(i, o_free, norm_variance=None):
                        for g in range(2 * QC):
                            pe.wait_ge(sq_done.sem, sq_done.at(i, g - 1))
                            for c in range(C):
                                mm = nc.tensor.matmul(ps_t[g % 2][:], wqkv[:, c, g * P:(g + 1) * P], hT[:, c, :],
                                                      start=(c == 0), stop=(c == C - 1))
                            mm.then_inc(proj_ready.sem, 1)
                            if g:
                                rope(i, g - 1, o_free)
                            if g == 1 and norm_variance:
                                norm_variance()
                        rope(i, 2 * QC - 1, o_free)

                    def body(pair, last):
                        i = l * PAIRS + pair
                        pe.wait_ge(rope_done.sem, rope_done.at(i, 2 * QC))

                        def tick(s):
                            if s < STEPS:
                                b, h = s // H2, s % H2
                                c = h // 2
                                pe.wait_ge(exp_done.sem, exp_done.at(i, 2 * (s - 2)))
                                bank = ps_s[s % 3]
                                nc.tensor.matmul(bank[:], ident16[:], mask16[:], start=True, stop=False, skip_group_check=True)
                                for w in range(2):
                                    n = (w + 1) * P
                                    mm = nc.tensor.matmul(bank[:, w * 2 * P:w * 2 * P + n],
                                                          qT[:, c, b * S + w * P:b * S + (w + 1) * P],
                                                          kT[h % 2][:, c, b * S:b * S + n],
                                                          start=False, stop=True, skip_group_check=True)
                                mm.then_inc(s_ready.sem, 1)
                            if LAG_T <= s < STEPS + LAG_T:
                                n = s - LAG_T
                                if n < 2:
                                    pe.wait_ge(sq_done.sem, sq_done.at(i, 2 * QC))
                                else:
                                    pe.wait_ge(*t_copied(n - 2, i))
                                pe.wait_ge(exp_done.sem, exp_done.at(i, 2 * n + 2))
                                for k in range(3):
                                    mm = nc.tensor.transpose(ps_t[n % 2][:, k * P:(k + 1) * P], prob[n % 3][:, k * P:(k + 1) * P], ident)
                                mm.then_inc(t_ready.sem, 1)
                            if s > LAG_V and (s - LAG_V) % 2:
                                n = s - LAG_V - 1
                                b, h, bank = n // H2, n % H2, ps_o[n // 2 % 2]
                                pe.wait_ge(o_done.sem, o_done.at(i, n // 2 - 1))
                                pe.wait_ge(*t_copied(n, i))
                                pe.wait_ge(*t_copied(n + 1, i))
                                for of_ones in range(2):
                                    for k in range(2):
                                        for j in range(2):
                                            w = ones[:] if of_ones else V[:, 2 * b + k, (h + j) * D2:(h + j + 1) * D2]
                                            mm = nc.tensor.matmul(bank[j * D2:(j + 1) * D2, of_ones * S + k * P:(of_ones + 1) * S], w,
                                                                  probT[(n + j) % RING][:, k * S:S + k * P],
                                                                  start=(k == 0), stop=(k == 1))
                                mm.then_inc(pv_ready.sem, 1)

                        for s in range(STEPS + LAG_V):
                            tick(s)
                        pe.wait_ge(o_done.sem, o_done.at(i, STEPS // 2))
                        pe.wait_ge(weights["output_in"], l * 16 + 16)
                        for m in range(C):
                            for c in range(QC):
                                mm = nc.tensor.matmul(ps_o[m][:], wo[:, c, m * P:(m + 1) * P], oT[:, c, :],
                                                      start=(c == 0), stop=(c == QC - 1))
                            mm.then_inc(out_ready.sem, 1)
                        if not last:
                            front_v(i + 1)
                        pe.wait_ge(shifted_ff.sem, shifted_ff.at(i, 1))
                        for c in range(C):
                            mm = nc.tensor.matmul(ps_g[:], mean256, h_ff[:, c, :], start=(c == 0), stop=(c == C - 1))
                        mm.then_inc(norm_ready.sem, 1)

                        def norm_variance():
                            pe.wait_ge(squared.sem, squared.at(i, 1))
                            for c in range(C):
                                mm = nc.tensor.matmul(ps_g[:], mean256, squares[:, c, :], start=(c == 0), stop=(c == C - 1))
                            mm.then_inc(norm_ready.sem, 1)

                        if last:
                            norm_variance()
                        else:
                            front_qk(i + 1, (added.sem, added.at(i, C)), norm_variance)
                            pe.wait_ge(sq_done.sem, sq_done.at(i + 1, 2 * QC))
                            pe.wait_ge(sin_done.sem, sin_done.at(i + 1, 2 * QC))
                        pe.wait_ge(weights["feed_in"], l * (16 * FEED_LOADS) + 16 * FEED_LOADS)
                        pe.wait_ge(h2_done.sem, h2_done.at(i, C))
                        for j in range(HC):
                            m = hrows(j)
                            pe.wait_ge(gelu_done.sem, gelu_done.at(i, j - 1))
                            for c in range(C):
                                mm = nc.tensor.matmul(ps_t[j % 2][0:m, :], w1[:, c, HID + j * P:HID + j * P + m], h2[:, c, :],
                                                      start=(c == 0), stop=(c == C - 1))
                            mm.then_inc(g_ready.sem, 1)
                            pe.wait_ge(hid_done.sem, hid_done.at(i, j - 1))
                            for c in range(C):
                                mm = nc.tensor.matmul(ps_s[j % 2][0:m, :], w1[:, c, j * P:j * P + m], h2[:, c, :],
                                                      start=(c == 0), stop=(c == C - 1))
                            mm.then_inc(a_ready.sem, 1)
                        if not last:
                            pe.wait_ge(floored.sem, floored.at(i + 1, 2 * QC))
                        for m in range(C):
                            for j in range(HC):
                                n = hrows(j)
                                if m == 0:
                                    pe.wait_ge(hid_done.sem, hid_done.at(i, j + 1))
                                mm = nc.tensor.matmul(ps_o[m][:], w2[0:n, j, m * P:(m + 1) * P], hid[0:n, j, :],
                                                      start=(j == 0), stop=(j == HC - 1))
                            mm.then_inc(ff_ready.sem, 1)

                    first = l * PAIRS
                    pe.wait_ge(weights["attention_in"], l * 32 + 32)
                    pe.wait_ge(turn_scaled, l * 2 + 2)
                    front_v(first)
                    front_qk(first, (grown.sem, grown.at(first, 0)))
                    with pe.Fori(0, PAIRS - 1) as pair:
                        body(pair, last=False)
                    body(PAIRS - 1, last=True)

            @block.scalar
            def _(act):
                start_ahead(act, [shifted, shifted_ff, v_copied, raw_done, sq_done, exp_done, t_odd, squared, h2_done,
                                  gelu_done, ln_done, rn_done, logged, rstd_done])
                act.wait_ge(zeroed, 1)
                with act.Fori(0, DEPTH) as l:
                    def shift(to, pair, signal):
                        act.sem_inc(waited, 1)
                        nc.scalar.copy(to[:, 0, :], now_y(pair, 0))
                        late = two(to[:, 1, :])[:, :, 1:S]
                        nc.scalar.copy(late, two(now_y(pair, 1))[:, :, 0:S - 1]).then_inc(signal.sem, 1)

                    def front_v(i):
                        for t in range(TT):
                            act.wait_ge(v_ready.sem, v_ready.at(i, t + 1))
                            nc.scalar.copy(V[:, t, :], ps_s[t % 2][:]).then_inc(v_copied.sem, 1)

                    def length(i, g):
                        act.wait_ge(floored.sem, floored.at(i, g + 1))
                        nc.scalar.activation(ln[g % 2][:], fl[g % 2][:], ACT.Ln).then_inc(ln_done.sem, 1)
                        act.wait_ge(ln_done.sem, ln_done.at(i, g + 1))
                        act.wait_ge(rope_done.sem, rope_done.at(i, g - 1))
                        nc.scalar.activation(rn[g % 2][:], ln[g % 2][:], ACT.Exp, scale=-0.5).then_inc(rn_done.sem, 1)

                    def front_qk(i, between={}):
                        for g in range(2 * QC):
                            act.wait_ge(proj_ready.sem, proj_ready.at(i, g + 1))
                            act.wait_ge(turned.sem, turned.at(i, g - 1))
                            act.wait_ge(cos_done.sem, cos_done.at(i, g - 1))
                            nc.scalar.copy(raw[g % 2][:], ps_t[g % 2][:]).then_inc(raw_done.sem, 1)
                            act.wait_ge(length_ready.sem, length_ready.at(i, g - 1))
                            nc.scalar.activation(sq[g % 2][:], ps_t[g % 2][:], ACT.Square).then_inc(sq_done.sem, 1)
                            if g:
                                length(i, g - 1)
                            if g in between:
                                between[g]()
                        length(i, 2 * QC - 1)

                    def body(pair, last):
                        i = l * PAIRS + pair
                        nc.scalar.preload_act_table_set(LOG_EXP)
                        if not last:
                            act.wait_ge(proj_ready.sem, proj_ready.at(i, 2 * QC))
                            shift(hT, pair + 1, shifted)

                        def tick(s):
                            if s < STEPS:
                                act.wait_ge(peaked.sem, peaked.at(i, s + 1))
                                act.wait_ge(t_ready.sem, t_ready.at(i, s - 2))
                                for w in range(2):
                                    n = (w + 1) * P
                                    nc.scalar.activation(prob[s % 3][:, w * P:w * P + n], ps_s[s % 3][:, w * 2 * P:w * 2 * P + n],
                                                         ACT.Exp, bias=peak[:, s % 3, w:w + 1]).then_inc(exp_done.sem, 1)
                            n = s - LAG_T
                            if 0 <= n < STEPS and n % 2:
                                act.wait_ge(t_ready.sem, t_ready.at(i, n + 1))
                                act.wait_ge(pv_ready.sem, pv_ready.at(i, (n - RING) // 2 + 1))
                                nc.scalar.copy(probT[n % RING][:], ps_t[1][:, 0:PW]).then_inc(t_odd.sem, 1)

                        for s in range(STEPS + LAG_V):
                            tick(s)
                        act.wait_ge(added.sem, added.at(i, C))
                        shift(h_ff, pair, shifted_ff)
                        if not last:
                            front_v(i + 1)

                        def norm_squares():
                            act.wait_ge(centred_done.sem, centred_done.at(i, 1))
                            nc.scalar.activation(squares[:], centred[:], ACT.Square).then_inc(squared.sem, 1)

                        def norm_deviation():
                            act.wait_ge(norm_ready.sem, norm_ready.at(i, 2))
                            nc.scalar.activation(log[:], ps_g[:], ACT.Ln, bias=sh["eps"][:]).then_inc(logged.sem, 1)
                            act.wait_ge(logged.sem, logged.at(i, 1))
                            nc.scalar.activation(rstd[:], log[:], ACT.Exp, scale=-0.5).then_inc(rstd_done.sem, 1)

                        def norm_scale():
                            act.wait_ge(weights["feed_in"], l * (16 * FEED_LOADS) + 16 * FEED_LOADS)
                            act.wait_ge(normed_done.sem, normed_done.at(i, 1))
                            for c in range(C):
                                nc.scalar.activation(h2[:, c, :], normed[:, c, :], ACT.Identity, scale=cols[:, c:c + 1],
                                                     bias=cols[:, 2 + c:3 + c]).then_inc(h2_done.sem, 1)

                        if last:
                            norm_squares()
                            norm_deviation()
                            norm_scale()
                        else:
                            front_qk(i + 1, {0: norm_squares, 1: norm_deviation, 3: norm_scale})
                        for j in range(HC):
                            m = hrows(j)
                            act.wait_ge(g_ready.sem, g_ready.at(i, j + 1))
                            act.wait_ge(hid_done.sem, hid_done.at(i, j - 1))
                            nc.scalar.activation(gelu[j % 2][0:m, :], ps_t[j % 2][0:m, :], ACT.Gelu,
                                                 bias=cols[0:m, 6 + HC + j:7 + HC + j]).then_inc(gelu_done.sem, 1)

                    nc.scalar.preload_act_table_set(LOG_EXP)
                    act.wait_ge(grown.sem, grown.at(l * PAIRS, 0))
                    shift(hT, 0, shifted)
                    front_v(l * PAIRS)
                    front_qk(l * PAIRS)
                    with act.Fori(0, PAIRS - 1) as pair:
                        body(pair, last=False)
                    body(PAIRS - 1, last=True)

            @block.gpsimd
            def _(pool):
                start_ahead(pool, [rope_sum, rope_even, rope_done])
                with pool.Fori(0, DEPTH * PAIRS) as i:
                    for g in range(2 * QC):
                        pool.wait_ge(sin_done.sem, sin_done.at(i, g + 1))
                        nc.gpsimd.tensor_tensor(tc[g % 2][:], ta[g % 2][:], tb[g % 2][:], ALU.add).then_inc(rope_sum.sem, 1)
                        pool.wait_ge(rope_sum.sem, rope_sum.at(i, g + 1))
                        pool.wait_ge(rn_done.sem, rn_done.at(i, g + 1))
                        if g < QC:
                            nc.gpsimd.tensor_tensor(qT[:, g, :], tc[g % 2][:], rn[g % 2][:], ALU.mult).then_inc(rope_done.sem, 1)
                        else:
                            for odd in range(2):
                                rows = slice(odd * D2, (odd + 1) * D2)
                                done = rope_done if odd else rope_even
                                nc.gpsimd.tensor_tensor(kT[odd][rows, g - QC, :], tc[g % 2][rows, :], rn[g % 2][rows, :],
                                                        ALU.mult).then_inc(done.sem, 1)
                                pool.wait_ge(done.sem, done.at(i, g + 1 if odd else g - QC + 1))

            @block.vector
            def _(dve):
                start_ahead(dve, [floored, cos_done, sin_done, peaked, t_even, summed, o_done, added, centred_done,
                                  normed_done, hid_done, grown])
                nc.vector.memset(ones[:], 1.0)
                for odd in range(2):
                    nc.vector.memset(kT[odd][(1 - odd) * D2:(2 - odd) * D2, :, :], 0.0)
                nc.vector.memset(two(hT[:, 1, :])[:, :, 0:1], 0.0)
                nc.vector.memset(two(h_ff[:, 1, :])[:, :, 0:1], 0.0).then_inc(zeroed, 1)
                dve.wait_ge(tables_in, 32)
                nc.vector.tensor_copy(ident16[:], sh["mat"]("ident"))
                nc.vector.tensor_copy(mask16[:], squares[:, 0, :]).then_inc(mask_done, 1)
                with dve.Fori(0, DEPTH) as l:
                    def front(i, normalise=None):
                        for g in range(2 * QC):
                            n = g // QC
                            dve.wait_ge(rope_done.sem, rope_done.at(i, g - 1))
                            dve.wait_ge(raw_done.sem, raw_done.at(i, g + 1))
                            nc.vector.scalar_tensor_tensor(two(ta[g % 2][:]), two(raw[g % 2][:]), scales[:, n:n + 1],
                                                           spread(tables[:, 2 * n, :], 2, 1), ALU.mult, ALU.mult).then_inc(cos_done.sem, 1)
                            if g == 1 and normalise:
                                normalise()
                            dve.wait_ge(length_ready.sem, length_ready.at(i, g + 1))
                            dve.wait_ge(ln_done.sem, ln_done.at(i, g - 1))
                            nc.vector.tensor_scalar(fl[g % 2][:], ps_o[g % 2][:], 1e-24, 2.0 ** 16, ALU.max, ALU.mult).then_inc(floored.sem, 1)
                            dve.wait_ge(turned.sem, turned.at(i, g + 1))
                            nc.vector.tensor_tensor(two(tb[g % 2][:]), two(ps_s[g % 2][:]), spread(tables[:, 2 * n + 1, :], 2, 1),
                                                    ALU.mult).then_inc(sin_done.sem, 1)

                    def body(pair, last):
                        i = l * PAIRS + pair

                        def tick(s):
                            if s < STEPS:
                                dve.wait_ge(s_ready.sem, s_ready.at(i, s + 1))
                                nc.vector.tensor_reduce(peak[:, s % 3, :], two(ps_s[s % 3][:]), AX.X, ALU.max,
                                                        negate=True).then_inc(peaked.sem, 1)
                            n = s - LAG_T
                            if 0 <= n < STEPS and n % 2 == 0:
                                dve.wait_ge(t_ready.sem, t_ready.at(i, n + 1))
                                dve.wait_ge(pv_ready.sem, pv_ready.at(i, (n - RING) // 2 + 1))
                                nc.vector.tensor_copy(probT[n % RING][:], ps_t[0][:, 0:PW]).then_inc(t_even.sem, 1)
                            if s > LAG_V and (s - LAG_V) % 2:
                                q = (s - LAG_V) // 2
                                b, c, bank = q // QC, q % QC, ps_o[q % 2]
                                dve.wait_ge(pv_ready.sem, pv_ready.at(i, q + 1))
                                nc.vector.reciprocal(rsum[:, q % 2, :], bank[:, S:2 * S]).then_inc(summed.sem, 1)
                                dve.wait_ge(summed.sem, summed.at(i, q + 1))
                                nc.vector.tensor_tensor(oT[:, c, b * S:(b + 1) * S], bank[:, 0:S], rsum[:, q % 2, :],
                                                        ALU.mult).then_inc(o_done.sem, 1)

                        for s in range(STEPS + LAG_V):
                            tick(s)
                        for m in range(C):
                            dve.wait_ge(out_ready.sem, out_ready.at(i, m + 1))
                            nc.vector.tensor_tensor(now_y(pair, m), ps_o[m][:], now_y(pair, m), ALU.add).then_inc(added.sem, 1)
                        dve.wait_ge(norm_ready.sem, norm_ready.at(i, 1))
                        nc.vector.tensor_tensor(centred[:], h_ff[:], spread(ps_g[:], C, 1), ALU.subtract).then_inc(centred_done.sem, 1)

                        def normalise():
                            dve.wait_ge(rstd_done.sem, rstd_done.at(i, 1))
                            nc.vector.tensor_tensor(normed[:], centred[:], spread(rstd[:], C, 1), ALU.mult).then_inc(normed_done.sem, 1)

                        if last:
                            normalise()
                        else:
                            front(i + 1, normalise)
                        dve.wait_ge(weights["feed_in"], l * (16 * FEED_LOADS) + 16 * FEED_LOADS)
                        for j in range(HC):
                            m = hrows(j)
                            dve.wait_ge(a_ready.sem, a_ready.at(i, j + 1))
                            dve.wait_ge(gelu_done.sem, gelu_done.at(i, j + 1))
                            nc.vector.scalar_tensor_tensor(hid[0:m, j, :], ps_s[j % 2][0:m, :], cols[0:m, 6 + j:7 + j],
                                                           gelu[j % 2][0:m, :], ALU.add, ALU.mult).then_inc(hid_done.sem, 1)
                        for m in range(C):
                            dve.wait_ge(ff_ready.sem, ff_ready.at(i, m + 1))
                            nc.vector.scalar_tensor_tensor(now_y(pair, m), ps_o[m][:], cols[:, 4 + m:5 + m], now_y(pair, m),
                                                           ALU.add, ALU.add).then_inc(grown.sem, 1)

                    dve.wait_ge(weights["attention_in"], l * 32 + 32)
                    for n in range(2):
                        nc.vector.tensor_scalar(turn[n][:], sh["mat"]("rotate"), scales[:, n:n + 1], None, ALU.mult).then_inc(turn_scaled, 1)
                    front(l * PAIRS)
                    with dve.Fori(0, PAIRS - 1) as pair:
                        body(pair, last=False)
                    body(PAIRS - 1, last=True)

    with ExitStack() as st:
        final = st.enter_context(nc.semaphore("e_final"))
        sent = st.enter_context(nc.semaphore("e_sent"))
        x_all, y_all = sh["x"], sh["y"]
        with nc.Block() as block:
            @block.vector
            def _(dve):
                for n in range(4):
                    part = (slice(None), slice(None), slice(n * W, (n + 1) * W))
                    nc.vector.scalar_tensor_tensor(x_all[part], y_all[part], sh["tanh"][:, 3:4], x_all[part],
                                                   ALU.mult, ALU.add).then_inc(final, 1)

            @block.sync
            def _(sp):
                for n in range(4):
                    sp.wait_ge(final, n + 1)
                    sp.dma_start(io["out"][:, :, n * W:(n + 1) * W], x_all[:, :, n * W:(n + 1) * W]).then_inc(sent, 16)
                sp.wait_ge(sent, 64)


def build(nc, io):
    with ExitStack() as st:
        def sb(name, shape, dt=F32):
            return st.enter_context(nc.sbuf_tensor(name, shape, dt))

        const = sb("const", [P, len(CONST), P])
        sh = {
            "const": const,
            "mat": lambda name: const[:, CONST[name], :],
            "small": sb("small_sb", [P, SMALL]),
            "tanh": sb("tanh_gates", [P, 4]),
            "slot": sb("slot_of_token", [P, NT], I32),
            "owner": sb("expert_of_tile", [P, SLOTS], I32),
            "sorted_x": nc.dram_tensor("sorted_x", [SLOTS * P, D], F32, kind="Internal").ap(),
            "sorted_y": nc.dram_tensor("sorted_y", [SLOTS * P, D], F32, kind="Internal").ap(),
            "x": sb("x_all", [P, C, T]),
            "eps": sb("eps_sb", [P, 1]),
        }
        with ExitStack() as early:
            sh["rows"] = early.enter_context(nc.sbuf_tensor("rows", [P, NT, D], F32))
            sh["logits"] = early.enter_context(nc.sbuf_tensor("logits", [P, NT, E], F32))
            attend_linear(nc, io, sh)
            route(nc, io, sh)
        experts(nc, io, sh)
        attend_heads(nc, io, sh)
        sh["y"] = sb("y_all", [P, C, T])
        sh["layer_weights"] = {
            "wqkv": sb("wqkv", [P, C, 3 * INNER]), "wo": sb("wo", [P, INNER // P, D]),
            "w1": sb("w1", [P, C, 2 * HID]), "w2": sb("w2", [P, HC, D]),
            "scales": sb("scales", [P, 2]),
            "cols": sb("cols", [P, 6 + 2 * HC]),
            "attention_in": st.enter_context(nc.semaphore("attention_weights_in")),
            "output_in": st.enter_context(nc.semaphore("output_weights_in")),
            "feed_in": st.enter_context(nc.semaphore("feed_weights_in")),
        }
        start_layers(nc, io, sh)
        local_layers(nc, io, sh)


def constants():
    import numpy as np

    p = np.arange(P)
    same16 = p[:, None] // D1 == p[None, :] // D1
    same64 = p[:, None] // D2 == p[None, :] // D2
    half = D2 // 2
    rotate = np.zeros((P, P), np.float32)
    for m in range(P):
        if m % D2 < half:
            rotate[m + half, m] = -1.0
        else:
            rotate[m - half, m] = 1.0
    mats = {
        "ident": np.eye(P), "mean256": np.full((P, P), 1.0 / D), "mean16": same16 / D1,
        "heads16": same16 / float(D1) ** 0.5, "before": p[:, None] < p[None, :], "ones": np.ones((P, P)),
        "rotate": rotate, "heads64": same64,
    }
    consts = np.stack([np.asarray(mats[n], np.float32) for n in CONST], axis=1)
    small = np.zeros((P, SMALL), np.float32)
    small[:, 0:E] = np.arange(E, 0, -1)
    small[:, E:E + NT] = P * np.arange(NT)
    small[:, E + NT:E + NT + SLOTS] = np.arange(SLOTS)

    f = np.float32
    half_idx = np.arange(0, D2, 2, dtype=f)
    inv_freq = f(1.0) / f(10000.0) ** (half_idx / f(D2))
    t = np.arange(S, dtype=f)
    freqs = t[:, None] * inv_freq[None, :]
    base = (half_idx + f(0.4 * D2)) / f(1.4 * D2)
    power = (t - f(S // 2)) / f(64.0)
    decay = base[None, :] ** power[:, None]
    wide = [np.tile(np.concatenate([a, a], axis=1).T, (P // D2, 1)) for a in (np.cos(freqs), np.sin(freqs), decay)]
    cos, sin, decay = wide
    rope = np.stack([cos * decay * f(8 * 256), sin * decay * f(8 * 256), cos / decay * f(256), sin / decay * f(256)],
                    axis=1).astype(f)

    q, k = np.arange(P)[:, None], np.arange(S)[None, :]
    first = np.where(k <= q, 0.0, -1e30)
    second = np.where((k <= q + P) & (k >= q), 0.0, -1e30)
    mask = np.concatenate([first, second], axis=1).astype(f)
    return {"consts": consts, "small": small, "rope": rope, "mask": mask}


def kernel(**inputs):
    import numpy as np
    import concourse.bacc as bacc
    from concourse.bass_utils import run_bass_kernel_spmd

    a = {k: np.asarray(v) for k, v in inputs.items()}

    def turned(x):
        return np.ascontiguousarray(x.reshape(T, C, P).transpose(2, 1, 0))

    def chunks(v):
        n = -(-v.shape[0] // P)
        out = np.zeros((n * P,), v.dtype)
        out[:v.shape[0]] = v
        return out.reshape(n, P).T

    def per_head(v):
        return np.tile(v, P // v.shape[0])[:, None]

    def layer_cols(l):
        b1 = a["L1_ffn_b1"][l]
        return np.concatenate([chunks(a["L1_ffn_ln_g"][l]), chunks(a["L1_ffn_ln_b"][l]), chunks(a["L1_ffn_b2"][l]),
                               chunks(b1[:HID]), chunks(b1[HID:])], axis=1)

    arrays = {
        "xT": turned(a["x"]), "ctxT": turned(a["ctx_1024"]),
        "L0_Wkv": np.concatenate([a["L0_xattn_Wk"].T, a["L0_xattn_Wv"].T], axis=1),
        "L0_Wq": a["L0_xattn_Wq"].T, "L0_Wo": a["L0_xattn_Wo"].T,
        "Wg": a["L0_ffn_Wg"], "bg": a["L0_ffn_bg"],
        "gates": np.tile(np.concatenate([a["g_xattn"][0:1], a["g_ffn"][0:1], a["g_xattn"][1:2], a["g_ffn"][1:2]])[None], (P, 1)),
        "W1": a["L0_ffn_W1"], "b1": a["L0_ffn_b1"].reshape(E, FC, P).transpose(0, 2, 1), "W2": a["L0_ffn_W2"],
        "b2": a["L0_ffn_b2"],
        "L1_Wq": a["L1_xattn_Wq"], "L1_Wkv": a["L1_xattn_Wkv"], "L1_Wp": a["L1_xattn_Wp"],
        "L1_cols": np.concatenate([chunks(a["L1_xattn_bp"]), per_head(a["L1_xattn_ln_g"]), per_head(a["L1_xattn_ln_b"])], axis=1),
        "F_wqkv": a["L1_ffn_wqkv"], "F_wo": a["L1_ffn_wo"], "F_w1": a["L1_ffn_w1"], "F_w2": a["L1_ffn_w2"],
        "F_scales": np.stack([np.concatenate([per_head(a["L1_ffn_q_scale"][l]), per_head(a["L1_ffn_k_scale"][l])], axis=1)
                              for l in range(DEPTH)]),
        "F_cols": np.stack([layer_cols(l) for l in range(DEPTH)]),
        **constants(),
    }
    arrays = {k: np.ascontiguousarray(v) for k, v in arrays.items()}
    nc = bacc.Bacc("TRN2", target_bir_lowering=False, num_devices=1)
    io = {k: nc.dram_tensor(k, v.shape, mybir.dt.from_np(v.dtype), kind="ExternalInput").ap() for k, v in arrays.items()}
    io["out"] = nc.dram_tensor("out", (P, C, T), F32, kind="ExternalOutput").ap()
    build(nc, io)
    r = run_bass_kernel_spmd(nc, [arrays], core_ids=[0])
    got = r.results[0]["out"]
    return np.ascontiguousarray(got.transpose(2, 1, 0)).reshape(B, S, D)
```

```python
from contextlib import ExitStack

import concourse.bass as bass
from concourse import mybir

ALU = mybir.AluOpType
LOG_EXP = "natural_log_exp_and_others"
ACT = mybir.ActivationFunctionType
AX = mybir.AxisListType
F32 = mybir.dt.float32
BF16 = mybir.dt.bfloat16
I32 = mybir.dt.int32

P = 128
B, S, D = 8, 256, 256
T = B * S
C = D // P
W = 2 * S
PAIRS = T // W
TT = W // P
NT = T // P
E, FF = 8, 1024
FC = FF // P
SLOTS = 24
UNROLL = 3
H1, D1 = 16, 16
H2, D2 = 8, 64
INNER = H2 * D2
DEPTH = 2
HID = int(D * 4 * 2 / 3)
HC = -(-HID // P)
HL = HID - (HC - 1) * P
EPS = 1e-5

CONST = {n: i for i, n in enumerate(
    ["ident", "mean256", "mean16", "heads16", "before", "ones", "heads64"])}
SMALL = 8 + 16 + SLOTS


class Signal:

    def __init__(self, stack, nc, name, per):
        self.sem = stack.enter_context(nc.semaphore(name))
        self.per = per

    def at(self, step, k):
        return step * self.per + (self.per + k)

    def before(self, step, k):
        return step * self.per + k


def start_ahead(engine, signals):
    for s in signals:
        engine.sem_inc(s.sem, s.per)


def spread(ap, n, at):
    shape = list(ap.shape)
    shape.insert(at, n)
    return ap.unsqueeze(at).to_broadcast(shape)


def attend_linear(nc, io, sh):
    with ExitStack() as st:
        def sb(name, shape, dt=F32):
            return st.enter_context(nc.sbuf_tensor("a_" + name, shape, dt))

        def pb(name):
            return st.enter_context(nc.psum_tensor("a_" + name, [P, 512], F32))

        def sig(name, per):
            return Signal(st, nc, "a_" + name, per)

        wkv, wq, wo = sb("wkv", [P, C, 2 * D]), sb("wq", [P, C, D]), sb("wo", [P, C, D])
        wg = sb("wg", [P, C, E])
        bg = sb("bg", [P, E])
        gin = sb("gin", [P, 4])
        ctx = sb("ctx", [P, C, W])
        centred, squares, normed = ([sb(f"{n}{i}", [P, C, W]) for i in range(2)] for n in ("centred", "squares", "normed"))
        log, rstd = ([sb(f"{n}{i}", [P, W]) for i in range(2)] for n in ("log", "rstd"))
        kv = sb("kv", [P, TT, 2 * D])
        ktv = sb("ktv", [P, 2 * C, P])
        qT = sb("qT", [P, C, W])
        aT = sb("aT", [P, C, W])
        zeros = sb("zeros", [P, D])

        ps_kv = [pb(f"ps_kv{i}") for i in range(2)]
        ps_ktv, ps_norm = pb("ps_ktv"), pb("ps_norm")
        ps_q = [pb(f"ps_q{i}") for i in range(2)]
        ps_o, ps_logit = pb("ps_o"), pb("ps_logit")
        ps_of = [ps_norm, ps_o]

        loaded = st.enter_context(nc.semaphore("a_loaded"))
        gates_in = st.enter_context(nc.semaphore("a_gates_in"))
        wkv_in = st.enter_context(nc.semaphore("a_wkv_in"))
        norm_in = st.enter_context(nc.semaphore("a_norm_in"))
        zeroed = st.enter_context(nc.semaphore("a_zeroed"))
        waited = st.enter_context(nc.semaphore("a_waited"))
        eps_set = st.enter_context(nc.semaphore("a_eps_set"))
        slots_zeroed = st.enter_context(nc.semaphore("a_slots_zeroed"))
        gates = st.enter_context(nc.semaphore("a_gates"))
        ctx_in = st.enter_context(nc.semaphore("a_ctx_in"))
        norm_ready = [sig(f"norm_ready{n}", 2) for n in range(2)]
        kv_ready = sig("kv_ready", TT)
        kv_copied = sig("kv_copied", TT)
        ktv_ready = sig("ktv_ready", 1)
        ktv_masked = sig("ktv_masked", 1)
        centred_done = [sig(f"centred_done{n}", 1) for n in range(2)]
        squared = [sig(f"squared{n}", 1) for n in range(2)]
        logged = [sig(f"logged{n}", 1) for n in range(2)]
        rstd_done = [sig(f"rstd_done{n}", 1) for n in range(2)]
        normed_done = [sig(f"normed_done{n}", 1) for n in range(2)]
        q_ready = sig("q_ready", 6)
        q_copied = sig("q_copied", 6)
        o_ready = sig("o_ready", C)
        added = sig("added", C)
        logit_ready = sig("logit_ready", 1)
        logit_done = sig("logit_done", 1)

        weights = [(wq, io["L0_Wq"]), (wo, io["L0_Wo"]), (wg, io["Wg"])]
        nloads = 16 * (len(weights) + 3)

        x_all = sh["x"]

        def now_x(i, c):
            return x_all[:, c, bass.ds(i * W, W)]

        with nc.Block() as block:
            @block.sync
            def _(sp):
                sp.dma_start(gin[:], io["gates"]).then_inc(gates_in, 16)
                sp.dma_start(wkv[:], io["L0_Wkv"].rearrange("(c p) n -> p c n", p=P)).then_inc(wkv_in, 16)
                sp.dma_start(ctx[:], io["ctxT"][:, :, 0:W]).then_inc(ctx_in, 16)
                sp.dma_start(sh["const"][:], io["consts"]).then_inc(norm_in, 16)
                sp.dma_start(x_all[:, :, 0:W], io["xT"][:, :, 0:W]).then_inc(norm_in, 16)
                for to, of in weights:
                    sp.dma_start(to[:], of.rearrange("(c p) n -> p c n", p=P)).then_inc(loaded, 16)
                sp.dma_start(x_all[:, :, W:T], io["xT"][:, :, W:T]).then_inc(loaded, 16)
                sp.dma_start(bg[:], spread(io["bg"], P, 0)).then_inc(loaded, 16)
                sp.dma_start(sh["small"][:], io["small"]).then_inc(loaded, 16)
                with sp.Fori(1, PAIRS) as i:
                    sp.wait_ge(kv_ready.sem, kv_ready.before(i, TT))
                    sp.dma_start(ctx[:], io["ctxT"][:, :, bass.ds(i * W, W)]).then_inc(ctx_in, 16)
                sp.wait_ge(zeroed, 1)
                sp.dma_start(sh["sorted_x"].rearrange("(n p) d -> p n d", p=P),
                             spread(zeros[:], SLOTS, 1)).then_inc(slots_zeroed, 16)
                sp.wait_ge(slots_zeroed, 16)

            @block.gpsimd
            def _(pool):
                nc.gpsimd.memset(sh["eps"][:], EPS).then_inc(eps_set, 1)
                nc.gpsimd.memset(zeros[:], 0.0).then_inc(zeroed, 1)

            @block.tensor
            def _(pe):
                start_ahead(pe, [*norm_ready, kv_ready, ktv_ready, q_ready, o_ready, logit_ready])
                mean256 = sh["mat"]("mean256")

                def mean(i, n):
                    if n == 0:
                        pe.wait_ge(logged[0].sem, logged[0].at(i, 0))
                    else:
                        pe.wait_ge(added.sem, added.at(i, C))
                    for c in range(C):
                        mm = nc.tensor.matmul(ps_of[n][:], mean256, now_x(i, c), start=(c == 0), stop=(c == C - 1))
                    mm.then_inc(norm_ready[n].sem, 1)

                def variance(i, n):
                    pe.wait_ge(squared[n].sem, squared[n].at(i, 1))
                    for c in range(C):
                        mm = nc.tensor.matmul(ps_of[n][:], mean256, squares[n][:, c, :], start=(c == 0), stop=(c == C - 1))
                    mm.then_inc(norm_ready[n].sem, 1)

                def keys_values(i, t):
                    if t == 0:
                        pe.wait_ge(ctx_in, i * 16 + 16)
                    pe.wait_ge(kv_copied.sem, kv_copied.at(i, t - 1))
                    for c in range(C):
                        mm = nc.tensor.matmul(ps_kv[t % 2][:], ctx[:, c, t * P:(t + 1) * P], wkv[:, c, :],
                                              start=(c == 0), stop=(c == C - 1))
                    mm.then_inc(kv_ready.sem, 1)

                def keys_times_values(i):
                    pe.wait_ge(kv_copied.sem, kv_copied.at(i, TT))
                    pe.wait_ge(ktv_masked.sem, ktv_masked.at(i, 0))
                    for b in range(2):
                        for c in range(C):
                            for t in range(2):
                                mm = nc.tensor.matmul(ps_ktv[:, (b * C + c) * P:(b * C + c + 1) * P],
                                                      kv[:, 2 * b + t, c * P:(c + 1) * P],
                                                      kv[:, 2 * b + t, D + c * P:D + (c + 1) * P],
                                                      start=(t == 0), stop=(t == 1))
                    mm.then_inc(ktv_ready.sem, 1)

                def body(i, last):
                    pe.wait_ge(normed_done[0].sem, normed_done[0].at(i, 1))
                    for m in range(C):
                        pe.wait_ge(q_copied.sem, q_copied.before(i, 5 + m))
                        for c in range(C):
                            mm = nc.tensor.matmul(ps_q[m][:], wq[:, c, m * P:(m + 1) * P], normed[0][:, c, :],
                                                  start=(c == 0), stop=(c == C - 1))
                        mm.then_inc(q_ready.sem, 1)
                    pe.wait_ge(ktv_masked.sem, ktv_masked.at(i, 1))
                    for c in range(C):
                        pe.wait_ge(q_copied.sem, q_copied.at(i, 1 + c))
                        for b in range(2):
                            mm = nc.tensor.matmul(ps_q[c][:, b * S:(b + 1) * S], ktv[:, b * C + c, :],
                                                  qT[:, c, b * S:(b + 1) * S], start=True, stop=True)
                        mm.then_inc(q_ready.sem, 1)
                    if not last:
                        mean(i + 1, 0)
                    pe.wait_ge(q_copied.sem, q_copied.at(i, 4))
                    for m in range(C):
                        if m == 0:
                            pe.wait_ge(logged[1].sem, logged[1].at(i, 0))
                        else:
                            pe.wait_ge(added.sem, added.at(i, m))
                        for c in range(C):
                            mm = nc.tensor.matmul(ps_o[:], wo[:, c, m * P:(m + 1) * P], aT[:, c, :],
                                                  start=(c == 0), stop=(c == C - 1))
                        mm.then_inc(o_ready.sem, 1)
                        if m == 0 and not last:
                            keys_values(i + 1, 0)
                    if not last:
                        keys_values(i + 1, 1)
                    mean(i, 1)
                    if not last:
                        variance(i + 1, 0)
                        keys_values(i + 1, 2)
                    variance(i, 1)
                    if not last:
                        keys_values(i + 1, 3)
                        keys_times_values(i + 1)
                    pe.wait_ge(normed_done[1].sem, normed_done[1].at(i, 1))
                    pe.wait_ge(logit_done.sem, logit_done.before(i, 1))
                    for t in range(TT):
                        for c in range(C):
                            mm = nc.tensor.matmul(ps_logit[:, t * E:(t + 1) * E], normed[1][:, c, t * P:(t + 1) * P],
                                                  wg[:, c, :], start=(c == 0), stop=(c == C - 1))
                    mm.then_inc(logit_ready.sem, 1)
                    for h in range(2):
                        for t in range(2):
                            for c in range(C):
                                mm = nc.tensor.transpose(ps_q[h][:, (t * C + c) * P:(t * C + c + 1) * P],
                                                         normed[1][:, c, (2 * h + t) * P:(2 * h + t + 1) * P],
                                                         sh["mat"]("ident"))
                        mm.then_inc(q_ready.sem, 1)

                pe.wait_ge(wkv_in, 16)
                keys_values(0, 0)
                pe.wait_ge(norm_in, 32)
                mean(0, 0)
                for t in range(1, TT):
                    keys_values(0, t)
                variance(0, 0)
                keys_times_values(0)
                pe.wait_ge(loaded, nloads)
                with pe.Fori(0, PAIRS - 1) as i:
                    body(i, last=False)
                body(PAIRS - 1, last=True)

            @block.scalar
            def _(act):
                start_ahead(act, [kv_copied, *squared, q_copied, *logged, *rstd_done])
                act.wait_ge(gates_in, 16)
                act.wait_ge(eps_set, 1)
                nc.scalar.activation(sh["tanh"][:], gin[:], ACT.Tanh).then_inc(gates, 1)
                nc.scalar.preload_act_table_set(LOG_EXP)

                def square(i, n):
                    act.wait_ge(centred_done[n].sem, centred_done[n].at(i, 1))
                    nc.scalar.activation(squares[n][:], centred[n][:], ACT.Square).then_inc(squared[n].sem, 1)

                def deviate(i, n):
                    act.wait_ge(norm_ready[n].sem, norm_ready[n].at(i, 2))
                    nc.scalar.activation(log[n][:], ps_of[n][:], ACT.Ln, bias=sh["eps"][:]).then_inc(logged[n].sem, 1)
                    act.wait_ge(logged[n].sem, logged[n].at(i, 1))
                    nc.scalar.activation(rstd[n][:], log[n][:], ACT.Exp, scale=-0.5).then_inc(rstd_done[n].sem, 1)

                def keys_values(i, t):
                    act.wait_ge(kv_ready.sem, kv_ready.at(i, t + 1))
                    if t == 0:
                        act.wait_ge(ktv_ready.sem, ktv_ready.at(i, 0))
                    nc.scalar.copy(kv[:, t, :], ps_kv[t % 2][:]).then_inc(kv_copied.sem, 1)

                def body(i, last):
                    for c in range(C):
                        act.wait_ge(q_ready.sem, q_ready.at(i, 1 + c))
                        nc.scalar.copy(qT[:, c, :], ps_q[c][:]).then_inc(q_copied.sem, 1)
                    for c in range(C):
                        act.wait_ge(q_ready.sem, q_ready.at(i, 3 + c))
                        nc.scalar.copy(aT[:, c, :], ps_q[c][:]).then_inc(q_copied.sem, 1)
                    if not last:
                        square(i + 1, 0)
                        keys_values(i + 1, 0)
                        keys_values(i + 1, 1)
                    square(i, 1)
                    if not last:
                        deviate(i + 1, 0)
                        keys_values(i + 1, 2)
                    deviate(i, 1)
                    if not last:
                        keys_values(i + 1, 3)
                    for h in range(2):
                        act.wait_ge(q_ready.sem, q_ready.at(i, 5 + h))
                        act.sem_inc(waited, 1)
                        nc.scalar.copy(sh["rows"][:, bass.ds(i * TT + 2 * h, 2), :],
                                       ps_q[h][:].rearrange("p (t n) -> p t n", t=2)).then_inc(q_copied.sem, 1)

                keys_values(0, 0)
                square(0, 0)
                for t in range(1, TT):
                    keys_values(0, t)
                deviate(0, 0)
                with act.Fori(0, PAIRS - 1) as i:
                    body(i, last=False)
                body(PAIRS - 1, last=True)

            @block.vector
            def _(dve):
                start_ahead(dve, [ktv_masked, *centred_done, *normed_done, added, logit_done])
                dve.wait_ge(gates, 1)

                def centre(i, n):
                    dve.wait_ge(norm_ready[n].sem, norm_ready[n].at(i, 1))
                    if n:
                        dve.wait_ge(added.sem, added.at(i, C))
                    nc.vector.tensor_tensor(centred[n][:], x_all[:, :, bass.ds(i * W, W)],
                                            spread(ps_of[n][:], C, 1), ALU.subtract).then_inc(centred_done[n].sem, 1)

                def normalise(i, n):
                    dve.wait_ge(rstd_done[n].sem, rstd_done[n].at(i, 1))
                    dve.wait_ge(q_ready.sem, q_ready.before(i, 6 if n else 2))
                    nc.vector.tensor_tensor(normed[n][:], centred[n][:], spread(rstd[n][:], C, 1),
                                            ALU.mult).then_inc(normed_done[n].sem, 1)

                def mask_heads(i):
                    dve.wait_ge(ktv_ready.sem, ktv_ready.at(i, 1))
                    nc.vector.tensor_tensor(ktv[:], ps_ktv[:].rearrange("p (n m) -> p n m", m=P),
                                            spread(sh["mat"]("heads16"), 2 * C, 1), ALU.mult).then_inc(ktv_masked.sem, 1)

                def body(i, last):
                    if not last:
                        centre(i + 1, 0)
                    for m in range(C):
                        dve.wait_ge(o_ready.sem, o_ready.at(i, m + 1))
                        nc.vector.scalar_tensor_tensor(now_x(i, m), ps_o[:], sh["tanh"][:, 0:1], now_x(i, m),
                                                       ALU.mult, ALU.add).then_inc(added.sem, 1)
                    centre(i, 1)
                    if not last:
                        normalise(i + 1, 0)
                    normalise(i, 1)
                    if not last:
                        mask_heads(i + 1)
                    dve.wait_ge(logit_ready.sem, logit_ready.at(i, 1))
                    nc.vector.tensor_tensor(sh["logits"][:, bass.ds(i * TT, TT), :],
                                            ps_logit[:, 0:TT * E].rearrange("p (t e) -> p t e", e=E),
                                            spread(bg[:], TT, 1), ALU.add).then_inc(logit_done.sem, 1)

                centre(0, 0)
                normalise(0, 0)
                mask_heads(0)
                dve.wait_ge(loaded, nloads)
                with dve.Fori(0, PAIRS - 1) as i:
                    body(i, last=False)
                body(PAIRS - 1, last=True)


def route(nc, io, sh):
    with ExitStack() as st:
        def sb(name, shape, dt=F32):
            return st.enter_context(nc.sbuf_tensor("r_" + name, shape, dt))

        best = sb("best", [P, NT])
        tied = sb("tied", [P, NT, E])
        rank = sb("rank", [P, NT])
        chosen = sb("chosen", [P, NT, E])
        total = sb("total", [P, NT, E])
        ahead = sb("ahead", [P, NT + 1, E])
        full = sb("full", [P, E, NT])
        tiles = sb("tiles", [P, E])
        first = sb("first", [P, E + 1])
        base = sb("base", [P, E])
        place = sb("place", [P, NT, E])
        slot = sb("slot", [P, NT])
        begun = sb("begun", [P, SLOTS, E - 1])
        owner = sb("owner", [P, SLOTS])
        ps_before = st.enter_context(nc.psum_tensor("r_ps_before", [P, 512], F32))
        ps_total = st.enter_context(nc.psum_tensor("r_ps_total", [P, 512], F32))
        chain = st.enter_context(nc.semaphore("r_chain"))
        counted = st.enter_context(nc.semaphore("r_counted"))
        picked = st.enter_context(nc.semaphore("r_picked"))
        small = sh["small"]
        order, steps, numbers = small[:, 0:E], small[:, E:E + NT], small[:, E + NT:E + NT + SLOTS]

        with nc.Block() as block:
            @block.vector
            def _(dve):
                made = [0]

                def then(op):
                    made[0] += 1
                    op.then_inc(chain, 1)
                    dve.wait_ge(chain, made[0])

                logits = sh["logits"]
                then(nc.vector.tensor_reduce(best[:], logits[:], AX.X, ALU.max))
                then(nc.vector.tensor_tensor(tied[:], logits[:], spread(best[:], E, 2), ALU.is_ge))
                then(nc.vector.tensor_tensor(tied[:], tied[:], spread(order, NT, 1), ALU.mult))
                then(nc.vector.tensor_reduce(rank[:], tied[:], AX.X, ALU.max))
                nc.vector.tensor_tensor(chosen[:], tied[:], spread(rank[:], E, 2), ALU.is_equal).then_inc(picked, 1)
                nc.vector.memset(ahead[:, 0, :], 0.0)
                nc.vector.memset(first[:, 0:1], 0.0)
                dve.wait_ge(counted, 1)
                then(nc.vector.tensor_copy(total[:], ps_total[:, 0:NT * E].rearrange("p (t e) -> p t e", e=E)))
                for t in range(NT):
                    then(nc.vector.tensor_tensor(ahead[:, t + 1, :], ahead[:, t, :], total[:, t, :], ALU.add))
                then(nc.vector.tensor_tensor(full[:], spread(ahead[:, NT, :], NT, 2), spread(steps, E, 1), ALU.is_gt))
                then(nc.vector.tensor_reduce(tiles[:], full[:], AX.X, ALU.add))
                for e in range(E):
                    then(nc.vector.tensor_tensor(first[:, e + 1:e + 2], first[:, e:e + 1], tiles[:, e:e + 1], ALU.add))
                then(nc.vector.tensor_scalar(base[:], first[:, 0:E], float(P), None, ALU.mult))
                then(nc.vector.tensor_tensor(place[:], ps_before[:, 0:NT * E].rearrange("p (t e) -> p t e", e=E),
                                             ahead[:, 0:NT, :], ALU.add))
                then(nc.vector.tensor_tensor(place[:], place[:], spread(base[:], NT, 1), ALU.add))
                then(nc.vector.tensor_tensor(place[:], place[:], chosen[:], ALU.mult))
                then(nc.vector.tensor_reduce(slot[:], place[:], AX.X, ALU.add))
                then(nc.vector.tensor_copy(sh["slot"][:], slot[:]))
                then(nc.vector.tensor_tensor(begun[:], spread(numbers, E - 1, 2), spread(first[:, 1:E], SLOTS, 1),
                                             ALU.is_ge))
                then(nc.vector.tensor_reduce(owner[:], begun[:], AX.X, ALU.add))
                then(nc.vector.tensor_copy(sh["owner"][:], owner[:]))

            @block.tensor
            def _(pe):
                pe.wait_ge(picked, 1)
                rhs = chosen[:].rearrange("p t e -> p (t e)")
                nc.tensor.matmul(ps_before[:, 0:NT * E], sh["mat"]("before"), rhs, start=True, stop=True)
                nc.tensor.matmul(ps_total[:, 0:NT * E], sh["mat"]("ones"), rhs, start=True, stop=True).then_inc(counted, 1)


def experts(nc, io, sh):
    with ExitStack() as st:
        def sb(name, shape, dt=F32):
            return st.enter_context(nc.sbuf_tensor("m_" + name, shape, dt))

        def pb(name):
            return st.enter_context(nc.psum_tensor("m_" + name, [P, 512], F32))

        def sem(name):
            return st.enter_context(nc.semaphore("m_" + name))

        U = UNROLL
        w1 = [sb(f"w1_{u}", [P, C, FF]) for u in range(U)]
        w2 = [sb(f"w2_{u}", [P, FC, D]) for u in range(U)]
        b1 = [sb(f"b1_{u}", [P, FC]) for u in range(U)]
        b2 = [sb(f"b2_{u}", [P, D]) for u in range(U)]
        xr = [sb(f"xr_{u}", [P, D]) for u in range(U)]
        xt = [sb(f"xt_{u}", [P, C, P]) for u in range(U)]
        hid = [sb(f"hid_{u}", [P, FC, P]) for u in range(U)]
        y = [sb(f"y_{u}", [P, D]) for u in range(U)]
        NH = 4
        ps_h = [pb(f"ps_h{i}") for i in range(NH)]
        ps_y = [pb(f"ps_y{i}") for i in range(U)]

        rows_in, weights_in = [sem(f"rows_in{u}") for u in range(U)], [sem(f"weights_in{u}") for u in range(U)]
        scattered, stored = sem("scattered"), [sem(f"stored{u}") for u in range(U)]
        turned = Signal(st, nc, "m_turned", U)
        turned_copied = Signal(st, nc, "m_turned_copied", U)
        hid_ready = Signal(st, nc, "m_hid_ready", U * FC)
        gelu_done = Signal(st, nc, "m_gelu_done", U * FC)
        y_ready = Signal(st, nc, "m_y_ready", U)
        y_done = Signal(st, nc, "m_y_done", U)

        with nc.Block() as block:
            @block.sync
            def _(sp):
                def load_rows(i):
                    for u in range(U):
                        sp.wait_ge(turned.sem, turned.before(i, u + 1))
                        sp.dma_start(xr[u][:], sh["sorted_x"][bass.ds((i * U + u) * P, P), :]).then_inc(rows_in[u], 16)

                def load_weights(i, tiles=range(U)):
                    for u in tiles:
                        e = sp.value_load(sh["owner"][0:1, bass.ds(i * U + u, 1)], min_val=0, max_val=E - 1)
                        sp.wait_ge(y_ready.sem, y_ready.before(i, u + 1))
                        sp.dma_start(w1[u][:], io["W1"][bass.ds(e, 1), :, :].rearrange("e (c p) n -> p (e c) n", p=P)).then_inc(weights_in[u], 16)
                        sp.dma_start(b1[u][:], io["b1"][bass.ds(e, 1), :, :].rearrange("e p c -> p (e c)")).then_inc(weights_in[u], 16)
                        sp.dma_start(w2[u][:], io["W2"][bass.ds(e, 1), :, :].rearrange("e (c p) n -> p (e c) n", p=P)).then_inc(weights_in[u], 16)
                        sp.wait_ge(y_done.sem, y_done.before(i, u + 1))
                        sp.dma_start(b2[u][:], io["b2"][bass.ds(e, 1), :].to_broadcast([P, D])).then_inc(weights_in[u], 16)
                load_weights(0, [0, 1])
                sp.wait_ge(scattered, 16 * NT)
                load_rows(0)
                load_weights(0, [2])
                with sp.Fori(1, SLOTS // U) as i:
                    load_rows(i)
                    load_weights(i)
                ahead = sh["head_weights"]
                for to, of in [(ahead["wq"], io["L1_Wq"]), (ahead["wkv"], io["L1_Wkv"]), (ahead["wp"], io["L1_Wp"])]:
                    sp.dma_start(to[:], of.rearrange("(c p) n -> p c n", p=P)).then_inc(ahead["in"], 16)
                sp.dma_start(ahead["cols"][:], io["L1_cols"]).then_inc(ahead["in"], 16)

            @block.gpsimd
            def _(pool):
                for t in range(NT):
                    nc.gpsimd.indirect_dma_start(
                        sh["sorted_x"], bass.IndirectOffsetOnAxis(ap=sh["slot"][:, t:t + 1], axis=0),
                        sh["rows"][:, t, :], None).then_inc(scattered, 16)
                pool.wait_ge(scattered, 16 * NT)
                with pool.Fori(0, SLOTS // U) as i:
                    for u in range(U):
                        pool.wait_ge(y_done.sem, y_done.at(i, u + 1))
                        pool.dma_start(sh["sorted_y"][bass.ds((i * U + u) * P, P), :], y[u][:]).then_inc(stored[u], 16)
                for u in range(U):
                    pool.wait_ge(stored[u], 16 * (SLOTS // U))

            @block.tensor
            def _(pe):
                start_ahead(pe, [turned, hid_ready, y_ready])
                with pe.Fori(0, SLOTS // U) as i:
                    for u in range(U):
                        pe.wait_ge(rows_in[u], i * 16 + 16)
                        pe.wait_ge(y_done.sem, y_done.at(i, u + 1 - U))
                        for c in range(C):
                            mm = nc.tensor.transpose(ps_y[u][:, c * P:(c + 1) * P], xr[u][:, c * P:(c + 1) * P], sh["mat"]("ident"))
                        mm.then_inc(turned.sem, 1)

                    def hidden(u):
                        pe.wait_ge(turned_copied.sem, turned_copied.at(i, u + 1))
                        pe.wait_ge(weights_in[u], i * 64 + 64)
                        for m in range(FC):
                            k = u * FC + m
                            pe.wait_ge(gelu_done.sem, gelu_done.at(i, k + 1 - NH))
                            for c in range(C):
                                mm = nc.tensor.matmul(ps_h[m % NH][:, 0:P], w1[u][:, c, m * P:(m + 1) * P], xt[u][:, c, :],
                                                      start=(c == 0), stop=(c == C - 1))
                            mm.then_inc(hid_ready.sem, 1)

                    def values(u):
                        for m in range(FC):
                            pe.wait_ge(gelu_done.sem, gelu_done.at(i, u * FC + m + 1))
                            mm = nc.tensor.matmul(ps_y[u][:, 0:D], hid[u][:, m, :], w2[u][:, m, :],
                                                  start=(m == 0), stop=(m == FC - 1))
                        mm.then_inc(y_ready.sem, 1)

                    hidden(0)
                    for u in range(1, U):
                        hidden(u)
                        values(u - 1)
                    values(U - 1)

            @block.scalar
            def _(act):
                start_ahead(act, [gelu_done])
                with act.Fori(0, SLOTS // U) as i:
                    for u in range(U):
                        act.wait_ge(weights_in[u], i * 64 + 64)
                        for m in range(FC):
                            act.wait_ge(hid_ready.sem, hid_ready.at(i, u * FC + m + 1))
                            if m == 0:
                                act.wait_ge(y_ready.sem, y_ready.at(i, u + 1 - U))
                            nc.scalar.activation(hid[u][:, m, :], ps_h[m % NH][:, 0:P], ACT.Gelu,
                                                 bias=b1[u][:, m:m + 1]).then_inc(gelu_done.sem, 1)

            @block.vector
            def _(dve):
                start_ahead(dve, [turned_copied, y_done])
                with dve.Fori(0, SLOTS // U) as i:
                    for u in range(U):
                        dve.wait_ge(turned.sem, turned.at(i, u + 1))
                        dve.wait_ge(hid_ready.sem, hid_ready.before(i, (u + 1) * FC))
                        nc.vector.tensor_copy(xt[u][:], ps_y[u][:, 0:D].rearrange("p (c t) -> p c t", c=C)).then_inc(turned_copied.sem, 1)
                    for u in range(U):
                        dve.wait_ge(y_ready.sem, y_ready.at(i, u + 1))
                        dve.wait_ge(weights_in[u], i * 64 + 64)
                        dve.wait_ge(stored[u], i * 16)
                        nc.vector.tensor_tensor(y[u][:], ps_y[u][:, 0:D], b2[u][:], ALU.add).then_inc(y_done.sem, 1)


def attend_heads(nc, io, sh):
    with ExitStack() as st:
        def sb(name, shape, dt=F32):
            return st.enter_context(nc.sbuf_tensor("h_" + name, shape, dt))

        def pb(name):
            return st.enter_context(nc.psum_tensor("h_" + name, [P, 512], F32))

        def sig(name, per):
            return Signal(st, nc, "h_" + name, per)

        G = 2 * D1
        HC1 = P // D1
        UNITS = 2 * C
        STEPS = UNITS * HC1
        BATCH = HC1 // 2
        RING = 2 * BATCH
        PROBS = 5
        LAG_T, LAG_V = 3, 5

        wq, wkv, wp, cols = (sh["head_weights"][n] for n in ("wq", "wkv", "wp", "cols"))
        loaded = sh["head_weights"]["in"]
        q_scale, k_scale = sb("q_scale", [P, 2]), sb("k_scale", [P, HC1, 2])
        bias = sb("bias", [P, C])
        sums = sb("sums", [P, C, H1])
        ctx = sb("ctx", [P, C, W])
        taken = sb("taken", [P, TT, D])
        index = sb("index", [P, TT], I32)
        centred, squares = sb("centred", [P, C, W]), sb("squares", [P, C, W])
        log, rstd, normed = sb("log", [P, W]), sb("rstd", [P, W]), sb("normed", [P, C, W])
        sq = [sb(f"sq{i}", [P, W]) for i in range(4)]
        hrstd = [sb(f"hrstd{i}", [P, W]) for i in range(4)]
        hn = [sb(f"hn{i}", [P, W]) for i in range(4)]
        qT = sb("qT", [P, C, W])
        kT = sb("kT", [P, C, HC1, W])
        V = sb("V", [P, TT, H1 // 2, 2, G])
        peak = sb("peak", [P, 3, 2])
        prob = [sb(f"prob{i}", [P, 2, S]) for i in range(PROBS)]
        probT = [sb(f"probT{i}", [P, 2, S]) for i in range(RING)]
        exp_sum, rsum = sb("exp_sum", [P, PROBS, 2]), sb("rsum", [P, PROBS, 2])
        oT = sb("oT", [P, C, W])

        ps_s = [pb(f"ps_s{i}") for i in range(3)]
        ps_t = [pb(f"ps_t{i}") for i in range(2)]
        ps_o = [pb(f"ps_o{i}") for i in range(2)]
        ps_g = pb("ps_g")
        ps_proj, ps_var, ps_out = [ps_s[0], ps_s[1], *ps_t], [ps_g, ps_s[2], *ps_o], [ps_g, ps_s[2]]

        prepared = st.enter_context(nc.semaphore("h_prepared"))
        ctx_in = st.enter_context(nc.semaphore("h_ctx_in"))
        rows_in = st.enter_context(nc.semaphore("h_rows_in"))
        waited = st.enter_context(nc.semaphore("h_waited"))
        index_done = st.enter_context(nc.semaphore("h_index_done"))
        y_turned = sig("y_turned", C)
        y_added = sig("y_added", C)
        norm_ready = sig("norm_ready", 2)
        centred_done = sig("centred_done", 1)
        squared = sig("squared", 1)
        logged = sig("logged", 1)
        rstd_done = sig("rstd_done", 1)
        normed_done = sig("normed_done", 1)
        v_ready = sig("v_ready", 2)
        v_copied = sig("v_copied", 2)
        proj_ready = sig("proj_ready", 4)
        head_squared = sig("head_squared", 4)
        head_var = sig("head_var", 4)
        head_logged = sig("head_logged", 4)
        head_rstd = sig("head_rstd", 4)
        head_normed = sig("head_normed", 4)
        head_out = sig("head_out", 2 * HC1 + 2)
        s_ready = sig("s_ready", STEPS)
        peaked = sig("peaked", STEPS)
        exp_done = sig("exp_done", 2 * STEPS)
        inverted = sig("inverted", STEPS)
        prob_done = sig("prob_done", STEPS)
        t_ready = sig("t_ready", STEPS)
        t_copied = sig("t_copied", STEPS)
        pv_ready = sig("pv_ready", STEPS // BATCH)
        o_done = sig("o_done", UNITS)
        out_ready = sig("out_ready", C)
        added = sig("added", C)

        NORM_AT = [11, 14, 17, 21]

        x_all = sh["x"]

        def now_x(i, c):
            return x_all[:, c, bass.ds(i * W, W)]

        def unit(s):
            return s // HC1 // 2, s // HC1 % 2

        def head_of(s):
            return 2 * (s % BATCH) + s % HC1 // BATCH

        with nc.Block() as block:
            @block.sync
            def _(sp):
                with sp.Fori(0, PAIRS) as i:
                    sp.wait_ge(proj_ready.sem, proj_ready.before(i, 3))
                    sp.dma_start(ctx[:], io["ctxT"][:, :, bass.ds(i * W, W)]).then_inc(ctx_in, 16)

            @block.gpsimd
            def _(pool):
                start_ahead(pool, [prob_done])

                def find_rows(i):
                    pool.wait_ge(y_turned.sem, y_turned.at(i, 0))
                    pool.wait_ge(rows_in, i * (16 * TT))
                    nc.gpsimd.tensor_copy(index[:], sh["slot"][:, bass.ds(i * TT, TT)]).then_inc(index_done, 1)
                    pool.wait_ge(index_done, i + 1)
                    pool.sem_inc(waited, 1)

                def gather(t):
                    nc.gpsimd.indirect_dma_start(
                        taken[:, t, :], None, sh["sorted_y"],
                        bass.IndirectOffsetOnAxis(ap=index[:, t:t + 1], axis=0)).then_inc(rows_in, 16)

                def body(i, last):
                    for s in range(STEPS):
                        pool.wait_ge(inverted.sem, inverted.at(i, s + 1))
                        nc.gpsimd.tensor_tensor(prob[s % PROBS][:], prob[s % PROBS][:],
                                                spread(rsum[:, s % PROBS, :], S, 2), ALU.mult).then_inc(prob_done.sem, 1)
                        if not last and s == 0:
                            find_rows(i + 1)
                        if not last and s % 2 == 0 and s < 2 * TT:
                            gather(s // 2)

                find_rows(0)
                for t in range(TT):
                    gather(t)
                with pool.Fori(0, PAIRS - 1) as i:
                    body(i, last=False)
                body(PAIRS - 1, last=True)

            @block.tensor
            def _(pe):
                start_ahead(pe, [y_turned, norm_ready, v_ready, proj_ready, head_var, s_ready, t_ready, pv_ready,
                                 out_ready])
                pe.wait_ge(loaded, 64)
                mean256, mean16, ident = sh["mat"]("mean256"), sh["mat"]("mean16"), sh["mat"]("ident")

                def rows_turned(i, c):
                    for t in range(TT):
                        mm = nc.tensor.transpose(ps_g[:, t * P:(t + 1) * P], taken[:, t, c * P:(c + 1) * P], ident)
                    mm.then_inc(y_turned.sem, 1)

                def mean_of(i, of):
                    for c in range(C):
                        mm = nc.tensor.matmul(ps_g[:], mean256, of(c), start=(c == 0), stop=(c == C - 1))
                    mm.then_inc(norm_ready.sem, 1)

                def norm(i, n):
                    if n == 0:
                        pe.wait_ge(head_logged.sem, head_logged.at(i, -3))
                        pe.wait_ge(rows_in, i * (16 * TT) + 16 * TT)
                        rows_turned(i, 0)
                    elif n == 1:
                        pe.wait_ge(y_added.sem, y_added.at(i, 1))
                        rows_turned(i, 1)
                    elif n == 2:
                        pe.wait_ge(y_added.sem, y_added.at(i, 2))
                        mean_of(i, lambda c: now_x(i, c))
                    else:
                        pe.wait_ge(squared.sem, squared.at(i, 1))
                        mean_of(i, lambda c: squares[:, c, :])

                def front(i, between):
                    pe.wait_ge(ctx_in, i * 16 + 16)
                    for g in range(2):
                        for t in range(2):
                            for c in range(C):
                                mm = nc.tensor.matmul(ps_t[g][:, t * D:(t + 1) * D],
                                                      ctx[:, c, (2 * g + t) * P:(2 * g + t + 1) * P], wkv[:, c, D:2 * D],
                                                      start=(c == 0), stop=(c == C - 1))
                        mm.then_inc(v_ready.sem, 1)
                    between()

                    def project(g):
                        if g >= 2:
                            pe.wait_ge(v_copied.sem, v_copied.at(i, g - 1))
                        if g == 1:
                            pe.wait_ge(normed_done.sem, normed_done.at(i, 1))
                        for c in range(C):
                            w, of = (wq, normed) if g % 2 else (wkv, ctx)
                            mm = nc.tensor.matmul(ps_proj[g][:], w[:, c, (g // 2) * P:(g // 2 + 1) * P], of[:, c, :],
                                                  start=(c == 0), stop=(c == C - 1))
                        mm.then_inc(proj_ready.sem, 1)

                    def head_variance(g):
                        pe.wait_ge(head_squared.sem, head_squared.at(i, g + 1))
                        if g < 2:
                            pe.wait_ge(added.sem, added.at(i, g + 1 - C))
                        nc.tensor.matmul(ps_var[g][:], mean16, sq[g][:], start=True, stop=True).then_inc(head_var.sem, 1)

                    project(0)
                    project(1)
                    head_variance(0)
                    project(2)
                    head_variance(1)
                    project(3)
                    head_variance(2)
                    head_variance(3)

                def body(i, last):
                    def tick(s):
                        if s < STEPS:
                            c, b = unit(s)
                            if s < HC1:
                                pe.wait_ge(head_out.sem, head_out.at(i, s + 2))
                            if s == 2 * HC1:
                                pe.wait_ge(head_out.sem, head_out.at(i, 2 * HC1 + 2))
                            pe.wait_ge(exp_done.sem, exp_done.at(i, 2 * (s - 2)))
                            for u in range(2):
                                mm = nc.tensor.matmul(ps_s[s % 3][:, u * S:(u + 1) * S],
                                                      qT[:, c, b * S + u * P:b * S + (u + 1) * P],
                                                      kT[:, c, head_of(s), b * S:(b + 1) * S],
                                                      start=True, stop=True)
                            mm.then_inc(s_ready.sem, 1)
                        if LAG_T <= s < STEPS + LAG_T:
                            n = s - LAG_T
                            if n < 2:
                                pe.wait_ge(head_normed.sem, head_normed.at(i, n + 3))
                            else:
                                pe.wait_ge(t_copied.sem, t_copied.at(i, n - 1))
                            pe.wait_ge(prob_done.sem, prob_done.at(i, n + 1))
                            for k in range(2):
                                for u in range(2):
                                    mm = nc.tensor.transpose(ps_t[n % 2][:, k * S + u * P:k * S + (u + 1) * P],
                                                             prob[n % PROBS][:, u, k * P:(k + 1) * P], ident)
                            mm.then_inc(t_ready.sem, 1)
                        if s >= LAG_V and (s - LAG_V) % BATCH == BATCH - 1:
                            n = s - LAG_V - (BATCH - 1)
                            c, b = unit(n)
                            odd, bank = n % HC1 // BATCH, ps_o[n // HC1 % 2]
                            if not odd:
                                pe.wait_ge(o_done.sem, o_done.at(i, n // HC1 - 1))
                            pe.wait_ge(t_copied.sem, t_copied.at(i, n + BATCH))
                            for k in range(2):
                                for j in range(BATCH):
                                    mm = nc.tensor.matmul(bank[G * j:G * (j + 1), 0:S], V[:, 2 * b + k, BATCH * c + j, odd, :],
                                                          probT[(n + j) % RING][:, k, :],
                                                          start=(odd == 0 and k == 0), stop=(odd == 1 and k == 1))
                            mm.then_inc(pv_ready.sem, 1)

                        if not last and s in NORM_AT:
                            norm(i + 1, NORM_AT.index(s))

                    for s in range(STEPS + LAG_V):
                        tick(s)

                    def output():
                        pe.wait_ge(o_done.sem, o_done.at(i, UNITS))
                        if not last:
                            pe.wait_ge(logged.sem, logged.at(i + 1, 1))
                        for m in range(C):
                            for c in range(C):
                                mm = nc.tensor.matmul(ps_out[m][:], wp[:, c, m * P:(m + 1) * P], oT[:, c, :],
                                                      start=(c == 0), stop=(c == C - 1))
                            mm.then_inc(out_ready.sem, 1)

                    if last:
                        output()
                    else:
                        front(i + 1, output)

                for n in range(3):
                    norm(0, n)

                def rest():
                    norm(0, 3)
                    pe.wait_ge(prepared, 1)

                front(0, rest)
                with pe.Fori(0, PAIRS - 1) as i:
                    body(i, last=False)
                body(PAIRS - 1, last=True)

            @block.scalar
            def _(act):
                start_ahead(act, [squared, v_copied, head_squared, head_out, exp_done, logged, rstd_done,
                                  head_logged, head_rstd])
                nc.scalar.preload_act_table_set(LOG_EXP)

                def norm_squares(i):
                    act.wait_ge(centred_done.sem, centred_done.at(i, 1))
                    nc.scalar.activation(squares[:], centred[:], ACT.Square).then_inc(squared.sem, 1)

                def norm_deviation(i):
                    act.wait_ge(norm_ready.sem, norm_ready.at(i, 2))
                    nc.scalar.activation(log[:], ps_g[:], ACT.Ln, bias=sh["eps"][:]).then_inc(logged.sem, 1)
                    act.wait_ge(logged.sem, logged.at(i, 1))
                    nc.scalar.activation(rstd[:], log[:], ACT.Exp, scale=-0.5).then_inc(rstd_done.sem, 1)

                def scale_shift(i, out, g, by):
                    act.wait_ge(head_normed.sem, head_normed.at(i, g + 1))
                    nc.scalar.activation(out, hn[g][:], ACT.Identity, scale=by[:, 0:1],
                                         bias=by[:, 1:2]).then_inc(head_out.sem, 1)

                def k_head(i, c, n):
                    h = head_of(n)
                    scale_shift(i, kT[:, c, h, :], 2 * c, k_scale[:, h, :])

                def deviate(i, g):
                    act.wait_ge(head_var.sem, head_var.at(i, g + 1))
                    nc.scalar.activation(hrstd[g][:], ps_var[g][:], ACT.Ln, bias=sh["eps"][:]).then_inc(head_logged.sem, 1)
                    act.wait_ge(head_logged.sem, head_logged.at(i, g + 1))
                    nc.scalar.activation(hrstd[g][:], hrstd[g][:], ACT.Exp, scale=-0.5).then_inc(head_rstd.sem, 1)

                def front(i):
                    for g in range(2):
                        act.wait_ge(v_ready.sem, v_ready.at(i, g + 1))
                        heads = ps_t[g][:].rearrange("p (t h e d) -> p t h e d", t=2, e=2, d=D1)
                        nc.scalar.copy(V[:, 2 * g:2 * g + 2, :, 0, 0:D1], heads[:, :, :, 0, :])
                        nc.scalar.copy(V[:, 2 * g:2 * g + 2, :, 1, D1:G], heads[:, :, :, 1, :]).then_inc(v_copied.sem, 1)

                    def square(g):
                        act.wait_ge(proj_ready.sem, proj_ready.at(i, g + 1))
                        nc.scalar.activation(sq[g][:], ps_proj[g][:], ACT.Square).then_inc(head_squared.sem, 1)

                    square(0)
                    square(1)
                    deviate(i, 0)
                    square(2)
                    deviate(i, 1)
                    k_head(i, 0, 0)
                    square(3)
                    scale_shift(i, qT[:, 0, :], 1, q_scale)
                    deviate(i, 2)
                    k_head(i, 0, 1)
                    k_head(i, 0, 2)

                def body(i, last):
                    def tick(s):
                        if s < STEPS:
                            act.wait_ge(peaked.sem, peaked.at(i, s + 1))
                            act.wait_ge(t_ready.sem, t_ready.at(i, s - PROBS + 1))
                            for h in range(2):
                                nc.scalar.activation(prob[s % PROBS][:, h, :], ps_s[s % 3][:, h * S:(h + 1) * S], ACT.Exp,
                                                     bias=peak[:, s % 3, h:h + 1],
                                                     accum_out=exp_sum[:, s % PROBS, h:h + 1]).then_inc(exp_done.sem, 1)
                        if s == 0:
                            deviate(i, 3)
                        if s < HC1 - 3:
                            k_head(i, 0, s + 3)
                        elif s == HC1 - 3:
                            scale_shift(i, qT[:, 1, :], 3, q_scale)
                        elif s < 2 * HC1 - 2:
                            k_head(i, 1, s - (HC1 - 2))
                        if not last and s == NORM_AT[2] + 2:
                            norm_squares(i + 1)
                        if not last and s == NORM_AT[3] + 2:
                            norm_deviation(i + 1)

                    for s in range(STEPS + LAG_V):
                        tick(s)
                    if not last:
                        front(i + 1)

                norm_squares(0)
                norm_deviation(0)
                act.wait_ge(prepared, 1)
                front(0)
                with act.Fori(0, PAIRS - 1) as i:
                    body(i, last=False)
                body(PAIRS - 1, last=True)

            @block.vector
            def _(dve):
                start_ahead(dve, [y_added, centred_done, normed_done, head_normed, peaked,
                                  t_copied, inverted, o_done, added])
                tanh = sh["tanh"]

                def norm(i, n):
                    if n < 2:
                        dve.wait_ge(y_turned.sem, y_turned.at(i, n + 1))
                        nc.vector.scalar_tensor_tensor(now_x(i, n), ps_g[:], tanh[:, 1:2], now_x(i, n),
                                                       ALU.mult, ALU.add).then_inc(y_added.sem, 1)
                    elif n == 2:
                        dve.wait_ge(norm_ready.sem, norm_ready.at(i, 1))
                        nc.vector.tensor_tensor(centred[:], x_all[:, :, bass.ds(i * W, W)], spread(ps_g[:], C, 1),
                                                ALU.subtract).then_inc(centred_done.sem, 1)
                    else:
                        dve.wait_ge(rstd_done.sem, rstd_done.at(i, 1))
                        nc.vector.tensor_tensor(normed[:], centred[:], spread(rstd[:], C, 1), ALU.mult).then_inc(normed_done.sem, 1)

                def head_norm(i, g):
                    dve.wait_ge(head_rstd.sem, head_rstd.at(i, g + 1))
                    if g == 0:
                        dve.wait_ge(head_out.sem, head_out.at(i, 0))
                    nc.vector.tensor_tensor(hn[g][:], ps_proj[g][:], hrstd[g][:], ALU.mult).then_inc(head_normed.sem, 1)

                def front(i):
                    for g in range(3):
                        head_norm(i, g)

                def body(i, last):
                    def tick(s):
                        if s == 1:
                            head_norm(i, 3)
                        if s < STEPS:
                            dve.wait_ge(s_ready.sem, s_ready.at(i, s + 1))
                            nc.vector.tensor_reduce(peak[:, s % 3, :], ps_s[s % 3][:].rearrange("p (h k) -> p h k", h=2),
                                                    AX.X, ALU.max, negate=True).then_inc(peaked.sem, 1)
                        if 1 <= s <= STEPS:
                            n = s - 1
                            dve.wait_ge(exp_done.sem, exp_done.at(i, 2 * n + 2))
                            dve.wait_ge(prob_done.sem, prob_done.at(i, n - PROBS + 1))
                            nc.vector.reciprocal(rsum[:, n % PROBS, :], exp_sum[:, n % PROBS, :]).then_inc(inverted.sem, 1)
                        if LAG_T <= s < STEPS + LAG_T:
                            n = s - LAG_T
                            dve.wait_ge(t_ready.sem, t_ready.at(i, n + 1))
                            dve.wait_ge(pv_ready.sem, pv_ready.at(i, n // BATCH - 1))
                            nc.vector.tensor_copy(probT[n % RING][:].rearrange("p k q -> p (k q)"), ps_t[n % 2][:]).then_inc(t_copied.sem, 1)
                        if s > LAG_V and (s - LAG_V) % HC1 == HC1 - 1:
                            u = (s - LAG_V) // HC1
                            c, b = unit(u * HC1)
                            dve.wait_ge(pv_ready.sem, pv_ready.at(i, 2 * (u + 1)))
                            nc.vector.tensor_copy(oT[:, c, b * S:(b + 1) * S], ps_o[u % 2][:, 0:S]).then_inc(o_done.sem, 1)
                        if not last and s - 1 in NORM_AT[:3]:
                            norm(i + 1, NORM_AT.index(s - 1))
                        if not last and s == NORM_AT[3] + 3:
                            norm(i + 1, 3)

                    for s in range(STEPS + LAG_V):
                        tick(s)
                    for m in range(C):
                        dve.wait_ge(out_ready.sem, out_ready.at(i, m + 1))
                        nc.vector.scalar_tensor_tensor(now_x(i, m), ps_out[m][:], bias[:, m:m + 1], now_x(i, m),
                                                       ALU.add, ALU.add).then_inc(added.sem, 1)
                    if not last:
                        front(i + 1)

                for n in range(3):
                    norm(0, n)
                nc.vector.memset(V[:], 0.0)
                chain = st.enter_context(nc.semaphore("h_chain"))
                made = [0]

                def then(op):
                    made[0] += 1
                    op.then_inc(chain, 1)
                    dve.wait_ge(chain, made[0])

                dve.wait_ge(loaded, 64)
                for w in (wq[:], wkv[:, :, 0:D]):
                    heads = w.rearrange("p c (h d) -> p c h d", d=D1)
                    then(nc.vector.tensor_reduce(sums[:], heads, AX.X, ALU.add))
                    then(nc.vector.tensor_scalar(sums[:], sums[:], 1.0 / D1, None, ALU.mult))
                    then(nc.vector.tensor_tensor(heads, heads, spread(sums[:], D1, 3), ALU.subtract))
                then(nc.vector.tensor_scalar(q_scale[:], cols[:, 2:4], float(D1) ** 0.5, None, ALU.mult))
                of_head = sh["mat"]("mean16")[:, ::D1]
                then(nc.vector.scalar_tensor_tensor(k_scale[:], spread(of_head, 2, 2), float(D1), spread(cols[:, 2:4], HC1, 1),
                                                    ALU.mult, ALU.mult))
                then(nc.vector.tensor_scalar(bias[:], cols[:, 0:2], tanh[:, 2:3], None, ALU.mult))
                nc.vector.tensor_scalar(wp[:], wp[:], tanh[:, 2:3], None, ALU.mult).then_inc(prepared, 1)
                norm(0, 3)
                front(0)
                with dve.Fori(0, PAIRS - 1) as i:
                    body(i, last=False)
                body(PAIRS - 1, last=True)


FEED_LOADS = 4


def load_attention_weights(engine, io, weights, one):
    engine.dma_start(weights["wqkv"][:], io["F_wqkv"][one].rearrange("l (c p) n -> p (l c) n", p=P)).then_inc(weights["attention_in"], 16)
    engine.dma_start(weights["scales"][:], io["F_scales"][one].rearrange("l p n -> p (l n)")).then_inc(weights["attention_in"], 16)


def load_output_weights(engine, io, weights, one):
    engine.dma_start(weights["wo"][:], io["F_wo"][one].rearrange("l (c p) n -> p (l c) n", p=P)).then_inc(weights["output_in"], 16)


def load_feed_weights(engine, io, weights, one):
    full = HID - HL
    for to, of in [(weights["cols"][:], io["F_cols"][one].rearrange("l p n -> p (l n)")),
                   (weights["w1"][:], io["F_w1"][one].rearrange("l (c p) n -> p (l c) n", p=P)),
                   (weights["w2"][:, 0:HC - 1, :], io["F_w2"][one, 0:full, :].rearrange("l (c p) n -> p (l c) n", p=P)),
                   (weights["w2"][0:HL, HC - 1, :], io["F_w2"][one, full:HID, :].rearrange("l p n -> p (l n)"))]:
        engine.dma_start(to, of).then_inc(weights["feed_in"], 16)


def start_layers(nc, io, sh):
    with ExitStack() as st:
        def sig(name):
            return Signal(st, nc, "y_" + name, 2)

        centred, squares = ([st.enter_context(nc.sbuf_tensor(f"y_{n}{i}", [P, C, W], F32)) for i in range(2)]
                            for n in ("centred", "squares"))
        log, rstd = ([st.enter_context(nc.sbuf_tensor(f"y_{n}{i}", [P, W], F32)) for i in range(2)] for n in ("log", "rstd"))
        ps_mean, ps_var = ([st.enter_context(nc.psum_tensor(f"y_ps_{n}{i}", [P, W], F32)) for i in range(2)]
                           for n in ("mean", "var"))
        mean_ready, var_ready = sig("mean_ready"), sig("var_ready")
        centred_done, y_done = sig("centred_done"), sig("y_done")
        squared, logged, rstd_done = sig("squared"), sig("logged"), sig("rstd_done")
        x_all, y_all = sh["x"], sh["y"]

        def tokens(i, n):
            return bass.ds((2 * i + n) * W, W)

        with nc.Block() as block:
            @block.sync
            def _(sp):
                for load in (load_attention_weights, load_output_weights, load_feed_weights):
                    load(sp, io, sh["layer_weights"], slice(0, 1))

            @block.tensor
            def _(pe):
                start_ahead(pe, [mean_ready, var_ready])
                mean256 = sh["mat"]("mean256")
                with pe.Fori(0, PAIRS // 2) as i:
                    for n in range(2):
                        pe.wait_ge(centred_done.sem, centred_done.at(i, n - 1))
                        for c in range(C):
                            mm = nc.tensor.matmul(ps_mean[n][:], mean256, x_all[:, c, tokens(i, n)], start=(c == 0), stop=(c == C - 1))
                        mm.then_inc(mean_ready.sem, 1)
                    for n in range(2):
                        pe.wait_ge(squared.sem, squared.at(i, n + 1))
                        for c in range(C):
                            mm = nc.tensor.matmul(ps_var[n][:], mean256, squares[n][:, c, :], start=(c == 0), stop=(c == C - 1))
                        mm.then_inc(var_ready.sem, 1)

            @block.vector
            def _(dve):
                start_ahead(dve, [centred_done, y_done])
                with dve.Fori(0, PAIRS // 2) as i:
                    for n in range(2):
                        dve.wait_ge(mean_ready.sem, mean_ready.at(i, n + 1))
                        dve.wait_ge(y_done.sem, y_done.at(i, n - 1))
                        nc.vector.tensor_tensor(centred[n][:], x_all[:, :, tokens(i, n)], spread(ps_mean[n][:], C, 1),
                                                ALU.subtract).then_inc(centred_done.sem, 1)
                    for n in range(2):
                        dve.wait_ge(rstd_done.sem, rstd_done.at(i, n + 1))
                        nc.vector.tensor_tensor(y_all[:, :, tokens(i, n)], centred[n][:], spread(rstd[n][:], C, 1),
                                                ALU.mult).then_inc(y_done.sem, 1)

            @block.scalar
            def _(act):
                start_ahead(act, [squared, logged, rstd_done])
                with act.Fori(0, PAIRS // 2) as i:
                    for n in range(2):
                        act.wait_ge(centred_done.sem, centred_done.at(i, n + 1))
                        nc.scalar.activation(squares[n][:], centred[n][:], ACT.Square).then_inc(squared.sem, 1)
                    for n in range(2):
                        act.wait_ge(var_ready.sem, var_ready.at(i, n + 1))
                        nc.scalar.activation(log[n][:], ps_var[n][:], ACT.Ln, bias=sh["eps"][:]).then_inc(logged.sem, 1)
                        act.wait_ge(logged.sem, logged.at(i, n + 1))
                        nc.scalar.activation(rstd[n][:], log[n][:], ACT.Exp, scale=-0.5).then_inc(rstd_done.sem, 1)


def local_layers(nc, io, sh):
    with ExitStack() as st:
        def sb(name, shape, dt=F32):
            return st.enter_context(nc.sbuf_tensor("l_" + name, shape, dt))

        def pb(name):
            return st.enter_context(nc.psum_tensor("l_" + name, [P, 512], F32))

        def sem(name):
            return st.enter_context(nc.semaphore("l_" + name))

        def sig(name, per):
            return Signal(st, nc, "l_" + name, per)

        QC = INNER // P
        STEPS = 2 * H2
        LAG_T, LAG_V = 3, 6
        PROBS = 4
        TURN = 16 * 4
        RING = 6
        PW = 3 * P

        weights = sh["layer_weights"]
        wqkv, scales, wo, w1, w2, cols = (weights[n] for n in ("wqkv", "scales", "wo", "w1", "w2", "cols"))
        tables = sb("tables", [P, 4, S])
        mask16 = sb("mask16", [P, PW], BF16)
        ident16 = sb("ident16", [P, P], BF16)
        hT, h_ff = sb("hT", [P, C, W]), sb("h_ff", [P, C, W])
        centred, squares = sb("centred", [P, C, W]), sb("squares", [P, C, W])
        log, rstd, normed, h2 = sb("log", [P, W]), sb("rstd", [P, W]), sb("normed", [P, C, W]), sb("h2", [P, C, W])
        V = sb("V", [P, TT, INNER])
        raw, turned, sq, fl, rn, ta, tb, tc = (
            [sb(f"{n}{i}", [P, W]) for i in range(2)] for n in ("raw", "turned", "sq", "fl", "rn", "ta", "tb", "tc"))
        qT = sb("qT", [P, QC, W])
        kT = [sb(f"kT{i}", [P, QC, W]) for i in range(2)]
        peak = sb("peak", [P, 3, 2])
        prob = [sb(f"prob{i}", [P, PW]) for i in range(PROBS)]
        probT = [sb(f"probT{i}", [P, PW]) for i in range(RING)]
        sums, rsum = sb("sums", [P, PROBS, 2]), sb("rsum", [P, PROBS, 2])
        oT = sb("oT", [P, QC, W])
        gelu = [sb(f"gelu{i}", [P, W]) for i in range(2)]
        hid = sb("hid", [P, HC, W])

        ps_s = [pb(f"ps_s{i}") for i in range(3)]
        ps_t = [pb(f"ps_t{i}") for i in range(2)]
        ps_o = [pb(f"ps_o{i}") for i in range(2)]
        ps_g = pb("ps_g")

        tables_in = sem("tables_in")
        zeroed, mask_done = sem("zeroed"), sem("mask_done")
        waited, turn_due = sem("waited"), sem("turn_due")
        shifted = sig("shifted", 1)
        shifted_ff = sig("shifted_ff", 1)
        v_ready = sig("v_ready", TT)
        v_copied = sig("v_copied", TT)
        proj_ready = sig("proj_ready", 2 * QC)
        raw_done = sig("raw_done", 2 * QC)
        sq_done = sig("sq_done", 2 * QC)
        length_ready = sig("length_ready", 2 * QC)
        turned_in = [sig(f"turned_in{i}", QC * TURN) for i in range(2)]
        floored = sig("floored", 2 * QC)
        ln_done = sig("ln_done", 2 * QC)
        rn_done = sig("rn_done", 2 * QC)
        cos_done = sig("cos_done", 2 * QC)
        sin_done = sig("sin_done", 2 * QC)
        rope_sum = sig("rope_sum", QC)
        k_sum = sig("k_sum", QC)
        rope_even = sig("rope_even", QC)
        rope_done = sig("rope_done", 2 * QC)
        s_ready = sig("s_ready", STEPS)
        peaked = sig("peaked", STEPS)
        exp_done = sig("exp_done", 2 * STEPS)
        inverted = sig("inverted", STEPS)
        prob_done = sig("prob_done", STEPS)
        t_ready = sig("t_ready", STEPS)
        t_even = sig("t_even", STEPS // 2)
        t_odd = sig("t_odd", STEPS // 2)
        pv_ready = sig("pv_ready", STEPS // 2)
        o_done = sig("o_done", STEPS // 2)
        out_ready = sig("out_ready", C)
        added = sig("added", C)
        norm_ready = sig("norm_ready", 2)
        centred_done = sig("centred_done", 1)
        squared = sig("squared", 1)
        logged = sig("logged", 1)
        rstd_done = sig("rstd_done", 1)
        normed_done = sig("normed_done", 1)
        h2_done = sig("h2_done", C)
        g_ready = sig("g_ready", HC)
        a_ready = sig("a_ready", HC)
        gelu_done = sig("gelu_done", HC)
        hid_done = sig("hid_done", HC)
        ff_ready = sig("ff_ready", C)
        grown = sig("grown", C)

        x_all, y_all = sh["x"], sh["y"]

        def hrows(j):
            return P if j < HC - 1 else HL

        def now_y(i, c):
            return y_all[:, c, bass.ds(i * W, W)]

        def two(ap):
            return ap.rearrange("p (b t) -> p b t", b=2)

        def v_bank(t):
            return ps_s[(STEPS + t) % 3]

        def t_copied(n, step):
            s = t_odd if n % 2 else t_even
            return s.sem, s.at(step, n // 2 + 1)

        with nc.Block() as block:
            @block.sync
            def _(sp):
                sp.dma_start(tables[:], io["rope"]).then_inc(tables_in, 16)
                sp.dma_start(squares[:, 0, 0:PW], io["mask"]).then_inc(tables_in, 16)
                start_ahead(sp, turned_in)
                half = D2 // 2

                def turn(i):
                    for g in range(2 * QC):
                        sp.wait_ge(raw_done.sem, raw_done.at(i, g + 1))
                        sp.sem_inc(turn_due, 1)
                        sp.wait_ge(sin_done.sem, sin_done.at(i, g - 1))
                        for to in range(0, P, half):
                            of = to + half if to % D2 == 0 else to - half
                            sp.dma_start(turned[g % 2][to:to + half, :], raw[g % 2][of:of + half, :]).then_inc(turned_in[g % 2].sem, 16)

                for l in range(DEPTH):
                    first = l * PAIRS
                    if l:
                        sp.wait_ge(raw_done.sem, raw_done.at(first, 0))
                        load_attention_weights(sp, io, weights, slice(l, l + 1))
                        sp.wait_ge(out_ready.sem, out_ready.at(first, 0))
                        load_output_weights(sp, io, weights, slice(l, l + 1))
                    turn(first)
                    if l:
                        sp.wait_ge(grown.sem, grown.at(first, 0))
                        load_feed_weights(sp, io, weights, slice(l, l + 1))
                    with sp.Fori(first + 1, first + PAIRS) as i:
                        turn(i)

            @block.tensor
            def _(pe):
                start_ahead(pe, [v_ready, proj_ready, length_ready, s_ready, t_ready, pv_ready,
                                 out_ready, norm_ready, g_ready, a_ready, ff_ready])
                mean256, heads64, ident = sh["mat"]("mean256"), sh["mat"]("heads64"), sh["mat"]("ident")
                for l in range(DEPTH):
                    def front_v(i, t):
                        if t == 0:
                            pe.wait_ge(shifted.sem, shifted.at(i, 1))
                        pe.wait_ge(v_copied.sem, v_copied.at(i, t - 2))
                        for c in range(C):
                            mm = nc.tensor.matmul(v_bank(t)[:], hT[:, c, t * P:(t + 1) * P], wqkv[:, c, 2 * INNER:],
                                                  start=(c == 0), stop=(c == C - 1))
                        mm.then_inc(v_ready.sem, 1)

                    def length(i, g, o_free=None):
                        pe.wait_ge(sq_done.sem, sq_done.at(i, g + 1))
                        if g < 2:
                            pe.wait_ge(*o_free)
                        else:
                            pe.wait_ge(floored.sem, floored.at(i, g - 1))
                        nc.tensor.matmul(ps_o[g % 2][:], heads64, sq[g % 2][:], start=True, stop=True).then_inc(length_ready.sem, 1)

                    def front_qk(i, o_free, between={}):
                        for g in range(2 * QC):
                            pe.wait_ge(sq_done.sem, sq_done.at(i, g - 1))
                            for c in range(C):
                                mm = nc.tensor.matmul(ps_t[g % 2][:], wqkv[:, c, g * P:(g + 1) * P], hT[:, c, :],
                                                      start=(c == 0), stop=(c == C - 1))
                            mm.then_inc(proj_ready.sem, 1)
                            if g:
                                length(i, g - 1, o_free)
                            if g in between:
                                between[g]()

                    def body(pair, after):
                        i, last = l * PAIRS + pair, after is None
                        pe.wait_ge(rope_done.sem, rope_done.at(i, 2 * QC))

                        def tick(s):
                            if s < STEPS:
                                b, h = s // H2, s % H2
                                c = h // 2
                                pe.wait_ge(exp_done.sem, exp_done.at(i, 2 * (s - 2)))
                                bank = ps_s[s % 3]
                                nc.tensor.matmul(bank[:, 0:PW], ident16[:], mask16[:], start=True, stop=False, skip_group_check=True)
                                for w in range(2):
                                    n = (w + 1) * P
                                    mm = nc.tensor.matmul(bank[:, w * P:w * P + n],
                                                          qT[:, c, b * S + w * P:b * S + (w + 1) * P],
                                                          kT[h % 2][:, c, b * S:b * S + n],
                                                          start=False, stop=True, skip_group_check=True)
                                mm.then_inc(s_ready.sem, 1)
                            if LAG_T <= s < STEPS + LAG_T:
                                n = s - LAG_T
                                if n < 2:
                                    pe.wait_ge(sq_done.sem, sq_done.at(i, 2 * QC))
                                else:
                                    pe.wait_ge(*t_copied(n - 2, i))
                                pe.wait_ge(prob_done.sem, prob_done.at(i, n + 1))
                                for k in range(3):
                                    mm = nc.tensor.transpose(ps_t[n % 2][:, k * P:(k + 1) * P], prob[n % PROBS][:, k * P:(k + 1) * P], ident)
                                mm.then_inc(t_ready.sem, 1)
                            if s > LAG_V and (s - LAG_V) % 2:
                                n = s - LAG_V - 1
                                b, h, bank = n // H2, n % H2, ps_o[n // 2 % 2]
                                pe.wait_ge(o_done.sem, o_done.at(i, n // 2 - 1))
                                pe.wait_ge(*t_copied(n, i))
                                pe.wait_ge(*t_copied(n + 1, i))
                                for k in range(2):
                                    for j in range(2):
                                        mm = nc.tensor.matmul(bank[j * D2:(j + 1) * D2, k * P:S],
                                                              V[:, 2 * b + k, (h + j) * D2:(h + j + 1) * D2],
                                                              probT[(n + j) % RING][:, k * S:S + k * P],
                                                              start=(k == 0), stop=(k == 1))
                                mm.then_inc(pv_ready.sem, 1)

                        for s in range(STEPS + LAG_V + 1):
                            if not last and s - STEPS in (0, 1):
                                if s == STEPS and after == "layer":
                                    pe.wait_ge(weights["attention_in"], 32 * (l + 2))
                                pe.wait_ge(exp_done.sem, exp_done.at(i, 2 * (s - 2)))
                                front_v(i + 1, s - STEPS)
                            tick(s)
                        if not last:
                            pe.wait_ge(exp_done.sem, exp_done.at(i, 2 * STEPS))
                            front_v(i + 1, 2)
                        pe.wait_ge(o_done.sem, o_done.at(i, STEPS // 2))
                        pe.wait_ge(weights["output_in"], l * 16 + 16)
                        for m in range(C):
                            for c in range(QC):
                                mm = nc.tensor.matmul(ps_o[m][:], wo[:, c, m * P:(m + 1) * P], oT[:, c, :],
                                                      start=(c == 0), stop=(c == QC - 1))
                            mm.then_inc(out_ready.sem, 1)
                        if not last:
                            front_v(i + 1, TT - 1)

                        def norm_mean():
                            pe.wait_ge(shifted_ff.sem, shifted_ff.at(i, 1))
                            for c in range(C):
                                mm = nc.tensor.matmul(ps_g[:], mean256, h_ff[:, c, :], start=(c == 0), stop=(c == C - 1))
                            mm.then_inc(norm_ready.sem, 1)

                        def norm_variance():
                            pe.wait_ge(squared.sem, squared.at(i, 1))
                            for c in range(C):
                                mm = nc.tensor.matmul(ps_g[:], mean256, squares[:, c, :], start=(c == 0), stop=(c == C - 1))
                            mm.then_inc(norm_ready.sem, 1)

                        if last:
                            norm_mean()
                            norm_variance()
                        else:
                            front_qk(i + 1, (added.sem, added.at(i, C)), {0: norm_mean, 1: norm_variance})
                            pe.wait_ge(sq_done.sem, sq_done.at(i + 1, 2 * QC - 1))
                            pe.wait_ge(v_copied.sem, v_copied.at(i + 1, TT))
                        pe.wait_ge(weights["feed_in"], l * (16 * FEED_LOADS) + 16 * FEED_LOADS)
                        pe.wait_ge(h2_done.sem, h2_done.at(i, C))
                        for j in range(HC):
                            m = hrows(j)
                            pe.wait_ge(gelu_done.sem, gelu_done.at(i, j - 1))
                            for c in range(C):
                                mm = nc.tensor.matmul(ps_t[j % 2][0:m, :], w1[:, c, HID + j * P:HID + j * P + m], h2[:, c, :],
                                                      start=(c == 0), stop=(c == C - 1))
                            mm.then_inc(g_ready.sem, 1)
                            if j == 0 and not last:
                                length(i + 1, 2 * QC - 1)
                            pe.wait_ge(hid_done.sem, hid_done.at(i, j - 1))
                            for c in range(C):
                                mm = nc.tensor.matmul(ps_s[j % 2][0:m, :], w1[:, c, j * P:j * P + m], h2[:, c, :],
                                                      start=(c == 0), stop=(c == C - 1))
                            mm.then_inc(a_ready.sem, 1)
                        if not last:
                            pe.wait_ge(floored.sem, floored.at(i + 1, 2 * QC))
                        for m in range(C):
                            for j in range(HC):
                                n = hrows(j)
                                if m == 0:
                                    pe.wait_ge(hid_done.sem, hid_done.at(i, j + 1))
                                mm = nc.tensor.matmul(ps_o[m][:], w2[0:n, j, m * P:(m + 1) * P], hid[0:n, j, :],
                                                      start=(j == 0), stop=(j == HC - 1))
                            mm.then_inc(ff_ready.sem, 1)

                    if l == 0:
                        pe.wait_ge(weights["attention_in"], 32)
                        for t in range(TT):
                            front_v(0, t)
                        front_qk(0, (grown.sem, grown.at(0, 0)))
                        length(0, 2 * QC - 1)
                        pe.wait_ge(mask_done, 1)
                    with pe.Fori(0, PAIRS - 1) as pair:
                        body(pair, "pair")
                    body(PAIRS - 1, "layer" if l < DEPTH - 1 else None)

            @block.scalar
            def _(act):
                start_ahead(act, [shifted, shifted_ff, v_copied, raw_done, sq_done, exp_done, t_odd, squared, h2_done,
                                  gelu_done, ln_done, rn_done, logged, rstd_done])
                act.wait_ge(zeroed, 1)
                for l in range(DEPTH):
                    def shift(to, pair, signal):
                        act.sem_inc(waited, 1)
                        nc.scalar.copy(to[:, 0, :], now_y(pair, 0))
                        late = two(to[:, 1, :])[:, :, 1:S]
                        nc.scalar.copy(late, two(now_y(pair, 1))[:, :, 0:S - 1]).then_inc(signal.sem, 1)

                    def front_v(i, t):
                        act.wait_ge(v_ready.sem, v_ready.at(i, t + 1))
                        nc.scalar.copy(V[:, t, :], v_bank(t)[:]).then_inc(v_copied.sem, 1)

                    def length(i, g):
                        act.wait_ge(floored.sem, floored.at(i, g + 1))
                        nc.scalar.activation(fl[g % 2][:], fl[g % 2][:], ACT.Ln).then_inc(ln_done.sem, 1)
                        act.wait_ge(ln_done.sem, ln_done.at(i, g + 1))
                        act.wait_ge(rope_done.sem, rope_done.at(i, g - 1))
                        nc.scalar.activation(rn[g % 2][:], fl[g % 2][:], ACT.Exp, scale=-0.5).then_inc(rn_done.sem, 1)

                    def front_qk(i, between={}):
                        for g in range(2 * QC):
                            act.wait_ge(proj_ready.sem, proj_ready.at(i, g + 1))
                            act.wait_ge(turned_in[g % 2].sem, turned_in[g % 2].at(i, g // 2 * TURN))
                            act.wait_ge(cos_done.sem, cos_done.at(i, g - 1))
                            nc.scalar.activation(raw[g % 2][:], ps_t[g % 2][:], ACT.Identity,
                                                 scale=scales[:, g // QC:g // QC + 1]).then_inc(raw_done.sem, 1)
                            act.wait_ge(length_ready.sem, length_ready.at(i, g - 1))
                            nc.scalar.activation(sq[g % 2][:], ps_t[g % 2][:], ACT.Square).then_inc(sq_done.sem, 1)
                            if g:
                                length(i, g - 1)
                            if g in between:
                                between[g]()
                        length(i, 2 * QC - 1)

                    def body(pair, after):
                        i, last = l * PAIRS + pair, after is None
                        nc.scalar.preload_act_table_set(LOG_EXP)
                        if not last:
                            act.wait_ge(proj_ready.sem, proj_ready.at(i, 2 * QC))
                            shift(hT, pair + 1 if after == "pair" else 0, shifted)

                        def tick(s):
                            if s < STEPS:
                                act.wait_ge(peaked.sem, peaked.at(i, s + 1))
                                act.wait_ge(t_ready.sem, t_ready.at(i, s - PROBS + 1))
                                for w in range(2):
                                    n = (w + 1) * P
                                    nc.scalar.activation(prob[s % PROBS][:, w * P:w * P + n], ps_s[s % 3][:, w * P:w * P + n],
                                                         ACT.Exp, bias=peak[:, s % 3, w:w + 1],
                                                         accum_out=sums[:, s % PROBS, w:w + 1]).then_inc(exp_done.sem, 1)
                            n = s - LAG_T
                            if 0 <= n < STEPS and n % 2:
                                act.wait_ge(t_ready.sem, t_ready.at(i, n + 1))
                                act.wait_ge(pv_ready.sem, pv_ready.at(i, (n - RING) // 2 + 1))
                                nc.scalar.copy(probT[n % RING][:], ps_t[1][:, 0:PW]).then_inc(t_odd.sem, 1)

                        for s in range(STEPS + LAG_V + 1):
                            tick(s)
                        if not last:
                            act.wait_ge(pv_ready.sem, pv_ready.at(i, STEPS // 2))
                            for t in range(TT - 1):
                                front_v(i + 1, t)
                        act.wait_ge(added.sem, added.at(i, C))
                        shift(h_ff, pair, shifted_ff)
                        if after == "layer":
                            act.wait_ge(weights["attention_in"], 32 * (l + 2))
                        if not last:
                            front_v(i + 1, TT - 1)

                        def norm_squares():
                            act.wait_ge(centred_done.sem, centred_done.at(i, 1))
                            nc.scalar.activation(squares[:], centred[:], ACT.Square).then_inc(squared.sem, 1)

                        def norm_deviation():
                            act.wait_ge(norm_ready.sem, norm_ready.at(i, 2))
                            nc.scalar.activation(log[:], ps_g[:], ACT.Ln, bias=sh["eps"][:]).then_inc(logged.sem, 1)
                            act.wait_ge(logged.sem, logged.at(i, 1))
                            nc.scalar.activation(rstd[:], log[:], ACT.Exp, scale=-0.5).then_inc(rstd_done.sem, 1)

                        def norm_scale(c):
                            act.wait_ge(weights["feed_in"], l * (16 * FEED_LOADS) + 16 * FEED_LOADS)
                            act.wait_ge(normed_done.sem, normed_done.at(i, 1))
                            nc.scalar.activation(h2[:, c, :], normed[:, c, :], ACT.Identity, scale=cols[:, c:c + 1],
                                                 bias=cols[:, 2 + c:3 + c]).then_inc(h2_done.sem, 1)

                        if last:
                            norm_squares()
                            norm_deviation()
                            for c in range(C):
                                norm_scale(c)
                        else:
                            front_qk(i + 1, {0: norm_squares, 1: norm_deviation, 3: lambda: norm_scale(0), 5: lambda: norm_scale(1)})
                        for j in range(HC):
                            m = hrows(j)
                            act.wait_ge(g_ready.sem, g_ready.at(i, j + 1))
                            act.wait_ge(hid_done.sem, hid_done.at(i, j - 1))
                            nc.scalar.activation(gelu[j % 2][0:m, :], ps_t[j % 2][0:m, :], ACT.Gelu,
                                                 bias=cols[0:m, 6 + HC + j:7 + HC + j]).then_inc(gelu_done.sem, 1)

                    if l == 0:
                        nc.scalar.preload_act_table_set(LOG_EXP)
                        shift(hT, 0, shifted)
                        act.wait_ge(weights["attention_in"], 32)
                        for t in range(TT):
                            front_v(0, t)
                        front_qk(0)
                    with act.Fori(0, PAIRS - 1) as pair:
                        body(pair, "pair")
                    body(PAIRS - 1, "layer" if l < DEPTH - 1 else None)

            @block.gpsimd
            def _(pool):
                start_ahead(pool, [rope_sum, rope_even, rope_done])
                with pool.Fori(0, DEPTH * PAIRS) as i:
                    for g in range(2 * QC):
                        if g < QC:
                            pool.wait_ge(sin_done.sem, sin_done.at(i, g + 1))
                            nc.gpsimd.tensor_tensor(tc[g % 2][:], ta[g % 2][:], tb[g % 2][:], ALU.add).then_inc(rope_sum.sem, 1)
                            pool.wait_ge(rope_sum.sem, rope_sum.at(i, g + 1))
                        else:
                            pool.wait_ge(k_sum.sem, k_sum.at(i, g - QC + 1))
                        pool.wait_ge(rn_done.sem, rn_done.at(i, g + 1))
                        if g < QC:
                            nc.gpsimd.tensor_tensor(qT[:, g, :], tc[g % 2][:], rn[g % 2][:], ALU.mult).then_inc(rope_done.sem, 1)
                        else:
                            for odd in range(2):
                                rows = slice(odd * D2, (odd + 1) * D2)
                                done = rope_done if odd else rope_even
                                nc.gpsimd.tensor_tensor(kT[odd][rows, g - QC, :], tc[g % 2][rows, :], rn[g % 2][rows, :],
                                                        ALU.mult).then_inc(done.sem, 1)
                                pool.wait_ge(done.sem, done.at(i, g + 1 if odd else g - QC + 1))

            @block.vector
            def _(dve):
                start_ahead(dve, [floored, k_sum, cos_done, sin_done, peaked, inverted, prob_done, t_even, o_done, added, centred_done,
                                  normed_done, hid_done, grown])
                nc.vector.memset(two(hT[:, 1, :])[:, :, 0:1], 0.0)
                nc.vector.memset(two(h_ff[:, 1, :])[:, :, 0:1], 0.0).then_inc(zeroed, 1)
                for odd in range(2):
                    nc.vector.memset(kT[odd][(1 - odd) * D2:(2 - odd) * D2, :, :], 0.0)
                dve.wait_ge(tables_in, 32)
                nc.vector.tensor_copy(ident16[:], sh["mat"]("ident"))
                nc.vector.tensor_copy(mask16[:], squares[:, 0, 0:PW]).then_inc(mask_done, 1)
                for l in range(DEPTH):
                    def front(i, normalise=None):
                        def cosine(g):
                            dve.wait_ge(rope_done.sem, rope_done.at(i, g - 1))
                            dve.wait_ge(raw_done.sem, raw_done.at(i, g + 1))
                            nc.vector.tensor_tensor(two(ta[g % 2][:]), two(raw[g % 2][:]), spread(tables[:, 2 * (g // QC), :], 2, 1),
                                                    ALU.mult).then_inc(cos_done.sem, 1)

                        for g in range(2 * QC):
                            if g < 2 * QC - 1:
                                cosine(g)
                            if g == 1 and normalise:
                                normalise()
                            dve.wait_ge(length_ready.sem, length_ready.at(i, g + 1))
                            dve.wait_ge(rn_done.sem, rn_done.at(i, g - 1))
                            nc.vector.tensor_scalar(fl[g % 2][:], ps_o[g % 2][:], 1e-24, 2.0 ** 16, ALU.max, ALU.mult).then_inc(floored.sem, 1)
                            if g == 2 * QC - 1:
                                cosine(g)
                            dve.wait_ge(turned_in[g % 2].sem, turned_in[g % 2].at(i, (g // 2 + 1) * TURN))
                            nc.vector.tensor_tensor(two(tb[g % 2][:]), two(turned[g % 2][:]), spread(tables[:, 2 * (g // QC) + 1, :], 2, 1),
                                                    ALU.mult).then_inc(sin_done.sem, 1)
                            if g >= QC:
                                dve.wait_ge(sin_done.sem, sin_done.at(i, g + 1))
                                nc.vector.tensor_tensor(tc[g % 2][:], ta[g % 2][:], tb[g % 2][:], ALU.add).then_inc(k_sum.sem, 1)

                    def body(pair, after):
                        i, last = l * PAIRS + pair, after is None

                        def tick(s):
                            if s < STEPS:
                                dve.wait_ge(s_ready.sem, s_ready.at(i, s + 1))
                                for w in range(2):
                                    op = nc.vector.tensor_reduce(peak[:, s % 3, w:w + 1], ps_s[s % 3][:, w * P:(2 * w + 1) * P],
                                                                 AX.X, ALU.max, negate=True)
                                op.then_inc(peaked.sem, 1)
                            if 1 <= s <= STEPS:
                                n = s - 1
                                dve.wait_ge(exp_done.sem, exp_done.at(i, 2 * n + 2))
                                nc.vector.reciprocal(rsum[:, n % PROBS, :], sums[:, n % PROBS, :]).then_inc(inverted.sem, 1)
                                dve.wait_ge(inverted.sem, inverted.at(i, n + 1))
                                for w in range(2):
                                    part = prob[n % PROBS][:, w * P:(2 * w + 1) * P]
                                    op = nc.vector.tensor_scalar(part, part, rsum[:, n % PROBS, w:w + 1], None, ALU.mult)
                                op.then_inc(prob_done.sem, 1)
                            n = s - LAG_T
                            if 0 <= n < STEPS and n % 2 == 0:
                                dve.wait_ge(t_ready.sem, t_ready.at(i, n + 1))
                                dve.wait_ge(pv_ready.sem, pv_ready.at(i, (n - RING) // 2 + 1))
                                nc.vector.tensor_copy(probT[n % RING][:], ps_t[0][:, 0:PW]).then_inc(t_even.sem, 1)
                            if s > LAG_V + 1 and (s - LAG_V) % 2 == 0:
                                q = (s - LAG_V) // 2 - 1
                                b, c, bank = q // QC, q % QC, ps_o[q % 2]
                                dve.wait_ge(pv_ready.sem, pv_ready.at(i, q + 1))
                                nc.vector.tensor_copy(oT[:, c, b * S:(b + 1) * S], bank[:, 0:S]).then_inc(o_done.sem, 1)

                        for s in range(STEPS + LAG_V + 1):
                            tick(s)
                        for m in range(C):
                            dve.wait_ge(out_ready.sem, out_ready.at(i, m + 1))
                            nc.vector.tensor_tensor(now_y(pair, m), ps_o[m][:], now_y(pair, m), ALU.add).then_inc(added.sem, 1)
                        dve.wait_ge(norm_ready.sem, norm_ready.at(i, 1))
                        nc.vector.tensor_tensor(centred[:], h_ff[:], spread(ps_g[:], C, 1), ALU.subtract).then_inc(centred_done.sem, 1)

                        def normalise():
                            dve.wait_ge(rstd_done.sem, rstd_done.at(i, 1))
                            nc.vector.tensor_tensor(normed[:], centred[:], spread(rstd[:], C, 1), ALU.mult).then_inc(normed_done.sem, 1)

                        if last:
                            normalise()
                        else:
                            front(i + 1, normalise)
                        dve.wait_ge(weights["feed_in"], l * (16 * FEED_LOADS) + 16 * FEED_LOADS)
                        for j in range(HC):
                            m = hrows(j)
                            dve.wait_ge(a_ready.sem, a_ready.at(i, j + 1))
                            dve.wait_ge(gelu_done.sem, gelu_done.at(i, j + 1))
                            nc.vector.scalar_tensor_tensor(hid[0:m, j, :], ps_s[j % 2][0:m, :], cols[0:m, 6 + j:7 + j],
                                                           gelu[j % 2][0:m, :], ALU.add, ALU.mult).then_inc(hid_done.sem, 1)
                        for m in range(C):
                            dve.wait_ge(ff_ready.sem, ff_ready.at(i, m + 1))
                            nc.vector.scalar_tensor_tensor(now_y(pair, m), ps_o[m][:], cols[:, 4 + m:5 + m], now_y(pair, m),
                                                           ALU.add, ALU.add).then_inc(grown.sem, 1)

                    if l == 0:
                        front(0)
                    with dve.Fori(0, PAIRS - 1) as pair:
                        body(pair, "pair")
                    body(PAIRS - 1, "layer" if l < DEPTH - 1 else None)

    with ExitStack() as st:
        final = st.enter_context(nc.semaphore("e_final"))
        sent = st.enter_context(nc.semaphore("e_sent"))
        x_all, y_all = sh["x"], sh["y"]
        with nc.Block() as block:
            @block.vector
            def _(dve):
                for n in range(4):
                    part = (slice(None), slice(None), slice(n * W, (n + 1) * W))
                    nc.vector.scalar_tensor_tensor(x_all[part], y_all[part], sh["tanh"][:, 3:4], x_all[part],
                                                   ALU.mult, ALU.add).then_inc(final, 1)

            @block.sync
            def _(sp):
                for n in range(4):
                    sp.wait_ge(final, n + 1)
                    sp.dma_start(io["out"][:, :, n * W:(n + 1) * W], x_all[:, :, n * W:(n + 1) * W]).then_inc(sent, 16)
                sp.wait_ge(sent, 64)


def build(nc, io):
    with ExitStack() as st:
        def sb(name, shape, dt=F32):
            return st.enter_context(nc.sbuf_tensor(name, shape, dt))

        const = sb("const", [P, len(CONST), P])
        sh = {
            "const": const,
            "mat": lambda name: const[:, CONST[name], :],
            "small": sb("small_sb", [P, SMALL]),
            "tanh": sb("tanh_gates", [P, 4]),
            "slot": sb("slot_of_token", [P, NT], I32),
            "owner": sb("expert_of_tile", [P, SLOTS], I32),
            "sorted_x": nc.dram_tensor("sorted_x", [SLOTS * P, D], F32, kind="Internal").ap(),
            "sorted_y": nc.dram_tensor("sorted_y", [SLOTS * P, D], F32, kind="Internal").ap(),
            "x": sb("x_all", [P, C, T]),
            "eps": sb("eps_sb", [P, 1]),
        }
        with ExitStack() as early:
            sh["rows"] = early.enter_context(nc.sbuf_tensor("rows", [P, NT, D], F32))
            sh["logits"] = early.enter_context(nc.sbuf_tensor("logits", [P, NT, E], F32))
            sh["head_weights"] = {
                n: early.enter_context(nc.sbuf_tensor("head_" + n, shape, F32))
                for n, shape in [("wq", [P, C, D]), ("wkv", [P, C, 2 * D]), ("wp", [P, C, D]),
                                 ("cols", [P, 4])]}
            sh["head_weights"]["in"] = early.enter_context(nc.semaphore("head_weights_in"))
            attend_linear(nc, io, sh)
            route(nc, io, sh)
            experts(nc, io, sh)
            attend_heads(nc, io, sh)
        sh["y"] = sb("y_all", [P, C, T])
        sh["layer_weights"] = {
            "wqkv": sb("wqkv", [P, C, 3 * INNER]), "wo": sb("wo", [P, INNER // P, D]),
            "w1": sb("w1", [P, C, 2 * HID]), "w2": sb("w2", [P, HC, D]),
            "scales": sb("scales", [P, 2]),
            "cols": sb("cols", [P, 6 + 2 * HC]),
            "attention_in": st.enter_context(nc.semaphore("attention_weights_in")),
            "output_in": st.enter_context(nc.semaphore("output_weights_in")),
            "feed_in": st.enter_context(nc.semaphore("feed_weights_in")),
        }
        start_layers(nc, io, sh)
        local_layers(nc, io, sh)


def constants():
    import numpy as np

    p = np.arange(P)
    same16 = p[:, None] // D1 == p[None, :] // D1
    same64 = p[:, None] // D2 == p[None, :] // D2
    mats = {
        "ident": np.eye(P), "mean256": np.full((P, P), 1.0 / D), "mean16": same16 / D1,
        "heads16": same16 / float(D1) ** 0.5, "before": p[:, None] < p[None, :], "ones": np.ones((P, P)),
        "heads64": same64,
    }
    consts = np.stack([np.asarray(mats[n], np.float32) for n in CONST], axis=1)
    small = np.zeros((P, SMALL), np.float32)
    small[:, 0:E] = np.arange(E, 0, -1)
    small[:, E:E + NT] = P * np.arange(NT)
    small[:, E + NT:E + NT + SLOTS] = np.arange(SLOTS)

    f = np.float32
    half_idx = np.arange(0, D2, 2, dtype=f)
    inv_freq = f(1.0) / f(10000.0) ** (half_idx / f(D2))
    t = np.arange(S, dtype=f)
    freqs = t[:, None] * inv_freq[None, :]
    base = (half_idx + f(0.4 * D2)) / f(1.4 * D2)
    power = (t - f(S // 2)) / f(64.0)
    decay = base[None, :] ** power[:, None]
    wide = [np.tile(np.concatenate([a, a], axis=1).T, (P // D2, 1)) for a in (np.cos(freqs), np.sin(freqs), decay)]
    cos, sin, decay = wide
    sin = np.where(p[:, None] % D2 < D2 // 2, -sin, sin)
    rope = np.stack([cos * decay * f(8 * 256), sin * decay * f(8 * 256), cos / decay * f(256), sin / decay * f(256)],
                    axis=1).astype(f)

    q, k = np.arange(P)[:, None], np.arange(S)[None, :]
    first = np.where(k <= q, 0.0, -1e30)[:, :P]
    second = np.where((k <= q + P) & (k >= q), 0.0, -1e30)
    mask = np.concatenate([first, second], axis=1).astype(f)
    return {"consts": consts, "small": small, "rope": rope, "mask": mask}


def kernel(**inputs):
    import numpy as np
    import concourse.bacc as bacc
    from concourse.bass_utils import run_bass_kernel_spmd

    a = {k: np.asarray(v) for k, v in inputs.items()}

    def turned(x):
        return np.ascontiguousarray(x.reshape(T, C, P).transpose(2, 1, 0))

    def chunks(v):
        n = -(-v.shape[0] // P)
        out = np.zeros((n * P,), v.dtype)
        out[:v.shape[0]] = v
        return out.reshape(n, P).T

    def per_head(v):
        return np.tile(v, P // v.shape[0])[:, None]

    def layer_cols(l):
        b1 = a["L1_ffn_b1"][l]
        return np.concatenate([chunks(a["L1_ffn_ln_g"][l]), chunks(a["L1_ffn_ln_b"][l]), chunks(a["L1_ffn_b2"][l]),
                               chunks(b1[:HID]), chunks(b1[HID:])], axis=1)

    arrays = {
        "xT": turned(a["x"]), "ctxT": turned(a["ctx_1024"]),
        "L0_Wkv": np.concatenate([a["L0_xattn_Wk"].T, a["L0_xattn_Wv"].T], axis=1),
        "L0_Wq": a["L0_xattn_Wq"].T, "L0_Wo": a["L0_xattn_Wo"].T,
        "Wg": a["L0_ffn_Wg"], "bg": a["L0_ffn_bg"],
        "gates": np.tile(np.concatenate([a["g_xattn"][0:1], a["g_ffn"][0:1], a["g_xattn"][1:2], a["g_ffn"][1:2]])[None], (P, 1)),
        "W1": a["L0_ffn_W1"], "b1": a["L0_ffn_b1"].reshape(E, FC, P).transpose(0, 2, 1), "W2": a["L0_ffn_W2"],
        "b2": a["L0_ffn_b2"],
        "L1_Wq": a["L1_xattn_Wq"], "L1_Wkv": a["L1_xattn_Wkv"], "L1_Wp": a["L1_xattn_Wp"],
        "L1_cols": np.concatenate([chunks(a["L1_xattn_bp"]), per_head(a["L1_xattn_ln_g"]), per_head(a["L1_xattn_ln_b"])], axis=1),
        "F_wqkv": a["L1_ffn_wqkv"], "F_wo": a["L1_ffn_wo"], "F_w1": a["L1_ffn_w1"], "F_w2": a["L1_ffn_w2"],
        "F_scales": np.stack([np.concatenate([per_head(a["L1_ffn_q_scale"][l]), per_head(a["L1_ffn_k_scale"][l])], axis=1)
                              for l in range(DEPTH)]),
        "F_cols": np.stack([layer_cols(l) for l in range(DEPTH)]),
        **constants(),
    }
    arrays = {k: np.ascontiguousarray(v) for k, v in arrays.items()}
    nc = bacc.Bacc("TRN2", target_bir_lowering=False, num_devices=1)
    io = {k: nc.dram_tensor(k, v.shape, mybir.dt.from_np(v.dtype), kind="ExternalInput").ap() for k, v in arrays.items()}
    io["out"] = nc.dram_tensor("out", (P, C, T), F32, kind="ExternalOutput").ap()
    build(nc, io)
    r = run_bass_kernel_spmd(nc, [arrays], core_ids=[0])
    got = r.results[0]["out"]
    return np.ascontiguousarray(got.transpose(2, 1, 0)).reshape(B, S, D)
```
